# Optimizing a Trainium2 kernel written in Bass

```python
import numpy as np
import jax
import jax.numpy as jnp

def _softmax(x, axis=-1):
    return jax.nn.softmax(x, axis=axis)

def _gelu(x):
    return jax.nn.gelu(x, approximate=True)

def _silu(x):
    return jax.nn.silu(x)

def _sigmoid(x):
    return jax.nn.sigmoid(x)

def _layernorm(x, axis=-1, eps=1e-05):
    m = jnp.mean(x, axis=axis, keepdims=True)
    v = jnp.var(x, axis=axis, keepdims=True)
    return (x - m) / jnp.sqrt(v + eps)

def _scatter_add(tgt, idx, src, axis=0):
    return tgt.at[idx].add(src)

def _segment_sum(src, seg, n):
    return jax.ops.segment_sum(src, seg, n)
kernel_name = 'mk_prb_d2_jaxref_r8_4ac153'

def setup_inputs(seed: int=0):
    np.random.seed(seed)
    _w = jnp.asarray

    def _L0_attn_setup():
        import jax, jax.numpy as jnp
        import numpy as np
        D_MODEL = 128
        N_HEADS = 16
        key = jax.random.key(seed)
        k1, k2, k3, k4 = jax.random.split(key, 4)
        B, T, D = (4, 256, D_MODEL)
        x = jax.random.normal(k1, (B, T, D), dtype=jnp.float32)
        w_qkv = jax.random.normal(k2, (D, 3 * D), dtype=jnp.float32) / np.sqrt(D)
        w_out = jax.random.normal(k3, (D, D), dtype=jnp.float32) / np.sqrt(D)
        b_out = jax.random.normal(k4, (D,), dtype=jnp.float32) * 0.01
        return {'x': x, 'w_qkv': w_qkv, 'w_out': w_out, 'b_out': b_out}
    _L0_attn_in = _L0_attn_setup()

    def _L0_ffn_setup():
        import jax, jax.numpy as jnp
        import numpy as np
        EPS = 1e-05
        N_HEADS = 16
        TOP_K = 2

        def _ln(x, g, b):
            m = x.mean(-1, keepdims=True)
            v = ((x - m) ** 2).mean(-1, keepdims=True)
            return (x - m) / jnp.sqrt(v + EPS) * g + b

        def _block_fwd(x, ln1_g, ln1_b, ln2_g, ln2_b, Wq, bq, Wk, bk, Wv, bv, Wo, bo, Wr, br, e_w1, e_b1, e_w2, e_b2):
            B, S, D = x.shape
            H = N_HEADS
            hd = D // H
            h = _ln(x, ln1_g, ln1_b)
            q = (h @ Wq + bq).reshape(B, S, H, hd).transpose(0, 2, 1, 3)
            k = (h @ Wk + bk).reshape(B, S, H, hd).transpose(0, 2, 1, 3)
            v = (h @ Wv + bv).reshape(B, S, H, hd).transpose(0, 2, 1, 3)
            scores = jnp.einsum('bhqd,bhkd->bhqk', q, k) / hd ** 0.5
            causal = jnp.tril(jnp.ones((S, S), dtype=bool))
            scores = jnp.where(causal, scores, -jnp.inf)
            attn = jax.nn.softmax(scores, axis=-1)
            o = jnp.einsum('bhqk,bhkd->bhqd', attn, v).transpose(0, 2, 1, 3).reshape(B, S, D)
            a = o @ Wo + bo + x
            h2 = _ln(a, ln2_g, ln2_b)
            logits = h2 @ Wr + br
            topv = jax.lax.top_k(logits, TOP_K)[0]
            kmask = logits >= topv[..., -1:]
            w = jax.nn.softmax(jnp.where(kmask, logits, -jnp.inf), axis=-1)
            mid = jax.nn.gelu(jnp.einsum('bsd,edf->bsef', h2, e_w1) + e_b1, approximate=False)
            eo = jnp.einsum('bsef,efd->bsed', mid, e_w2) + e_b2
            moe = jnp.einsum('bse,bsed->bsd', w, eo)
            return moe + a
        key = jax.random.key(seed)
        B, S, D, E = (1, 256, 128, 8)
        F = 4 * D
        ks = jax.random.split(key, 8)

        def n(k, shape):
            return jax.random.normal(k, shape, jnp.float32) * 0.02
        return dict(x=jax.random.normal(ks[0], (B, S, D), jnp.float32), ln1_g=jnp.ones((D,), jnp.float32), ln1_b=jnp.zeros((D,), jnp.float32), ln2_g=jnp.ones((D,), jnp.float32), ln2_b=jnp.zeros((D,), jnp.float32), Wq=n(ks[1], (D, D)), bq=jnp.zeros((D,), jnp.float32), Wk=n(ks[2], (D, D)), bk=jnp.zeros((D,), jnp.float32), Wv=n(ks[3], (D, D)), bv=jnp.zeros((D,), jnp.float32), Wo=n(ks[4], (D, D)), bo=jnp.zeros((D,), jnp.float32), Wr=n(ks[5], (D, E)), br=jnp.zeros((E,), jnp.float32), e_w1=n(ks[6], (E, D, F)), e_b1=jnp.zeros((E, F), jnp.float32), e_w2=n(ks[7], (E, F, D)), e_b2=jnp.zeros((E, D), jnp.float32))
    _L0_ffn_in = _L0_ffn_setup()

    def _L1_attn_setup():
        import jax, jax.numpy as jnp
        import numpy as np
        N_HEADS = 16
        INPUT_DIM = 128
        EMBED_DIM = 128
        KEY_DIM = EMBED_DIM // N_HEADS
        BATCH = 4
        SEQ = 256

        def _uniform(key, shape, bound):
            return jax.random.uniform(key, shape, jnp.float32, -bound, bound)
        key = jax.random.key(seed)
        kq, k1, k2, k3, k4 = jax.random.split(key, 5)
        stdv_k = 1.0 / np.sqrt(KEY_DIM)
        stdv_e = 1.0 / np.sqrt(EMBED_DIM)
        return {'q': jax.random.normal(kq, (BATCH, SEQ, INPUT_DIM), jnp.float32), 'W_query': _uniform(k1, (N_HEADS, INPUT_DIM, KEY_DIM), stdv_k), 'W_key': _uniform(k2, (N_HEADS, INPUT_DIM, KEY_DIM), stdv_k), 'W_val': _uniform(k3, (N_HEADS, INPUT_DIM, KEY_DIM), stdv_k), 'W_out': _uniform(k4, (N_HEADS, KEY_DIM, EMBED_DIM), stdv_e)}
    _L1_attn_in = _L1_attn_setup()

    def _L1_ffn_setup():
        import jax, jax.numpy as jnp
        import numpy as np
        D, H, E, K = (128, 128, 8, 2)

        def _moe(x, router_w, w_in, b_in, w_out, b_out):
            B, S, Dm = x.shape
            T = B * S
            x2 = x.reshape(T, Dm)
            logits = x2 @ router_w
            probs = jax.nn.softmax(logits, axis=-1)
            top_p, top_e = jax.lax.top_k(probs, K)
            flat_e = top_e.reshape(-1)
            flat_p = top_p.reshape(-1)
            tok = jnp.repeat(jnp.arange(T), K)
            order = jnp.argsort(flat_e)
            se, sp, st = (flat_e[order], flat_p[order], tok[order])
            xd = x2[st]
            N = xd.shape[0]
            h = jnp.zeros((N, H), x.dtype)
            for e in range(E):
                m = (se == e)[:, None]
                h = h + jnp.where(m, jax.nn.gelu(xd @ w_in[e] + b_in[e]), 0.0)
            y = jnp.zeros((N, Dm), x.dtype)
            for e in range(E):
                m = (se == e)[:, None]
                y = y + jnp.where(m, h @ w_out[e] + b_out[e], 0.0)
            y = y * sp[:, None]
            out = jnp.zeros((T, Dm), x.dtype).at[st].add(y)
            return out.reshape(B, S, Dm)
        key = jax.random.key(seed)
        ks = jax.random.split(key, 5)
        s = lambda k, shape, scale: jax.random.normal(k, shape, dtype=jnp.float32) * scale
        return {'input_batch': s(ks[0], (2, 64, D), 1.0), 'router_w': s(ks[1], (D, E), D ** (-0.5)), 'w_in': s(ks[2], (E, D, H), D ** (-0.5)), 'b_in': jnp.zeros((E, H), jnp.float32), 'w_out': s(ks[3], (E, H, D), H ** (-0.5)), 'b_out': jnp.zeros((E, D), jnp.float32)}
    _L1_ffn_in = _L1_ffn_setup()
    _d = {'L0_attn_x': _L0_attn_in['x'], 'L0_attn_w_qkv': _L0_attn_in['w_qkv'], 'L0_attn_w_out': _L0_attn_in['w_out'], 'L0_attn_b_out': _L0_attn_in['b_out'], 'L0_ffn_ln1_g': _L0_ffn_in['ln1_g'], 'L0_ffn_ln1_b': _L0_ffn_in['ln1_b'], 'L0_ffn_ln2_g': _L0_ffn_in['ln2_g'], 'L0_ffn_ln2_b': _L0_ffn_in['ln2_b'], 'L0_ffn_Wq': _L0_ffn_in['Wq'], 'L0_ffn_bq': _L0_ffn_in['bq'], 'L0_ffn_Wk': _L0_ffn_in['Wk'], 'L0_ffn_bk': _L0_ffn_in['bk'], 'L0_ffn_Wv': _L0_ffn_in['Wv'], 'L0_ffn_bv': _L0_ffn_in['bv'], 'L0_ffn_Wo': _L0_ffn_in['Wo'], 'L0_ffn_bo': _L0_ffn_in['bo'], 'L0_ffn_Wr': _L0_ffn_in['Wr'], 'L0_ffn_br': _L0_ffn_in['br'], 'L0_ffn_e_w1': _L0_ffn_in['e_w1'], 'L0_ffn_e_b1': _L0_ffn_in['e_b1'], 'L0_ffn_e_w2': _L0_ffn_in['e_w2'], 'L0_ffn_e_b2': _L0_ffn_in['e_b2'], 'L1_attn_W_query': _L1_attn_in['W_query'], 'L1_attn_W_key': _L1_attn_in['W_key'], 'L1_attn_W_val': _L1_attn_in['W_val'], 'L1_attn_W_out': _L1_attn_in['W_out'], 'L1_ffn_router_w': _L1_ffn_in['router_w'], 'L1_ffn_w_in': _L1_ffn_in['w_in'], 'L1_ffn_b_in': _L1_ffn_in['b_in'], 'L1_ffn_w_out': _L1_ffn_in['w_out'], 'L1_ffn_b_out': _L1_ffn_in['b_out']}
    _x0 = _d['L0_attn_x']
    _d['L0_attn_x'] = jax.random.normal(jax.random.fold_in(jax.random.key(seed), 1), (4, 512, 128), dtype=_x0.dtype)
    del _x0
    return _d

def reference(L0_attn_x, L0_attn_w_qkv, L0_attn_w_out, L0_attn_b_out, L0_ffn_ln1_g, L0_ffn_ln1_b, L0_ffn_ln2_g, L0_ffn_ln2_b, L0_ffn_Wq, L0_ffn_bq, L0_ffn_Wk, L0_ffn_bk, L0_ffn_Wv, L0_ffn_bv, L0_ffn_Wo, L0_ffn_bo, L0_ffn_Wr, L0_ffn_br, L0_ffn_e_w1, L0_ffn_e_b1, L0_ffn_e_w2, L0_ffn_e_b2, L1_attn_W_query, L1_attn_W_key, L1_attn_W_val, L1_attn_W_out, L1_ffn_router_w, L1_ffn_w_in, L1_ffn_b_in, L1_ffn_w_out, L1_ffn_b_out):

    def _L0_attn_ref(x, w_qkv, w_out, b_out):
        import jax, jax.numpy as jnp
        import numpy as np
        D_MODEL = 128
        N_HEADS = 16
        B, T, D = x.shape
        h = N_HEADS
        Hd = D // h
        qkv = jnp.einsum('btd,de->bte', x, w_qkv).reshape(B, T, 3, h, Hd)
        q = jnp.transpose(qkv[:, :, 0], (0, 2, 1, 3))
        k = jnp.transpose(qkv[:, :, 1], (0, 2, 1, 3))
        v = jnp.transpose(qkv[:, :, 2], (0, 2, 1, 3))
        scale = 1.0 / jnp.sqrt(jnp.array(Hd, dtype=x.dtype))
        logits = jnp.einsum('bhqd,bhkd->bhqk', q, k) * scale
        mask = jnp.tril(jnp.ones((T, T), dtype=x.dtype))
        big_neg = jnp.array(-10000000000.0, dtype=x.dtype)
        logits = logits + (1.0 - mask)[None, None, :, :] * big_neg
        attn = jax.nn.softmax(logits, axis=-1)
        out = jnp.einsum('bhqk,bhkd->bhqd', attn, v)
        out = jnp.transpose(out, (0, 2, 1, 3)).reshape(B, T, D)
        return jnp.einsum('btd,de->bte', out, w_out) + b_out

    def _L0_ffn_ref(x, ln1_g, ln1_b, ln2_g, ln2_b, Wq, bq, Wk, bk, Wv, bv, Wo, bo, Wr, br, e_w1, e_b1, e_w2, e_b2):
        import jax, jax.numpy as jnp
        import numpy as np
        EPS = 1e-05
        N_HEADS = 16
        TOP_K = 2

        def _ln(x, g, b):
            m = x.mean(-1, keepdims=True)
            v = ((x - m) ** 2).mean(-1, keepdims=True)
            return (x - m) / jnp.sqrt(v + EPS) * g + b

        def _block_fwd(x, ln1_g, ln1_b, ln2_g, ln2_b, Wq, bq, Wk, bk, Wv, bv, Wo, bo, Wr, br, e_w1, e_b1, e_w2, e_b2):
            B, S, D = x.shape
            H = N_HEADS
            hd = D // H
            h = _ln(x, ln1_g, ln1_b)
            q = (h @ Wq + bq).reshape(B, S, H, hd).transpose(0, 2, 1, 3)
            k = (h @ Wk + bk).reshape(B, S, H, hd).transpose(0, 2, 1, 3)
            v = (h @ Wv + bv).reshape(B, S, H, hd).transpose(0, 2, 1, 3)
            scores = jnp.einsum('bhqd,bhkd->bhqk', q, k) / hd ** 0.5
            causal = jnp.tril(jnp.ones((S, S), dtype=bool))
            scores = jnp.where(causal, scores, -jnp.inf)
            attn = jax.nn.softmax(scores, axis=-1)
            o = jnp.einsum('bhqk,bhkd->bhqd', attn, v).transpose(0, 2, 1, 3).reshape(B, S, D)
            a = o @ Wo + bo + x
            h2 = _ln(a, ln2_g, ln2_b)
            logits = h2 @ Wr + br
            topv = jax.lax.top_k(logits, TOP_K)[0]
            kmask = logits >= topv[..., -1:]
            w = jax.nn.softmax(jnp.where(kmask, logits, -jnp.inf), axis=-1)
            mid = jax.nn.gelu(jnp.einsum('bsd,edf->bsef', h2, e_w1) + e_b1, approximate=False)
            eo = jnp.einsum('bsef,efd->bsed', mid, e_w2) + e_b2
            moe = jnp.einsum('bse,bsed->bsd', w, eo)
            return moe + a
        return _block_fwd(x, ln1_g, ln1_b, ln2_g, ln2_b, Wq, bq, Wk, bk, Wv, bv, Wo, bo, Wr, br, e_w1, e_b1, e_w2, e_b2)

    def _L1_attn_ref(q, W_query, W_key, W_val, W_out):
        import jax, jax.numpy as jnp
        import numpy as np
        N_HEADS = 16
        INPUT_DIM = 128
        EMBED_DIM = 128
        KEY_DIM = EMBED_DIM // N_HEADS
        BATCH = 4
        SEQ = 256

        def _uniform(key, shape, bound):
            return jax.random.uniform(key, shape, jnp.float32, -bound, bound)
        norm = 1.0 / np.sqrt(KEY_DIM)
        Q = jnp.einsum('bsd,hdk->hbsk', q, W_query)
        K = jnp.einsum('bsd,hdk->hbsk', q, W_key)
        V = jnp.einsum('bsd,hdv->hbsv', q, W_val)
        scores = norm * jnp.einsum('hbqk,hbnk->hbqn', Q, K)
        attn = jax.nn.softmax(scores, axis=-1)
        heads = jnp.einsum('hbqn,hbnv->hbqv', attn, V)
        out = jnp.einsum('hbqv,hve->bqe', heads, W_out)
        return out

    def _L1_ffn_ref(input_batch, router_w, w_in, b_in, w_out, b_out):
        import jax, jax.numpy as jnp
        import numpy as np
        D, H, E, K = (128, 128, 8, 2)

        def _moe(x, router_w, w_in, b_in, w_out, b_out):
            B, S, Dm = x.shape
            T = B * S
            x2 = x.reshape(T, Dm)
            logits = x2 @ router_w
            probs = jax.nn.softmax(logits, axis=-1)
            top_p, top_e = jax.lax.top_k(probs, K)
            flat_e = top_e.reshape(-1)
            flat_p = top_p.reshape(-1)
            tok = jnp.repeat(jnp.arange(T), K)
            order = jnp.argsort(flat_e)
            se, sp, st = (flat_e[order], flat_p[order], tok[order])
            xd = x2[st]
            N = xd.shape[0]
            h = jnp.zeros((N, H), x.dtype)
            for e in range(E):
                m = (se == e)[:, None]
                h = h + jnp.where(m, jax.nn.gelu(xd @ w_in[e] + b_in[e]), 0.0)
            y = jnp.zeros((N, Dm), x.dtype)
            for e in range(E):
                m = (se == e)[:, None]
                y = y + jnp.where(m, h @ w_out[e] + b_out[e], 0.0)
            y = y * sp[:, None]
            out = jnp.zeros((T, Dm), x.dtype).at[st].add(y)
            return out.reshape(B, S, Dm)
        return _moe(input_batch, router_w, w_in, b_in, w_out, b_out)
    x = L0_attn_x
    xn = _layernorm(x, axis=-1)
    x = x + _L0_attn_ref(xn, L0_attn_w_qkv, L0_attn_w_out, L0_attn_b_out) + _L0_ffn_ref(xn, L0_ffn_ln1_g, L0_ffn_ln1_b, L0_ffn_ln2_g, L0_ffn_ln2_b, L0_ffn_Wq, L0_ffn_bq, L0_ffn_Wk, L0_ffn_bk, L0_ffn_Wv, L0_ffn_bv, L0_ffn_Wo, L0_ffn_bo, L0_ffn_Wr, L0_ffn_br, L0_ffn_e_w1, L0_ffn_e_b1, L0_ffn_e_w2, L0_ffn_e_b2)
    xn = _layernorm(x, axis=-1)
    x = x + _L1_attn_ref(xn, L1_attn_W_query, L1_attn_W_key, L1_attn_W_val, L1_attn_W_out) + _L1_ffn_ref(xn, L1_ffn_router_w, L1_ffn_w_in, L1_ffn_b_in, L1_ffn_w_out, L1_ffn_b_out)
    return x

_drawn_inputs = setup_inputs


def setup_inputs(seed=0):
    import zlib

    import numpy as np

    out = dict(_drawn_inputs(seed))
    spreads = {'L0_ffn_ln1_g': (1.0, 0.6),
     'L0_ffn_ln1_b': (0.0, 0.8),
     'L0_ffn_ln2_g': (1.0, 0.2),
     'L0_ffn_ln2_b': (0.0, 0.535),
     'L0_ffn_bq': (0.0, 0.8),
     'L0_ffn_bk': (0.0, 0.8),
     'L0_ffn_bv': (0.0, 0.418),
     'L0_ffn_bo': (0.0, 0.1),
     'L0_ffn_br': (0.0, 0.1),
     'L0_ffn_e_b1': (0.0, 0.519),
     'L0_ffn_e_b2': (0.0, 0.1),
     'L1_ffn_b_in': (0.0, 0.578),
     'L1_ffn_b_out': (0.0, 0.395)}
    factors = {'L0_attn_b_out': 6.338,
     'L0_ffn_Wq': 8.0,
     'L0_ffn_Wk': 8.0,
     'L0_ffn_Wv': 5.552,
     'L0_ffn_Wo': 2.955}
    for name, (base, spread) in spreads.items():
        noise = np.random.default_rng([zlib.crc32(name.encode()), seed]).standard_normal(out[name].shape)
        drawn = base * np.exp(spread * noise) if base else spread * noise
        out[name] = jnp.asarray(drawn.astype(out[name].dtype))
    for name, factor in factors.items():
        out[name] = (out[name] * factor).astype(out[name].dtype)
    return out
```

```python
from contextlib import ExitStack

import concourse.bass as bass
from concourse import mybir

F32 = mybir.dt.float32
BF16 = mybir.dt.bfloat16
ALU = mybir.AluOpType
ACT = mybir.ActivationFunctionType
AX_X = mybir.AxisListType.X

P = 128
TILES = 4
HEADS, HD = 16, 8
QUADS, QH = 4, 4
EXPERTS = 8
EPS = 1e-5
SCALE = float(HD) ** -0.5
PARTS = 3
MAX_ROW = 96
SUM_COL = 8
MASKED = -1e30
PER = 2048
CAUSAL = (True, True, False)

COL_G1, COL_B1, COL_G2, COL_B2, COL_BQ, COL_BK, COL_EB1 = range(7)
COL_BIN = COL_EB1 + 4 * EXPERTS
N_COLS = COL_BIN + EXPERTS
ROW_BOUT, ROW_BO, ROW_BV, ROW_BR = 0, P, 2 * P, 3 * P
N_ROW = 3 * P + EXPERTS


def batch_plan():
    plan = [("load",), ("norm", "x"), ("turn", "x"), ("project", 0), ("norm", "h"), ("turn", "h"), ("project", 1)]

    def attention(quads, extra):
        first, second = quads[0], quads[1]
        for n, (u, g) in enumerate(quads):
            for j in range(TILES):
                yield ("scores", u, g, j)
                if n and j == 0:
                    yield ("values", *quads[n - 1], TILES - 1)
                if j:
                    yield ("values", u, g, j - 1)
                if j == 1 and n + 1 < len(quads):
                    yield ("max_turn", *quads[n + 1])
                if j == 2 and n:
                    yield ("heads_turn", *quads[n - 1])
                if n + 2 < len(quads):
                    yield ("max", *quads[n + 2], j)
                yield from extra.get((n, j), [])
        yield ("values", *quads[-1], TILES - 1)
        yield ("heads_turn", *quads[-1])

    def finish(u):
        return [("heads_back", u), ("out_project", u)]

    quads = [(u, g) for u in (0, 1) for g in range(QUADS)]
    plan += [("max", 0, 0, i) for i in range(TILES)]
    plan += [("max", 0, 1, 0), ("max", 0, 1, 1), ("max_turn", 0, 0), ("max", 0, 1, 2), ("max", 0, 1, 3)]
    done = finish(0)
    extra = {(4, 3): done[:1], (5, 0): done[1:]}
    plan += attention(quads, extra)
    plan += finish(1)
    plan += [("norm", "a"), ("turn", "a"), ("route", 0)]
    for e in range(EXPERTS + 1):
        if e < EXPERTS:
            plan.append(("expert_in", 0, e))
        if e == 1:
            plan += [("route_turn", 0), ("route_bias", 0)]
        if e:
            plan.append(("expert_out", 0, e - 1))
    plan += [("norm", "y"), ("turn", "y"), ("project", 2), ("route", 1)]
    first_max = [("max", 2, g, i) for g in (0, 1) for i in range(TILES)]
    first_max.insert(6, ("max_turn", 2, 0))
    for p in range(3):
        if p < 2:
            plan.append(("expert_in", 1, p))
        if p == 0:
            plan += [("route_turn", 1), ("route_bias", 1)]
        if p:
            plan.append(("expert_out", 1, p - 1))
        plan += first_max[3 * p:3 * p + 3]
    plan += attention([(2, g) for g in range(QUADS)], {})
    plan += finish(2)
    plan.append(("store",))
    return plan


def score_pairs(u, j):
    width = P * (TILES - j) if CAUSAL[u] else P * TILES
    per_bank = {P: 4, 2 * P: 2}.get(width, 1)
    heads = min(QH, 2 * per_bank)
    return [(list(range(c, c + heads)), width, per_bank) for c in range(0, QH, heads)]


def max_chunks(u, i):
    keys = P * (i + 1) if CAUSAL[u] else P * TILES
    per_bank = {P: 4, 2 * P: 2}.get(keys, 1)
    return [(list(range(c, c + per_bank)), keys) for c in range(0, QH, per_bank)]


class Signal:

    def __init__(self, nc, ctx, name, step=1, per=PER):
        self.sem = ctx.enter_context(nc.semaphore(name))
        self.step, self.n, self.per = step, 0, per

    def count(self):
        self.n += self.step
        assert self.n <= self.per
        return self.n


class Counts:

    pers = (PER, *sorted({16, 16 * PARTS * PARTS, 16 * len(CAUSAL) * QUADS // 2}))

    def __init__(self, eng, name):
        self.eng, self.k = eng, 0
        self.registers = [eng.alloc_register(f"{name}_count{i}") for i in range(6)]

    def sequence(self, b):
        self.base = {per: self.eng.snap(b * per) for per in self.pers}
        self.number = self.eng.snap(b + 1)

    def at(self, sig, n):
        register = self.registers[self.k % len(self.registers)]
        self.k += 1
        self.eng.reg_add(register, self.base[sig.per], n)
        return register


def build(nc, x, proj, w_expert_in, w_expert_out, w_in, w_out, routers, cols, row, expert_bias, out):
    BATCH = x.shape[0]
    plan = batch_plan()
    ctx = ExitStack()
    with ctx:
        def sb(name, shape, dt=F32):
            return ctx.enter_context(nc.sbuf_tensor(name, shape, dt))

        def signal(name, step=1, per=PER):
            return Signal(nc, ctx, name, step, per)

        projs = sb("projs", [P, 3, 4, P])
        ew1 = sb("ew1", [P, EXPERTS, 4, P])
        ew2 = sb("ew2", [P, EXPERTS, 4, P])
        win = sb("win", [P, EXPERTS, P])
        wout = sb("wout", [P, EXPERTS, P])
        router = sb("router", [P, 2, EXPERTS])
        col = sb("col", [P, N_COLS])
        rows = sb("rows", [P, N_ROW])
        ebias = sb("ebias", [EXPERTS, 2, P])
        ident = sb("ident", [P, P])
        ident16 = sb("ident16", [P, P], BF16)
        mask_qk = sb("mask_qk", [P, P], BF16)
        mask_kq = sb("mask_kq", [P, P], BF16)
        minus_half = sb("minus_half", [P, TILES])
        rank = sb("rank", [P, TILES, EXPERTS])

        x_in = sb("x_in", [P, TILES, P])
        xn = sb("xn", [P, TILES, P])
        hn = sb("hn", [P, TILES, P])
        x_bias = sb("x_bias", [P, TILES, P])
        a_sum = sb("a_sum", [P, TILES, P])
        acc = sb("acc", [P, TILES, P])
        xT = sb("xT", [P, TILES * P])
        hT = sb("hT", [P, TILES * P])
        q_stack = [sb(f"q_stack{s}", [P, HEADS, TILES * P], BF16) for s in range(2)]
        k_stack = [sb(f"k_stack{s}", [P, HEADS, TILES * P], BF16) for s in range(2)]
        v_ones = [sb(f"v_ones{s}", [P, TILES, HEADS, 32]) for s in range(2)]
        part = [sb(f"part{s}", [P, 2, PARTS, TILES * P], BF16) for s in range(2)]
        rest = sb("rest", [P, 2, TILES * P])
        probs = sb("probs", [P, 3, QH, TILES * P])
        head_sums = sb("head_sums", [P, 2, TILES * P])
        heads = sb("heads", [P, TILES, P])
        inv_sum = sb("inv_sum", [P, TILES, QH])
        headsT = sb("headsT", [P, TILES * P])
        neg_max = sb("neg_max", [P, 2, QH, TILES])
        max_part = sb("max_part", [P, 2, PARTS, QH * TILES], BF16)
        max_rest = sb("max_rest", [P, 2, QH * TILES])
        maxT = sb("maxT", [PARTS * QH * TILES, 2, P], BF16)
        stats = sb("stats", [P, TILES, 6])
        mean_var = sb("mean_var", [P, TILES, 2])
        var_eps = sb("var_eps", [P, TILES])
        rstd = sb("rstd", [P, TILES])
        logit = sb("logit", [P, TILES, EXPERTS])
        top8 = sb("top8", [P, TILES, 8])
        gate_a = sb("gate_a", [P, TILES, EXPERTS])
        gate_b = sb("gate_b", [P, TILES, EXPERTS])
        gate_c = sb("gate_c", [P, TILES, EXPERTS])
        gate_s = sb("gate_s", [P, TILES])
        gate_t = sb("gate_t", [P, TILES])
        gate = sb("gate", [P, TILES, EXPERTS])
        gateT = sb("gateT", [EXPERTS, TILES * P])

        psum = ctx.enter_context(nc.psum_tensor("psum", [P, 8, 512], F32))
        work_bank = [psum[:, 0, :], psum[:, 1, :]]
        pair_bank = [psum[:, 2:4, :], psum[:, 4:6, :]]
        sum_bank = [psum[:, 6, :], psum[:, 7, :]]

        loaded = ctx.enter_context(nc.semaphore("loaded"))
        experts_loaded = ctx.enter_context(nc.semaphore("experts_loaded"))
        made = ctx.enter_context(nc.semaphore("made"))
        cleared = ctx.enter_context(nc.semaphore("cleared"))
        arrived = {e: ctx.enter_context(nc.semaphore(f"arrived_{e}")) for e in ("pe", "act", "dve", "pool", "sp")}
        passed = {e: ctx.enter_context(nc.semaphore(f"passed_{e}")) for e in arrived}
        work_full = signal("work_full")
        pair_full = signal("pair_full")
        values_done = signal("values_done")
        expert_sum = signal("expert_sum")
        vector_done = signal("dve_done")
        probs_ready = signal("probs_ready")
        scalar_done = signal("act_done")
        gpsimd_done = signal("pool_done")
        x_landed = signal("x_landed", 16, 16)
        q_landed = [signal(f"q_landed{u}", 16, 16 * PARTS * PARTS) for u in range(3)]
        k_landed = [signal(f"k_landed{u}", 16, 16 * PARTS * PARTS) for u in range(3)]
        max_landed = [signal(f"max_landed{s}", 16, 16 * len(CAUSAL) * QUADS // 2) for s in range(2)]
        stored = signal("stored", 16, 16)

        N_LOADS, N_EXPERT_LOADS = 5, 4
        N_MADE, N_CLEARED = 9, 6
        STACK_DMAS = PARTS * PARTS

        WORKS = {"turn": 1, "project": 3, "max_turn": 1, "heads_turn": 1, "heads_back": 1, "out_project": 1,
                 "route": 1, "route_turn": 1, "route_bias": 1}

        def works(step):
            return len(max_chunks(step[1], step[3])) if step[0] == "max" else WORKS.get(step[0], 0)

        def pairs(step):
            if step[0] == "scores":
                return len(score_pairs(step[1], step[3]))
            return 2 if step[0] == "expert_in" else 0

        first_work, first_pair, n_work, n_pair = {}, {}, 0, 0
        slot_of, sum_of, n_slot, n_sum = {}, {}, 0, 0
        for step in plan:
            first_work[step], first_pair[step] = n_work, n_pair
            n_work += works(step)
            n_pair += pairs(step)
            if step[0] in ("scores", "expert_in"):
                slot_of[step] = n_slot
                n_slot += 1
            if step[0] == "values" and step[3] == TILES - 1:
                sum_of[step] = n_sum
                n_sum += 1
            if step[0] == "expert_out":
                sum_of[step] = n_sum
                n_sum += 1 if step[1] == 0 else 4
        for step in plan:
            if step[0] == "values":
                sum_of[step] = sum_of[("values", step[1], step[2], TILES - 1)]
        max_quads = [step[1:] for step in plan if step[0] == "max_turn"]
        head_quads = [step[1:] for step in plan if step[0] == "heads_turn"]
        act_at, pool_at, n_act, n_pool = {}, {}, 0, 0
        sum_freed_act = {}
        for step in plan:
            if step[0] == "project":
                for k in range(2):
                    n_act += 1
                    act_at["part", step[1], k] = n_act
            elif step[0] == "values" and step[3] == TILES - 1:
                n_act += 1
                sum_freed_act[sum_of[step]] = n_act
                act_at["sums", step[1], step[2]] = n_act
            elif step[0] == "route":
                n_act += 1
                act_at["gate_exp", step[1]] = n_act
            elif step[0] == "norm":
                n_pool += 1
                pool_at["pow", step[1]] = n_pool
                if step[1] == "h":
                    for u in range(2):
                        n_pool += TILES
                        pool_at["bias", u] = n_pool
        work_freed, sum_freed_dve, dve_at = {}, {}, {}

        block = ctx.enter_context(nc.Block())

        @block.vector
        def _(eng):
            U32 = mybir.dt.uint32
            for s in range(2):
                eng.memset(v_ones[s][:, :, :, :], 0.0).then_inc(cleared, 1)
            for stack in (q_stack[0], k_stack[0]):
                eng.memset(stack[64:P, :, :].bitcast(U32), 0).then_inc(cleared, 1)
            eng.wait_ge(cleared, 4)
            for s in range(2):
                eng.memset(v_ones[s][:, :, :, SUM_COL:SUM_COL + 1], 1.0)
            eng.memset(k_stack[0][MAX_ROW:MAX_ROW + PARTS, :, :].bitcast(U32), 0x3F803F80).then_inc(cleared, 1)
            eng.memset(minus_half[:, :], -0.5)
            for e in range(EXPERTS):
                eng.memset(rank[:, :, e:e + 1], float(EXPERTS - e))
            eng.wait_ge(loaded, 16 * N_LOADS)
            eng.wait_ge(made, N_MADE)
            eng.tensor_copy(ident16[:, :], ident[:, :]).then_inc(cleared, 1)

            counts = Counts(eng, "dve")
            at = counts.at
            with eng.Fori(0, BATCH) as b:
                counts.sequence(b)

                def bank(step, k=0):
                    n = first_work[step] + k
                    eng.wait_ge(work_full.sem, at(work_full, n + 1))
                    return work_bank[n % 2]

                def free(step, k, count):
                    work_freed[first_work[step] + k] = count

                def normalise(what, src, dst):
                    for t in range(TILES):
                        eng.bn_stats(stats[:, t, :], src[:, t, :]).then_inc(vector_done.sem, 1)
                        n = vector_done.count()
                    eng.wait_ge(vector_done.sem, at(vector_done, n))
                    eng.sem_inc(passed["dve"], 1)
                    for t in range(TILES):
                        eng.bn_aggr(mean_var[:, t, :], stats[:, t, :]).then_inc(vector_done.sem, 1)
                        n = vector_done.count()
                    eng.wait_ge(vector_done.sem, at(vector_done, n))
                    eng.tensor_scalar(var_eps[:, :], mean_var[:, :, 1], EPS, None, ALU.add).then_inc(vector_done.sem, 1)
                    n = vector_done.count()
                    dve_at["pow", what] = n
                    eng.wait_ge(gpsimd_done.sem, at(gpsimd_done, pool_at["pow", what]))
                    for t in range(TILES):
                        eng.tensor_scalar(dst[:, t, :], src[:, t, :], mean_var[:, t, 0:1],
                                                     rstd[:, t:t + 1], ALU.subtract, ALU.mult).then_inc(vector_done.sem, 1)
                        n = vector_done.count()
                    return n

                for step in plan:
                    kind = step[0]
                    if kind == "norm":
                        what = step[1]
                        if what == "x":
                            eng.wait_ge(x_landed.sem, at(x_landed, 16))
                            n = normalise(what, x_in, xn)
                        elif what == "h":
                            eng.wait_ge(vector_done.sem, at(vector_done, dve_at["norm", "x"]))
                            n = normalise(what, xn, hn)
                        elif what == "a":
                            eng.wait_ge(vector_done.sem, at(vector_done, dve_at["out_project", 1]))
                            n = normalise(what, a_sum, hn)
                            eng.tensor_tensor(acc[:, :, :], x_bias[:, :, :], a_sum[:, :, :], ALU.add).then_inc(vector_done.sem, 1)
                            vector_done.count()
                        else:
                            eng.wait_ge(vector_done.sem, at(vector_done, dve_at["expert_out", 0, EXPERTS - 1]))
                            n = normalise(what, acc, xn)
                        dve_at[step] = n
                        if what == "x":
                            dve_at["xn"] = n
                    elif kind == "turn":
                        src = bank(step)
                        if step[1] in ("x", "y"):
                            eng.tensor_copy(xT[:, :], src).then_inc(vector_done.sem, 1)
                            n = vector_done.count()
                        else:
                            g = COL_G1 if step[1] == "h" else COL_G2
                            eng.tensor_scalar(hT[:, :], src, col[:, g:g + 1], col[:, g + 1:g + 2],
                                                         ALU.mult, ALU.add).then_inc(vector_done.sem, 1)
                            n = vector_done.count()
                        free(step, 0, n)
                        dve_at[step] = n
                    elif kind == "project":
                        u = step[1]
                        s = u % 2
                        if u == 2:
                            eng.wait_ge(q_landed[0].sem, at(q_landed[0], 16 * STACK_DMAS))
                            eng.wait_ge(k_landed[0].sem, at(k_landed[0], 16 * STACK_DMAS))
                        for k in range(2):
                            src = bank(step, k)
                            if u == 1:
                                c = (COL_BQ, COL_BK)[k]
                                eng.tensor_scalar(part[s][:, k, 0, :], src, col[:, c:c + 1], None, ALU.add).then_inc(vector_done.sem, 1)
                                n = vector_done.count()
                            else:
                                eng.tensor_copy(part[s][:, k, 0, :], src).then_inc(vector_done.sem, 1)
                                n = vector_done.count()
                            eng.wait_ge(vector_done.sem, at(vector_done, n))
                            if u:
                                eng.wait_ge(scalar_done.sem, at(scalar_done, act_at["part", u - 1, k]))
                                eng.wait_ge(vector_done.sem, at(vector_done, dve_at["part3", u - 1, k]))
                            if u == 1:
                                eng.scalar_tensor_tensor(out=rest[:, k, :], in0=src, scalar=col[:, c:c + 1],
                                                                    in1=part[s][:, k, 0, :], op0=ALU.add,
                                                                    op1=ALU.subtract).then_inc(vector_done.sem, 1)
                                n = vector_done.count()
                            else:
                                eng.tensor_tensor(rest[:, k, :], src, part[s][:, k, 0, :], ALU.subtract).then_inc(vector_done.sem, 1)
                                n = vector_done.count()
                            free(step, k, n)
                            dve_at["rest", u, k] = n
                            if k == 0:
                                continue
                            v = bank(step, 2).rearrange("p (t h c) -> p t h c", t=TILES, h=HEADS)
                            if u == 1:
                                bv = rows[:, ROW_BV:ROW_BV + P].rearrange("p (h c) -> p h c", h=HEADS)
                                for t in range(TILES):
                                    eng.tensor_tensor(v_ones[s][:, t, :, 0:HD], v[:, t], bv, ALU.add).then_inc(vector_done.sem, 1)
                                    n = vector_done.count()
                            else:
                                for t in range(TILES):
                                    eng.tensor_copy(v_ones[s][:, t, :, 0:HD], v[:, t]).then_inc(vector_done.sem, 1)
                                    n = vector_done.count()
                            free(step, 2, n)
                            dve_at["v", u] = n
                        for k in range(2):
                            eng.wait_ge(scalar_done.sem, at(scalar_done, act_at["part", u, k]))
                            eng.tensor_tensor(part[s][:, k, 2, :], rest[:, k, :], part[s][:, k, 1, :],
                                                  ALU.subtract).then_inc(vector_done.sem, 1)
                            dve_at["part3", u, k] = vector_done.count()
                    elif kind == "max":
                        _, u, g, i = step
                        q = max_quads.index((u, g))
                        for k, (hs, keys) in enumerate(max_chunks(u, i)):
                            src = bank(step, k)[:, 0:len(hs) * keys].rearrange("p (h k) -> p h k", h=len(hs))
                            eng.tensor_reduce(neg_max[:, q % 2, hs[0]:hs[0] + len(hs), i], src, AX_X,
                                                         ALU.max, negate=True).then_inc(vector_done.sem, 1)
                            n = vector_done.count()
                            free(step, k, n)
                        if i == TILES - 1:
                            m = neg_max[:, q % 2, :, :].rearrange("p h i -> p (h i)")
                            parts, left = max_part[:, q % 2], max_rest[:, q % 2, :]
                            eng.wait_ge(vector_done.sem, at(vector_done, n))
                            if q >= 2:
                                eng.wait_ge(work_full.sem, at(work_full, first_work["max_turn", *max_quads[q - 2]] + 1))
                            eng.tensor_copy(parts[:, 0, :], m).then_inc(vector_done.sem, 1)
                            eng.wait_ge(vector_done.sem, at(vector_done, vector_done.count()))
                            eng.tensor_tensor(left, m, parts[:, 0, :], ALU.subtract).then_inc(vector_done.sem, 1)
                            eng.wait_ge(vector_done.sem, at(vector_done, vector_done.count()))
                            eng.tensor_copy(parts[:, 1, :], left).then_inc(vector_done.sem, 1)
                            eng.wait_ge(vector_done.sem, at(vector_done, vector_done.count()))
                            eng.tensor_tensor(parts[:, 2, :], left, parts[:, 1, :], ALU.subtract).then_inc(vector_done.sem, 1)
                            dve_at["max_part", u, g] = vector_done.count()
                    elif kind == "max_turn":
                        q = max_quads.index(step[1:])
                        rows48 = PARTS * QH * TILES
                        src = bank(step)[0:rows48, 0:P // 2].bitcast(BF16)
                        if q >= 2:
                            eng.wait_ge(max_landed[q % 2].sem, at(max_landed[q % 2], 16 * (q // 2)))
                        eng.tensor_copy(maxT[:, q % 2, :], src).then_inc(vector_done.sem, 1)
                        n = vector_done.count()
                        free(step, 0, n)
                        dve_at[step] = n
                    elif kind == "heads_turn":
                        _, u, g = step
                        src = bank(step).rearrange("p (t h c) -> p t h c", t=TILES, h=QH)
                        eng.wait_ge(vector_done.sem, at(vector_done, vector_done.n))
                        eng.reciprocal(inv_sum[:, :, :], src[:, :, :, SUM_COL]).then_inc(vector_done.sem, 1)
                        eng.wait_ge(vector_done.sem, at(vector_done, vector_done.count()))
                        dst = heads[:, :, g * QH * HD:(g + 1) * QH * HD].rearrange("p t (h c) -> p t h c", h=QH)
                        inv = inv_sum[:, :, :].unsqueeze(3).to_broadcast([P, TILES, QH, HD])
                        eng.tensor_tensor(dst, src[:, :, :, 0:HD], inv, ALU.mult).then_inc(vector_done.sem, 1)
                        n = vector_done.count()
                        free(step, 0, n)
                        dve_at[step] = n
                    elif kind == "heads_back":
                        eng.tensor_copy(headsT[:, :], bank(step)).then_inc(vector_done.sem, 1)
                        n = vector_done.count()
                        free(step, 0, n)
                        dve_at[step] = n
                    elif kind == "out_project":
                        u = step[1]
                        dst = (x_bias, a_sum, acc)[u]
                        if u < 2:
                            eng.wait_ge(gpsimd_done.sem, at(gpsimd_done, pool_at["bias", u]))
                        else:
                            eng.wait_ge(vector_done.sem, at(vector_done, dve_at["expert_out", 1, 1]))
                        eng.tensor_tensor(dst[:, :, :].rearrange("p t c -> p (t c)"), bank(step),
                                                     dst[:, :, :].rearrange("p t c -> p (t c)"), ALU.add).then_inc(vector_done.sem, 1)
                        n = vector_done.count()
                        free(step, 0, n)
                        dve_at[step] = n
                    elif kind == "route":
                        layer = step[1]
                        src = bank(step)[:, 0:TILES * EXPERTS].rearrange("p (t e) -> p t e", t=TILES)

                        def wide(t):
                            return t[:, :].unsqueeze(2).to_broadcast([P, TILES, EXPERTS])

                        if layer == 0:
                            br = rows[:, ROW_BR:ROW_BR + EXPERTS]
                            for t in range(TILES):
                                eng.tensor_tensor(logit[:, t, :], src[:, t, :], br, ALU.add).then_inc(vector_done.sem, 1)
                                n = vector_done.count()
                        else:
                            eng.tensor_copy(logit[:, :, :], src).then_inc(vector_done.sem, 1)
                            n = vector_done.count()
                        free(step, 0, n)
                        eng.wait_ge(vector_done.sem, at(vector_done, n))
                        eng.tensor_reduce(gate_s[:, :], logit[:, :, :], AX_X, ALU.max).then_inc(vector_done.sem, 1)
                        eng.wait_ge(vector_done.sem, at(vector_done, vector_done.count()))
                        eng.tensor_tensor(gate_a[:, :, :], logit[:, :, :], wide(gate_s), ALU.subtract).then_inc(vector_done.sem, 1)
                        n = vector_done.count()
                        dve_at["logit", layer] = n
                        if layer == 0:
                            for t in range(TILES):
                                eng.max(top8[:, t, :], logit[:, t, :]).then_inc(vector_done.sem, 1)
                                n = vector_done.count()
                            eng.wait_ge(vector_done.sem, at(vector_done, n))
                            eng.tensor_tensor(gate_c[:, :, :], logit[:, :, :],
                                                         top8[:, :, 1:2].to_broadcast([P, TILES, EXPERTS]),
                                                         ALU.is_ge).then_inc(vector_done.sem, 1)
                            eng.wait_ge(vector_done.sem, at(vector_done, vector_done.count()))
                            eng.wait_ge(scalar_done.sem, at(scalar_done, act_at["gate_exp", 0]))
                            eng.tensor_tensor(gate_b[:, :, :], gate_b[:, :, :], gate_c[:, :, :], ALU.mult).then_inc(vector_done.sem, 1)
                            eng.wait_ge(vector_done.sem, at(vector_done, vector_done.count()))
                            eng.tensor_reduce(gate_s[:, :], gate_b[:, :, :], AX_X, ALU.add).then_inc(vector_done.sem, 1)
                            eng.wait_ge(vector_done.sem, at(vector_done, vector_done.count()))
                            eng.reciprocal(gate_t[:, :], gate_s[:, :]).then_inc(vector_done.sem, 1)
                            eng.wait_ge(vector_done.sem, at(vector_done, vector_done.count()))
                            eng.tensor_tensor(gate[:, :, :], gate_b[:, :, :], wide(gate_t), ALU.mult).then_inc(vector_done.sem, 1)
                            n = vector_done.count()
                        else:
                            eng.wait_ge(scalar_done.sem, at(scalar_done, act_at["gate_exp", 1]))
                            eng.tensor_reduce(gate_s[:, :], gate_b[:, :, :], AX_X, ALU.add).then_inc(vector_done.sem, 1)
                            eng.wait_ge(vector_done.sem, at(vector_done, vector_done.count()))
                            eng.reciprocal(gate_t[:, :], gate_s[:, :]).then_inc(vector_done.sem, 1)
                            eng.wait_ge(vector_done.sem, at(vector_done, vector_done.count()))
                            eng.tensor_tensor(logit[:, :, :], gate_b[:, :, :], wide(gate_t), ALU.mult).then_inc(vector_done.sem, 1)
                            n = vector_done.count()
                            eng.wait_ge(vector_done.sem, at(vector_done, n))
                            left = logit
                            for turn, picked in enumerate((gate_a, gate_b)):
                                eng.tensor_reduce(gate_s[:, :], left[:, :, :], AX_X, ALU.max).then_inc(vector_done.sem, 1)
                                eng.wait_ge(vector_done.sem, at(vector_done, vector_done.count()))
                                eng.tensor_tensor(gate_c[:, :, :], left[:, :, :], wide(gate_s), ALU.is_ge).then_inc(vector_done.sem, 1)
                                eng.wait_ge(vector_done.sem, at(vector_done, vector_done.count()))
                                eng.tensor_tensor(gate_c[:, :, :], gate_c[:, :, :], rank[:, :, :], ALU.mult).then_inc(vector_done.sem, 1)
                                eng.wait_ge(vector_done.sem, at(vector_done, vector_done.count()))
                                eng.tensor_reduce(gate_t[:, :], gate_c[:, :, :], AX_X, ALU.max).then_inc(vector_done.sem, 1)
                                eng.wait_ge(vector_done.sem, at(vector_done, vector_done.count()))
                                eng.tensor_tensor(picked[:, :, :], gate_c[:, :, :], wide(gate_t),
                                                             ALU.is_equal).then_inc(vector_done.sem, 1)
                                eng.wait_ge(vector_done.sem, at(vector_done, vector_done.count()))
                                if turn == 0:
                                    eng.scalar_tensor_tensor(out=top8[:, :, :], in0=picked[:, :, :],
                                                                        scalar=-2.0, in1=logit[:, :, :],
                                                                        op0=ALU.mult, op1=ALU.add).then_inc(vector_done.sem, 1)
                                    eng.wait_ge(vector_done.sem, at(vector_done, vector_done.count()))
                                    left = top8
                            eng.tensor_tensor(gate_a[:, :, :], gate_a[:, :, :], gate_b[:, :, :], ALU.add).then_inc(vector_done.sem, 1)
                            eng.wait_ge(vector_done.sem, at(vector_done, vector_done.count()))
                            eng.tensor_tensor(gate[:, :, :], gate_a[:, :, :], logit[:, :, :], ALU.mult).then_inc(vector_done.sem, 1)
                            n = vector_done.count()
                        dve_at[step] = n
                    elif kind == "route_turn":
                        eng.tensor_copy(gateT[:, :], bank(step)[0:EXPERTS, :]).then_inc(vector_done.sem, 1)
                        n = vector_done.count()
                        free(step, 0, n)
                        dve_at[step] = n
                    elif kind == "route_bias":
                        eng.wait_ge(vector_done.sem, at(vector_done, dve_at["norm", "a"] + 1 if step[1] == 0 else dve_at["norm", "y"]))
                        flat = acc[:, :, :].rearrange("p t c -> p (t c)")
                        eng.tensor_tensor(flat, bank(step), flat, ALU.add).then_inc(vector_done.sem, 1)
                        n = vector_done.count()
                        free(step, 0, n)
                        dve_at[step] = n
                    elif kind == "expert_out":
                        _, layer, e = step
                        for k in range(1 if layer == 0 else 4):
                            expert = e if layer == 0 else 4 * e + k
                            if layer == 0 or k == 3:
                                eng.wait_ge(values_done.sem, at(values_done, slot_of["expert_in", layer, e] + 1))
                            else:
                                eng.wait_ge(expert_sum.sem, at(expert_sum, 3 * e + k + 1))
                            src = sum_bank[(sum_of[step] + k) % 2]
                            eng.wait_ge(vector_done.sem, at(vector_done, vector_done.n))
                            for t in range(TILES):
                                eng.scalar_tensor_tensor(
                                    out=acc[:, t, :], in0=src[:, t * P:(t + 1) * P],
                                    scalar=gate[:, t, expert:expert + 1], in1=acc[:, t, :],
                                    op0=ALU.mult, op1=ALU.add).then_inc(vector_done.sem, 1)
                                n = vector_done.count()
                            sum_freed_dve[sum_of[step] + k] = n
                        dve_at[step] = n
                eng.wait_ge(vector_done.sem, at(vector_done, vector_done.n))
                eng.sem_inc(vector_done.sem, PER - vector_done.n)
                eng.sem_inc(arrived["dve"], 1)
                eng.wait_ge(arrived["pe"], counts.number)
                eng.sem_inc(passed["dve"], 1)
                eng.wait_ge(arrived["act"], counts.number)
                eng.sem_inc(passed["dve"], 1)
                eng.wait_ge(arrived["pool"], counts.number)
                eng.sem_inc(passed["dve"], 1)
                eng.wait_ge(arrived["sp"], counts.number)
                eng.sem_inc(passed["dve"], 1)

        @block.scalar
        def _(eng):
            eng.wait_ge(loaded, 16 * N_LOADS)
            counts = Counts(eng, "act")
            at = counts.at
            with eng.Fori(0, BATCH) as b:
                counts.sequence(b)

                def slot_free(step):
                    if slot_of[step] >= 3:
                        eng.wait_ge(values_done.sem, at(values_done, slot_of[step] - 2))

                for step in plan:
                    kind = step[0]
                    if kind == "project":
                        u = step[1]
                        for k in range(2):
                            eng.wait_ge(vector_done.sem, at(vector_done, dve_at["rest", u, k]))
                            eng.activation(part[u % 2][:, k, 1, :], rest[:, k, :], ACT.Copy).then_inc(scalar_done.sem, 1)
                            n = scalar_done.count()
                            assert n == act_at["part", u, k]
                    elif kind == "scores":
                        _, u, g, j = step
                        slot = slot_of[step] % 3
                        slot_free(step)
                        for k, (hs, width, per_bank) in enumerate(score_pairs(u, j)):
                            n = first_pair[step] + k
                            eng.wait_ge(pair_full.sem, at(pair_full, n + 1))
                            dst = probs[:, slot, hs[0]:hs[0] + len(hs), TILES * P - width:TILES * P]
                            if per_bank == 1:
                                src = pair_bank[n % 2][:, :, 0:width]
                            else:
                                src = pair_bank[n % 2].rearrange("p a q -> p (a q)")[:, 0:len(hs) * width]
                                src = src.rearrange("p (h q) -> p h q", h=len(hs))
                            eng.activation(dst, src, ACT.Exp, scale=SCALE).then_inc(probs_ready.sem, 1)
                            probs_ready.count()
                            assert probs_ready.n == n + 1
                    elif kind == "values" and step[3] == TILES - 1:
                        _, u, g, j = step
                        eng.wait_ge(values_done.sem, at(values_done, slot_of["scores", u, g, j] + 1))
                        q = head_quads.index((u, g))
                        if q >= 2:
                            eng.wait_ge(work_full.sem, at(work_full, first_work["heads_turn", *head_quads[q - 2]] + 1))
                        eng.activation(head_sums[:, q % 2, :], sum_bank[sum_of[step] % 2], ACT.Copy).then_inc(scalar_done.sem, 1)
                        n = scalar_done.count()
                        assert n == act_at["sums", u, g]
                    elif kind == "route":
                        eng.wait_ge(vector_done.sem, at(vector_done, dve_at["logit", step[1]]))
                        eng.activation(gate_b[:, :, :], gate_a[:, :, :], ACT.Exp).then_inc(scalar_done.sem, 1)
                        n = scalar_done.count()
                        assert n == act_at["gate_exp", step[1]]
                    elif kind == "expert_in":
                        _, layer, e = step
                        slot = slot_of[step] % 3
                        slot_free(step)
                        for k in range(4):
                            n = first_pair[step] + k // 2
                            if k % 2 == 0:
                                eng.wait_ge(pair_full.sem, at(pair_full, n + 1))
                            c = COL_EB1 + 4 * e + k if layer == 0 else COL_BIN + 4 * e + k
                            ins = eng.activation(probs[:, slot, k, :], pair_bank[n % 2][:, k % 2, :],
                                                 ACT.Gelu if layer == 0 else ACT.Gelu_apprx_tanh,
                                                 bias=col[:, c:c + 1])
                            if k % 2:
                                ins.then_inc(probs_ready.sem, 1)
                                probs_ready.count()
                eng.wait_ge(scalar_done.sem, at(scalar_done, scalar_done.n))
                eng.sem_inc(scalar_done.sem, PER - scalar_done.n)
                eng.wait_ge(probs_ready.sem, at(probs_ready, probs_ready.n))
                eng.sem_inc(probs_ready.sem, PER - probs_ready.n)
                eng.sem_inc(arrived["act"], 1)
                eng.wait_ge(arrived["pe"], counts.number)
                eng.sem_inc(passed["act"], 1)
                eng.wait_ge(arrived["dve"], counts.number)
                eng.sem_inc(passed["act"], 1)
                eng.wait_ge(arrived["pool"], counts.number)
                eng.sem_inc(passed["act"], 1)
                eng.wait_ge(arrived["sp"], counts.number)
                eng.sem_inc(passed["act"], 1)

        @block.tensor
        def _(eng):
            eng.wait_ge(loaded, 16 * N_LOADS)
            eng.wait_ge(made, N_MADE)
            eng.wait_ge(cleared, N_CLEARED)
            counts = Counts(eng, "pe")
            at = counts.at
            with eng.Fori(0, BATCH) as b:
                counts.sequence(b)

                def bank(step, k=0):
                    n = first_work[step] + k
                    if n >= 2:
                        eng.wait_ge(vector_done.sem, at(vector_done, work_freed[n - 2]))
                    return work_bank[n % 2]

                def pair(n):
                    if n >= 2:
                        eng.wait_ge(probs_ready.sem, at(probs_ready, n - 1))
                    return pair_bank[n % 2]

                for step in plan:
                    kind = step[0]
                    if kind == "turn":
                        src = hn if step[1] in ("h", "a") else xn
                        eng.wait_ge(vector_done.sem, at(vector_done, dve_at["norm", step[1]]))
                        dst = bank(step)
                        for t in range(TILES):
                            ins = eng.transpose(dst[:, t * P:(t + 1) * P], src[:, t, :], ident[:, :])
                        ins.then_inc(work_full.sem, 1)
                        work_full.count()
                    elif kind == "project":
                        u = step[1]
                        src = hT if u == 1 else xT
                        eng.wait_ge(vector_done.sem, at(vector_done, dve_at["turn", ("x", "h", "y")[u]]))
                        for k in range(2):
                            eng.matmul(bank(step, k), projs[:, u, k, :], src[:, :],
                                                    start=True, stop=True).then_inc(work_full.sem, 1)
                            work_full.count()
                        dst = bank(step, 2)
                        for t in range(TILES):
                            ins = eng.matmul(dst[:, t * P:(t + 1) * P], src[:, t * P:(t + 1) * P], projs[:, u, 2, :],
                                             start=True, stop=True)
                        ins.then_inc(work_full.sem, 1)
                        work_full.count()
                    elif kind == "max":
                        _, u, g, i = step
                        if (g, i) == (0, 0):
                            eng.wait_ge(q_landed[u].sem, at(q_landed[u], 16 * STACK_DMAS))
                            eng.wait_ge(k_landed[u].sem, at(k_landed[u], 16 * STACK_DMAS))
                        qs, ks = q_stack[u % 2], k_stack[u % 2]
                        for k, (hs, keys) in enumerate(max_chunks(u, i)):
                            dst = bank(step, k)
                            for c, h in enumerate(hs):
                                col0 = c * keys
                                ins = eng.matmul(dst[:, col0:col0 + keys], qs[0:MAX_ROW, 4 * g + h, i * P:(i + 1) * P],
                                                 ks[0:MAX_ROW, 4 * g + h, 0:keys], start=True, stop=not CAUSAL[u])
                                if CAUSAL[u]:
                                    ins = eng.matmul(dst[:, col0 + keys - P:col0 + keys], ident16[:, :], mask_qk[:, :],
                                                     start=False, stop=True)
                            ins.then_inc(work_full.sem, 1)
                            work_full.count()
                    elif kind == "max_turn":
                        q = max_quads.index(step[1:])
                        dst = bank(step)[0:PARTS * QH * TILES, 0:P // 2].bitcast(BF16)
                        eng.wait_ge(vector_done.sem, at(vector_done, dve_at["max_part", step[1], step[2]]))
                        eng.sem_inc(passed["pe"], 1)
                        eng.transpose(dst, max_part[:, q % 2].rearrange("p a b -> p (a b)"),
                                                   ident16[:, :]).then_inc(work_full.sem, 1)
                        work_full.count()
                    elif kind == "scores":
                        _, u, g, j = step
                        if j == 0:
                            q = max_quads.index((u, g))
                            eng.wait_ge(max_landed[q % 2].sem, at(max_landed[q % 2], 16 * (q // 2 + 1)))
                        qs, ks = q_stack[u % 2], k_stack[u % 2]
                        for k, (hs, width, per_bank) in enumerate(score_pairs(u, j)):
                            dst = pair(first_pair[step] + k)
                            for c, h in enumerate(hs):
                                col0 = (c % per_bank) * width
                                o = dst[:, c // per_bank, col0:col0 + width]
                                ins = eng.matmul(o, ks[:, 4 * g + h, j * P:(j + 1) * P],
                                                 qs[:, 4 * g + h, TILES * P - width:TILES * P],
                                                 start=True, stop=not CAUSAL[u])
                                if CAUSAL[u]:
                                    ins = eng.matmul(o[:, 0:P], ident16[:, :], mask_kq[:, :], start=False, stop=True)
                            ins.then_inc(pair_full.sem, 1)
                            pair_full.count()
                    elif kind == "values":
                        _, u, g, j = step
                        n = sum_of[step]
                        score = ("scores", u, g, j)
                        if j == 0 and n >= 2:
                            if n - 2 in sum_freed_dve:
                                eng.wait_ge(vector_done.sem, at(vector_done, sum_freed_dve[n - 2]))
                            else:
                                eng.wait_ge(scalar_done.sem, at(scalar_done, sum_freed_act[n - 2]))
                        if j == 0:
                            eng.wait_ge(vector_done.sem, at(vector_done, dve_at["v", u]))
                        eng.wait_ge(probs_ready.sem, at(probs_ready, first_pair[score] + pairs(score)))
                        width = P * (TILES - j) if CAUSAL[u] else P * TILES
                        q0 = TILES * P - width
                        for c in range(QH):
                            ins = eng.matmul(sum_bank[n % 2][32 * c:32 * c + 32, q0:TILES * P],
                                             v_ones[u % 2][:, j, 4 * g + c, :],
                                             probs[:, slot_of[score] % 3, c, q0:TILES * P],
                                             start=(j == 0), stop=(j == TILES - 1))
                        ins.then_inc(values_done.sem, 1)
                        values_done.count()
                    elif kind == "heads_turn":
                        _, u, g = step
                        eng.wait_ge(scalar_done.sem, at(scalar_done, act_at["sums", u, g]))
                        q = head_quads.index((u, g))
                        dst = bank(step)
                        for t in range(TILES):
                            ins = eng.transpose(dst[:, t * P:(t + 1) * P], head_sums[:, q % 2, t * P:(t + 1) * P],
                                                ident[:, :])
                        ins.then_inc(work_full.sem, 1)
                        work_full.count()
                    elif kind == "heads_back":
                        eng.wait_ge(vector_done.sem, at(vector_done, dve_at["heads_turn", step[1], QUADS - 1]))
                        dst = bank(step)
                        for t in range(TILES):
                            ins = eng.transpose(dst[:, t * P:(t + 1) * P], heads[:, t, :], ident[:, :])
                        ins.then_inc(work_full.sem, 1)
                        work_full.count()
                    elif kind == "out_project":
                        eng.wait_ge(vector_done.sem, at(vector_done, dve_at["heads_back", step[1]]))
                        dst = bank(step)
                        for t in range(TILES):
                            ins = eng.matmul(dst[:, t * P:(t + 1) * P], headsT[:, t * P:(t + 1) * P],
                                             projs[:, step[1], 3, :], start=True, stop=True)
                        ins.then_inc(work_full.sem, 1)
                        work_full.count()
                    elif kind == "route":
                        src = hT if step[1] == 0 else xT
                        eng.wait_ge(vector_done.sem, at(vector_done, dve_at["turn", "a" if step[1] == 0 else "y"]))
                        dst = bank(step)
                        for t in range(TILES):
                            ins = eng.matmul(dst[:, t * EXPERTS:(t + 1) * EXPERTS], src[:, t * P:(t + 1) * P],
                                             router[:, step[1], :], start=True, stop=True)
                        ins.then_inc(work_full.sem, 1)
                        work_full.count()
                    elif kind == "route_turn":
                        eng.wait_ge(vector_done.sem, at(vector_done, dve_at["route", step[1]]))
                        dst = bank(step)
                        for t in range(TILES):
                            ins = eng.transpose(dst[0:EXPERTS, t * P:(t + 1) * P], gate[:, t, :], ident[:, :])
                        ins.then_inc(work_full.sem, 1)
                        work_full.count()
                    elif kind == "route_bias":
                        eng.wait_ge(vector_done.sem, at(vector_done, dve_at["route_turn", step[1]]))
                        dst = bank(step)
                        for t in range(TILES):
                            ins = eng.matmul(dst[:, t * P:(t + 1) * P], gateT[:, t * P:(t + 1) * P],
                                             ebias[:, step[1], :], start=True, stop=True)
                        ins.then_inc(work_full.sem, 1)
                        work_full.count()
                    elif kind == "expert_in":
                        _, layer, e = step
                        src = hT if layer == 0 else xT
                        if e == 0:
                            eng.wait_ge(experts_loaded, 16 * N_EXPERT_LOADS)
                        for k in range(4):
                            if k % 2 == 0:
                                dst = pair(first_pair[step] + k // 2)
                            w = ew1[:, e, k, :] if layer == 0 else win[:, 4 * e + k, :]
                            ins = eng.matmul(dst[:, k % 2, :], w, src[:, :], start=True, stop=True)
                            if k % 2:
                                ins.then_inc(pair_full.sem, 1)
                                pair_full.count()
                    elif kind == "expert_out":
                        _, layer, e = step
                        source = ("expert_in", layer, e)
                        slot = slot_of[source] % 3
                        eng.wait_ge(probs_ready.sem, at(probs_ready, first_pair[source] + 2))
                        for k in range(1 if layer == 0 else 4):
                            n = sum_of[step] + k
                            if n - 2 in sum_freed_dve:
                                eng.wait_ge(vector_done.sem, at(vector_done, sum_freed_dve[n - 2]))
                            else:
                                eng.wait_ge(scalar_done.sem, at(scalar_done, sum_freed_act[n - 2]))
                            dst = sum_bank[n % 2]
                            for t in range(TILES):
                                chunks = range(4) if layer == 0 else (k,)
                                for f in chunks:
                                    w = ew2[:, e, f, :] if layer == 0 else wout[:, 4 * e + k, :]
                                    ins = eng.matmul(dst[:, t * P:(t + 1) * P], probs[:, slot, f, t * P:(t + 1) * P],
                                                     w, start=f == chunks[0], stop=f == chunks[-1])
                            ins.then_inc((values_done if layer == 0 or k == 3 else expert_sum).sem, 1)
                            (values_done if layer == 0 or k == 3 else expert_sum).count()
                eng.wait_ge(work_full.sem, at(work_full, work_full.n))
                eng.sem_inc(work_full.sem, PER - work_full.n)
                eng.wait_ge(pair_full.sem, at(pair_full, pair_full.n))
                eng.sem_inc(pair_full.sem, PER - pair_full.n)
                eng.wait_ge(values_done.sem, at(values_done, values_done.n))
                eng.sem_inc(values_done.sem, PER - values_done.n)
                eng.wait_ge(expert_sum.sem, at(expert_sum, expert_sum.n))
                eng.sem_inc(expert_sum.sem, PER - expert_sum.n)
                eng.sem_inc(arrived["pe"], 1)
                eng.wait_ge(arrived["act"], counts.number)
                eng.sem_inc(passed["pe"], 1)
                eng.wait_ge(arrived["dve"], counts.number)
                eng.sem_inc(passed["pe"], 1)
                eng.wait_ge(arrived["pool"], counts.number)
                eng.sem_inc(passed["pe"], 1)
                eng.wait_ge(arrived["sp"], counts.number)
                eng.sem_inc(passed["pe"], 1)

        @block.gpsimd
        def _(eng):
            eng.memset(ident[:, :], 0.0).then_inc(made, 1)
            eng.memset(mask_qk[:, :], 0.0).then_inc(made, 1)
            eng.memset(mask_kq[:, :], 0.0).then_inc(made, 1)
            for n, stack in enumerate((q_stack[1], k_stack[1])):
                eng.wait_ge(made, 3 + n)
                eng.memset(stack[64:P, :, :].bitcast(mybir.dt.uint32), 0).then_inc(made, 1)
            eng.wait_ge(made, 5)
            eng.memset(k_stack[1][MAX_ROW:MAX_ROW + PARTS, :, :].bitcast(mybir.dt.uint32), 0x3F803F80)\
               .then_inc(made, 1)
            eng.wait_ge(made, 6)
            eng.affine_select(out=ident[:, :], in_=ident[:, :], compare_op=ALU.not_equal, fill=1.0, base=0,
                              pattern=[[-1, P]], channel_multiplier=1).then_inc(made, 1)
            eng.affine_select(out=mask_qk[:, :], in_=mask_qk[:, :], compare_op=ALU.is_ge, fill=MASKED, base=0,
                              pattern=[[-1, P]], channel_multiplier=1).then_inc(made, 1)
            eng.affine_select(out=mask_kq[:, :], in_=mask_kq[:, :], compare_op=ALU.is_ge, fill=MASKED, base=0,
                              pattern=[[1, P]], channel_multiplier=-1).then_inc(made, 1)
            eng.wait_ge(loaded, 16 * N_LOADS)
            eng.wait_ge(cleared, N_CLEARED)
            counts = Counts(eng, "pool")
            at = counts.at
            with eng.Fori(0, BATCH) as b:
                counts.sequence(b)

                for step in plan:
                    kind = step[0]
                    if kind == "norm":
                        eng.wait_ge(vector_done.sem, at(vector_done, dve_at["pow", step[1]]))
                        eng.tensor_tensor(rstd[:, :], var_eps[:, :], minus_half[:, :], ALU.pow).then_inc(gpsimd_done.sem, 1)
                        n = gpsimd_done.count()
                        assert n == pool_at["pow", step[1]]
                        if step[1] == "h":
                            for u, (dst, src, row0) in enumerate(((x_bias, x_in, ROW_BOUT), (a_sum, xn, ROW_BO))):
                                bias = rows[:, row0:row0 + P]
                                for t in range(TILES):
                                    eng.tensor_tensor(dst[:, t, :], src[:, t, :], bias, ALU.add).then_inc(gpsimd_done.sem, 1)
                                    n = gpsimd_done.count()
                                assert n == pool_at["bias", u]
                    elif kind == "project":
                        u = step[1]
                        for j in (0, 1, 2):
                            if j == 0:
                                eng.wait_ge(vector_done.sem, at(vector_done, dve_at["rest", u, 1]))
                                eng.sem_inc(passed["pool"], 1)
                            elif j == 1:
                                eng.wait_ge(scalar_done.sem, at(scalar_done, act_at["part", u, 1]))
                                eng.sem_inc(passed["pool"], 1)
                            else:
                                eng.wait_ge(vector_done.sem, at(vector_done, dve_at["part3", u, 1]))
                                eng.sem_inc(passed["pool"], 1)
                            for i in range(PARTS):
                                r = 24 * i + 8 * j
                                eng.dma_start(k_stack[u % 2][r:r + 8, :, :], part[u % 2][:, 1, j, :]).then_inc(k_landed[u].sem, 16)
                                k_landed[u].count()
                eng.wait_ge(gpsimd_done.sem, at(gpsimd_done, gpsimd_done.n))
                eng.sem_inc(gpsimd_done.sem, PER - gpsimd_done.n)
                eng.sem_inc(arrived["pool"], 1)
                eng.wait_ge(arrived["pe"], counts.number)
                eng.sem_inc(passed["pool"], 1)
                eng.wait_ge(arrived["act"], counts.number)
                eng.sem_inc(passed["pool"], 1)
                eng.wait_ge(arrived["dve"], counts.number)
                eng.sem_inc(passed["pool"], 1)
                eng.wait_ge(arrived["sp"], counts.number)
                eng.sem_inc(passed["pool"], 1)

        @block.sync
        def _(eng):
            for dst, src in ((projs[:, :, :, :], proj), (col[:, :], cols), (router[:, :, :], routers),
                             (rows[:, :], row.to_broadcast([P, N_ROW])), (ebias[:, :, :], expert_bias)):
                eng.dma_start(dst, src).then_inc(loaded, 16)
            for dst, src in ((ew1[:, :, :, :], w_expert_in), (ew2[:, :, :, :], w_expert_out),
                             (win[:, :, :], w_in), (wout[:, :, :], w_out)):
                eng.dma_start(dst, src).then_inc(experts_loaded, 16)
            eng.wait_ge(cleared, N_CLEARED)
            counts = Counts(eng, "sp")
            at = counts.at
            with eng.Fori(0, BATCH) as b:
                counts.sequence(b)

                for step in plan:
                    kind = step[0]
                    if kind == "load":
                        eng.dma_start(x_in[:, :, :], x[bass.ds(b, 1), :, :].rearrange("b (t p) c -> p (b t) c", p=P)).then_inc(x_landed.sem, 16)
                        x_landed.count()
                    elif kind == "project":
                        u = step[1]
                        for i in (0, 1, 2):
                            if i == 0:
                                eng.wait_ge(vector_done.sem, at(vector_done, dve_at["rest", u, 0]))
                                eng.sem_inc(passed["sp"], 1)
                            elif i == 1:
                                eng.wait_ge(scalar_done.sem, at(scalar_done, act_at["part", u, 0]))
                                eng.sem_inc(passed["sp"], 1)
                            else:
                                eng.wait_ge(vector_done.sem, at(vector_done, dve_at["part3", u, 0]))
                                eng.sem_inc(passed["sp"], 1)
                            for j in range(PARTS):
                                r = 24 * i + 8 * j
                                eng.dma_start(q_stack[u % 2][r:r + 8, :, :], part[u % 2][:, 0, i, :]).then_inc(q_landed[u].sem, 16)
                                q_landed[u].count()
                    elif kind == "max_turn":
                        _, u, g = step
                        q = max_quads.index((u, g))
                        eng.wait_ge(vector_done.sem, at(vector_done, dve_at[step]))
                        eng.sem_inc(passed["sp"], 1)
                        eng.dma_start(q_stack[u % 2][MAX_ROW:MAX_ROW + PARTS, 4 * g:4 * g + 4, :],
                                                    maxT[:, q % 2, :]).then_inc(max_landed[q % 2].sem, 16)
                        max_landed[q % 2].count()
                    elif kind == "store":
                        eng.wait_ge(vector_done.sem, at(vector_done, dve_at["out_project", 2]))
                        eng.sem_inc(passed["sp"], 1)
                        eng.dma_start(out[bass.ds(b, 1), :, :].rearrange("b (t p) c -> p (b t) c", p=P),
                                                acc[:, :, :]).then_inc(stored.sem, 16)
                        stored.count()
                eng.wait_ge(stored.sem, at(stored, 16))
                eng.sem_inc(passed["sp"], 1)
                eng.sem_inc(arrived["sp"], 1)
                eng.wait_ge(arrived["pe"], counts.number)
                eng.sem_inc(passed["sp"], 1)
                eng.wait_ge(arrived["act"], counts.number)
                eng.sem_inc(passed["sp"], 1)
                eng.wait_ge(arrived["dve"], counts.number)
                eng.sem_inc(passed["sp"], 1)
                eng.wait_ge(arrived["pool"], counts.number)
                eng.sem_inc(passed["sp"], 1)


def kernel(**inputs):
    import numpy as np
    import concourse.bacc as bacc
    from concourse.bass_utils import run_bass_kernel_spmd

    a = {name: np.asarray(value) for name, value in inputs.items()}
    D = a["L0_attn_x"].shape[2]

    def by_channel(w):
        return w.reshape(*w.shape[:-1], HEADS, HD).swapaxes(-1, -2).reshape(w.shape)

    def of_heads(w):
        return w.transpose(1, 0, 2).reshape(D, D)

    wqkv = a["L0_attn_w_qkv"]
    proj = np.stack([
        np.stack([by_channel(wqkv[:, 0:D]), by_channel(wqkv[:, D:2 * D]), wqkv[:, 2 * D:], a["L0_attn_w_out"]], 1),
        np.stack([by_channel(a["L0_ffn_Wq"]), by_channel(a["L0_ffn_Wk"]), a["L0_ffn_Wv"], a["L0_ffn_Wo"]], 1),
        np.stack([by_channel(of_heads(a["L1_attn_W_query"])), by_channel(of_heads(a["L1_attn_W_key"])),
                  of_heads(a["L1_attn_W_val"]), a["L1_attn_W_out"].reshape(D, D)], 1)], 1)
    cols = np.stack([a["L0_ffn_ln1_g"], a["L0_ffn_ln1_b"], a["L0_ffn_ln2_g"], a["L0_ffn_ln2_b"],
                     by_channel(a["L0_ffn_bq"]), by_channel(a["L0_ffn_bk"]),
                     *a["L0_ffn_e_b1"].reshape(4 * EXPERTS, D), *a["L1_ffn_b_in"]], 1)
    row = np.concatenate([a["L0_attn_b_out"], a["L0_ffn_bo"], a["L0_ffn_bv"], a["L0_ffn_br"]])[None, :]
    arrays = {
        "x": a["L0_attn_x"],
        "proj": proj,
        "w_expert_in": a["L0_ffn_e_w1"].transpose(1, 0, 2).reshape(D, EXPERTS, 4, D),
        "w_expert_out": a["L0_ffn_e_w2"].reshape(EXPERTS, 4, D, D).transpose(2, 0, 1, 3),
        "w_in": a["L1_ffn_w_in"].transpose(1, 0, 2),
        "w_out": a["L1_ffn_w_out"].transpose(1, 0, 2),
        "routers": np.stack([a["L0_ffn_Wr"], a["L1_ffn_router_w"]], 1),
        "cols": cols,
        "row": row,
        "expert_bias": np.stack([a["L0_ffn_e_b2"], a["L1_ffn_b_out"]], 1),
    }
    arrays = {name: np.ascontiguousarray(value) for name, value in arrays.items()}
    nc = bacc.Bacc("TRN2", target_bir_lowering=False, num_devices=1)
    args = [nc.dram_tensor(name, value.shape, F32, kind="ExternalInput").ap() for name, value in arrays.items()]
    out = nc.dram_tensor("out", arrays["x"].shape, F32, kind="ExternalOutput").ap()
    build(nc, *args, out)
    result = run_bass_kernel_spmd(nc, [arrays], core_ids=[0])
    return result.results[0]["out"]
```

```python
from contextlib import ExitStack

import concourse.bass as bass
from concourse import mybir

F32 = mybir.dt.float32
BF16 = mybir.dt.bfloat16
ALU = mybir.AluOpType
ACT = mybir.ActivationFunctionType
AX_X = mybir.AxisListType.X

P = 128
TILES = 4
HEADS, HD = 16, 8
QUADS, QH = 4, 4
EXPERTS = 8
EPS = 1e-5
SCALE = float(HD) ** -0.5
WORK_BANKS = 3
PARTS = 3
MAX_ROW = 96
SUM_COL = 8
MASKED = -1e30
PER = 2048
CAUSAL = (True, True, False)

COL_G1, COL_B1, COL_G2, COL_B2, COL_BQ, COL_BK, COL_EB1 = range(7)
COL_BIN = COL_EB1 + 4 * EXPERTS
N_COLS = COL_BIN + EXPERTS
ROW_BOUT, ROW_BO, ROW_BV, ROW_BR = 0, P, 2 * P, 3 * P
N_ROW = 3 * P + EXPERTS


SLOT = {(1, 0): 0, (1, 1): 1, (0, 0): 2, (0, 1): 0, (2, 0): 1, (2, 1): 2}

COST = {"max": 3, "expert_in": 17, "expert_out": 17, "scores": 5, "values": 9, "project": 9, "turn": 5,
        "heads_turn": 4, "heads_back": 4, "out_project": 9, "route": 2, "route_turn": 4, "route_bias": 9}


def spread(main, extra):
    out, done, total, n = [], 0, sum(COST.get(step[0][0], 0) for step in main), 0
    for step in main:
        while n < len(extra) and done * len(extra) >= total * (n + 0.5):
            out.append(extra[n])
            n += 1
        out.append(step)
        done += COST.get(step[0][0], 0)
    return out + extra[n:]


def now(*steps):
    return [(step, False) for step in steps]


def ahead(*steps):
    return [(step, True) for step in steps]


def maxima(u, g, of=now):
    return of(*(("max", u, g, i, k) for i in range(TILES) for k in range(len(max_chunks(u, i)))))


def window(u, g, of, before=None, early=(), extra=(), late=()):
    steps = []
    for j in range(TILES):
        for k in range(len(score_pairs(u, j))):
            steps += of(("scores", u, g, j, k))
            if k == 0 and j == 0 and before:
                steps += before
            if k == 0 and j:
                steps += of(("values", u, g, j - 1))
            if k == 0 and j == 1:
                steps += early
    return spread(steps, list(extra)) + list(late)


def plans():
    def rest(u, g, of):
        return of(("values", u, g, TILES - 1))

    def turn(u, g, of=now):
        return of(("max_turn", u, g))

    def heads(u, g, of=now):
        return of(("heads_turn", u, g))

    def projection(u):
        return (("project", u, 0), ("project", u, 1), ("project", u, 2), ("parts", u))

    def stack(u, half):
        return tuple(("stack", u, half, n) for n in range(PARTS))

    p = []
    p += ahead(("load",))
    p += window(1, 0, now, extra=maxima(1, 2) + ahead(("stats", "x")),
                late=ahead(("norm", "x")))
    p += window(1, 1, now, rest(1, 0, now), early=turn(1, 2) + heads(1, 0),
                extra=maxima(1, 3)[:3] + ahead(("turn", "x")) + maxima(1, 3)[3:7]
                + ahead(("project", 0, 0), ("project", 0, 1)) + maxima(1, 3)[7:], late=turn(1, 3))
    p += window(1, 2, now, rest(1, 1, now), early=heads(1, 1) + ahead(("project", 0, 2), ("parts", 0)),
                extra=ahead(*stack(0, 0), *stack(0, 1)))
    p += window(1, 3, now, rest(1, 2, now), early=heads(1, 2), extra=maxima(0, 0, ahead))
    p += rest(1, 3, now) + maxima(0, 1, ahead)[:2] + turn(0, 0, ahead) + heads(1, 3) + maxima(0, 1, ahead)[2:4]
    p += now(("heads_back", 1)) + maxima(0, 1, ahead)[4:7] + now(("out_project", 1)) + now(("stats", "a"))
    p += maxima(0, 1, ahead)[7:]
    p += window(0, 0, ahead, 
                extra=maxima(0, 2, ahead)[:1] + now(("norm", "a")) + turn(0, 1, ahead) + maxima(0, 2, ahead)[1:4]
                + now(("turn", "a")) + maxima(0, 2, ahead)[4:7] + now(("route", 0)) + maxima(0, 2, ahead)[7:])
    p += ahead(("bias", 0), ("bias", 1))
    p += window(0, 1, ahead, rest(0, 0, ahead), early=heads(0, 0, ahead) + turn(0, 2, ahead),
                extra=maxima(0, 3, ahead)[:7], late=rest(0, 1, ahead))
    mixture = []
    for e in range(EXPERTS + 1):
        if e < EXPERTS:
            mixture += now(("expert_in", 0, e, 0), ("expert_in", 0, e, 1))
        if e == 1:
            mixture += now(("route_turn", 0), ("route_bias", 0))
        if e == EXPERTS - 1:
            mixture += ahead(("turn", "h"))
        if e:
            mixture += now(("expert_out", 0, e - 1, 0), ("expert_out", 0, e - 1, 1))
        if e == EXPERTS - 1:
            mixture += ahead(*projection(1))
    p += mixture[:3] + heads(0, 1, ahead) + spread(mixture[3:30], ahead(("stats", "h"), ("norm", "h"))
                                                   + maxima(0, 3, ahead)[7:] + turn(0, 3, ahead)) + mixture[30:]
    p += now(("stats", "y"))
    p += window(0, 2, ahead, early=now(("norm", "y"), ("turn", "y")),
                extra=(), late=now(*projection(2)[:2]))
    p += window(0, 3, ahead, rest(0, 2, ahead), early=heads(0, 2, ahead) + now(("project", 2, 2), ("parts", 2)),
                extra=now(("route", 1), *stack(2, 0)), late=rest(0, 3, ahead))
    experts = now(("expert_in", 1, 0, 0), ("expert_in", 1, 0, 1)) + heads(0, 3, ahead) + now(*stack(2, 1))
    experts += now(("route_turn", 1)) + ahead(("heads_back", 0)) + now(("route_bias", 1)) + ahead(("out_project", 0))
    experts += now(("expert_in", 1, 1, 0), ("expert_in", 1, 1, 1), *(("expert_out", 1, 0, k) for k in range(4)))
    experts += now(*(("expert_out", 1, 1, k) for k in range(4)))
    p += experts[:3] + spread(experts[3:], maxima(2, 0) + turn(2, 0) + maxima(2, 1))
    p += window(2, 0, now, early=turn(2, 1), extra=maxima(2, 2))
    p += ahead(*stack(1, 0))
    p += window(2, 1, now, rest(2, 0, now), early=turn(2, 2) + heads(2, 0), extra=maxima(2, 3))
    p += window(2, 2, now, rest(2, 1, now), early=turn(2, 3) + heads(2, 1) + ahead(*stack(1, 1)),
                extra=maxima(1, 0, ahead))
    p += window(2, 3, now, rest(2, 2, now), early=turn(1, 0, ahead) + heads(2, 2), extra=maxima(1, 1, ahead)[:7],
                late=rest(2, 3, now) + maxima(1, 1, ahead)[7:9])
    p += heads(2, 3) + maxima(1, 1, ahead)[9:] + now(("heads_back", 2)) + turn(1, 1, ahead)
    p += now(("out_project", 2), ("store",))
    return ([step for step, is_ahead in p if is_ahead], [step for step, _ in p],
            [step for step, is_ahead in p if not is_ahead])


def score_pairs(u, j):
    width = P * (TILES - j) if CAUSAL[u] else P * TILES
    per_bank = {P: 4, 2 * P: 2}.get(width, 1)
    heads = min(QH, 2 * per_bank)
    return [(list(range(c, c + heads)), width, per_bank) for c in range(0, QH, heads)]


def max_chunks(u, i):
    keys = P * (i + 1) if CAUSAL[u] else P * TILES
    per_bank = {P: 4, 2 * P: 2}.get(keys, 1)
    return [(list(range(c, c + per_bank)), keys) for c in range(0, QH, per_bank)]


class Signal:

    def __init__(self, nc, ctx, name, step=1, first=PER, each=PER):
        self.sem = ctx.enter_context(nc.semaphore(name))
        self.step, self.n, self.first, self.each = step, 0, first, each

    def count(self):
        self.n += self.step
        return self.n


class Counts:

    def __init__(self, eng, name, signals):
        self.eng, self.k = eng, 0
        self.kinds = sorted({(sig.first, sig.each) for sig in signals})
        self.registers = [eng.alloc_register(f"{name}_count{i}") for i in range(6)]

    def begin(self, number, owned):
        self.base = {(first, each): first * min(number, 1) + each * max(number - 1, 0) for first, each in self.kinds}
        self.number, self.looped = number + 1, False
        for sig in owned:
            sig.n = 0

    def begin_looped(self, b, owned):
        self.base = {(first, each): self.eng.snap(b * each + first) for first, each in self.kinds}
        self.number, self.looped = self.eng.snap(b + 2), True
        for sig in owned:
            sig.n = 0

    def at(self, sig, n):
        base = self.base[sig.first, sig.each]
        if not self.looped:
            return base + n
        register = self.registers[self.k % len(self.registers)]
        self.k += 1
        self.eng.reg_add(register, base, n)
        return register


class Pass:

    def __init__(self, plan):
        self.plan = plan
        self.place = {step: n for n, step in enumerate(plan)}
        assert len(self.place) == len(plan)
        works = {kind: 1 for kind in ("turn", "project", "max", "max_turn", "heads_turn", "heads_back",
                                      "out_project", "route", "route_turn", "route_bias")}
        self.work, self.pair = {}, {}
        self.bank, self.bank_before = {}, {}
        self.slot, self.slot_before = {}, {}
        self.sum_before = {}
        self.done = {}
        self.act, self.pool = {}, {}
        self.dve = {}
        self.work_freed = {}
        self.stack_before = {}
        self.landed = {}
        n_act = n_pool = 0
        for step in plan:
            if step[0] == "heads_turn":
                assert self.before(("values", *step[1:], TILES - 1), step), step
            if step[0] == "max_turn":
                assert self.before(("max", *step[1:], TILES - 1, 0), step), step
            if step[0] == "scores" and not self.before(("max_turn", *step[1:3]), step):
                assert step[1] == 1 and step[2] < 2, step
        free_slots, free_banks, last = [(n, None) for n in range(3)], [(n, None) for n in range(WORK_BANKS)], {}
        quad_before = None
        fills = {}
        self.max_quads = [step[1:] for step in plan if step[0] == "max_turn"]
        self.head_quads = [step[1:] for step in plan if step[0] == "heads_turn"]
        self.projects = [step[1] for step in plan if step[0] == "parts"]
        for step in plan:
            kind = step[0]
            if kind in works:
                self.work[step] = len(self.work)
            if kind in works or kind == "expert_out" and (step[1] or step[3] == 0):
                self.bank[step], self.bank_before[step] = free_banks.pop(0)
            if kind in works or kind == "expert_out" and step[1]:
                free_banks.append((self.bank[step], step))
            elif kind == "expert_out" and step[3]:
                self.bank[step] = self.bank[*step[:3], 0]
                free_banks.append((self.bank[step], step))
            if kind in ("scores", "expert_in"):
                self.pair[step] = len(self.pair)
                if step[-1] == 0:
                    self.slot[step[:-1]], self.slot_before[step[:-1]] = free_slots.pop(0)
            if kind in ("values", "expert_out"):
                self.done[step] = len(self.done) + 1
                if kind == "values" and step[3] == 0:
                    self.sum_before[step] = quad_before
                    quad_before = step[1:3]
                if kind == "values":
                    free_slots.append((self.slot["scores", *step[1:]], step))
                elif step[3] == (1, TILES - 1)[step[1]]:
                    free_slots.append((self.slot["expert_in", step[1], step[2]], step))
            if kind == "scores":
                last[SLOT[step[1], step[2] // 2]] = step
            if kind == "stack":
                slot = SLOT[step[1:3]]
                self.stack_before[step] = last.get(slot)
                fills[slot] = fills.get(slot, 0) + (step[3] == PARTS - 1)
                self.landed[step] = fills[slot]
            if kind == "project" and step[2] < 2 or kind == "route" or kind == "values" and step[3] == TILES - 1:
                n_act += 1
                self.act[step] = n_act
            if kind in ("norm", "bias"):
                n_pool += 1 if kind == "norm" else TILES
                self.pool[step] = n_pool

    def before(self, a, b):
        return a in self.place and self.place[a] < self.place[b]


def build(nc, x, proj, w_expert_in, w_expert_out, w_in, w_out, routers, cols, row, expert_bias, out):
    BATCH = x.shape[0]
    first_pass, middle_pass, last_pass = (Pass(plan) for plan in plans())
    ctx = ExitStack()
    with ctx:
        def sb(name, shape, dt=F32):
            return ctx.enter_context(nc.sbuf_tensor(name, shape, dt))

        signals = []

        def signal(name, counts_in=None, step=1):
            first, each = (counts_in(first_pass), counts_in(middle_pass)) if counts_in else (PER, PER)
            signals.append(Signal(nc, ctx, name, step, first, each))
            return signals[-1]

        projs = sb("projs", [P, 3, 4, P])
        ew1 = sb("ew1", [P, EXPERTS, 4, P])
        ew2 = sb("ew2", [P, EXPERTS, 4, P])
        win = sb("win", [P, EXPERTS, P])
        wout = sb("wout", [P, EXPERTS, P])
        router = sb("router", [P, 2, EXPERTS])
        col = sb("col", [P, N_COLS])
        rows = sb("rows", [P, N_ROW])
        ebias = sb("ebias", [EXPERTS, 2, P])
        ident = sb("ident", [P, P])
        ident16 = sb("ident16", [P, P], BF16)
        mask_qk = sb("mask_qk", [P, P], BF16)
        mask_kq = sb("mask_kq", [P, P], BF16)
        minus_half = sb("minus_half", [P, TILES])
        rank = sb("rank", [P, TILES, EXPERTS])

        x_in = sb("x_in", [P, TILES, P])
        xn = sb("xn", [P, TILES, P])
        hn = sb("hn", [P, TILES, P])
        x_bias = sb("x_bias", [P, TILES, P])
        a_sum = sb("a_sum", [P, TILES, P])
        acc = sb("acc", [P, TILES, P])
        xT = sb("xT", [P, TILES * P])
        hT = sb("hT", [P, TILES * P])
        q_stack = [sb(f"q_stack{s}", [P, HEADS // 2, TILES * P], BF16) for s in range(3)]
        k_stack = [sb(f"k_stack{s}", [P, HEADS // 2, TILES * P], BF16) for s in range(3)]
        v_ones = [sb(f"v_ones{u}", [P, TILES, HEADS, 32]) for u in range(3)]
        part = [sb(f"part{u}", [P, 2, PARTS, TILES * P], BF16) for u in range(3)]
        rest = sb("rest", [P, 2, TILES * P])
        probs = sb("probs", [P, 3, QH, TILES * P])
        head_sums = sb("head_sums", [P, 2, TILES * P])
        heads = sb("heads", [P, TILES, P])
        inv_sum = sb("inv_sum", [P, TILES, QH])
        headsT = sb("headsT", [P, TILES * P])
        neg_max = sb("neg_max", [P, 2, QH, TILES])
        max_part = sb("max_part", [P, 2, PARTS, QH * TILES], BF16)
        max_rest = sb("max_rest", [P, 2, QH * TILES])
        maxT = sb("maxT", [PARTS * QH * TILES, 2, P], BF16)
        stats = sb("stats", [P, TILES, 6])
        mean_var = sb("mean_var", [P, TILES, 2])
        var_eps = sb("var_eps", [P, TILES])
        rstd = sb("rstd", [P, TILES])
        logit = sb("logit", [P, TILES, EXPERTS])
        top8 = sb("top8", [P, TILES, 8])
        gate_a = sb("gate_a", [P, TILES, EXPERTS])
        gate_b = sb("gate_b", [P, TILES, EXPERTS])
        gate_c = sb("gate_c", [P, TILES, EXPERTS])
        gate_s = sb("gate_s", [P, TILES])
        gate_t = sb("gate_t", [P, TILES])
        gate = sb("gate", [P, TILES, EXPERTS])
        gateT = sb("gateT", [EXPERTS, TILES * P])

        psum = ctx.enter_context(nc.psum_tensor("psum", [P, 8, 512], F32))
        pair_bank = [psum[:, 0:2, :], psum[:, 2:4, :]]
        sum_bank = psum[:, 4, :]
        work_bank = [psum[:, 5 + n, :] for n in range(WORK_BANKS)]

        loaded = ctx.enter_context(nc.semaphore("loaded"))
        experts_loaded = ctx.enter_context(nc.semaphore("experts_loaded"))
        made = ctx.enter_context(nc.semaphore("made"))
        cleared = ctx.enter_context(nc.semaphore("cleared"))
        arrived = {e: ctx.enter_context(nc.semaphore(f"arrived_{e}")) for e in ("pe", "act", "dve", "pool", "sp")}
        passed = {e: ctx.enter_context(nc.semaphore(f"passed_{e}")) for e in arrived}
        work_full = signal("work_full")
        pair_full = signal("pair_full")
        values_done = signal("values_done")
        vector_done = signal("vector_done")
        probs_ready = signal("probs_ready")
        scalar_done = signal("scalar_done")
        gpsimd_done = signal("gpsimd_done")

        def fills(slot):
            return lambda ps: 16 * PARTS * sum(SLOT[step[1:3]] == slot for step in ps.landed)

        x_landed = signal("x_landed", lambda ps: 16 * (("load",) in ps.place), 16)
        q_landed = [signal(f"q_landed{slot}", fills(slot), 16) for slot in range(3)]
        k_landed = [signal(f"k_landed{slot}", fills(slot), 16) for slot in range(3)]
        max_landed = [signal("max_landed0", lambda ps: 16 * ((len(ps.max_quads) + 1) // 2), 16),
                      signal("max_landed1", lambda ps: 16 * (len(ps.max_quads) // 2), 16)]
        stored = signal("stored", lambda ps: 16 * (("store",) in ps.place), 16)

        N_LOADS, N_EXPERT_LOADS = 5, 4
        N_MADE, N_CLEARED = 9, 10
        STACK_DMAS = PARTS * PARTS

        block = ctx.enter_context(nc.Block())

        @block.vector
        def _(eng):
            U32 = mybir.dt.uint32
            for slot in (2, 0):
                for stack in (q_stack[slot], k_stack[slot]):
                    eng.memset(stack[64:P, :, :].bitcast(U32), 0).then_inc(cleared, 1)
            for u in range(3):
                eng.memset(v_ones[u][:, :, :, :], 0.0).then_inc(cleared, 1)
            eng.wait_ge(cleared, 7)
            for u in range(3):
                eng.memset(v_ones[u][:, :, :, SUM_COL:SUM_COL + 1], 1.0)
            for slot in (2, 0):
                eng.memset(k_stack[slot][MAX_ROW:MAX_ROW + PARTS, :, :].bitcast(U32), 0x3F803F80).then_inc(cleared, 1)
            eng.memset(minus_half[:, :], -0.5)
            for e in range(EXPERTS):
                eng.memset(rank[:, :, e:e + 1], float(EXPERTS - e))
            eng.wait_ge(loaded, 16 * N_LOADS)
            eng.wait_ge(made, N_MADE)
            eng.tensor_copy(ident16[:, :], ident[:, :]).then_inc(cleared, 1)

            counts = Counts(eng, "dve", signals)
            at = counts.at
            owned = (vector_done,)

            def run(ps, b):

                def bank(step):
                    eng.wait_ge(work_full.sem, at(work_full, ps.work[step] + 1))
                    return work_bank[ps.bank[step]]

                for step in ps.plan:
                    kind = step[0]
                    if kind == "stats":
                        what = step[1]
                        src = {"x": x_in, "h": xn, "a": a_sum, "y": acc}[what]
                        if what == "x":
                            eng.wait_ge(x_landed.sem, at(x_landed, 16))
                        eng.wait_ge(vector_done.sem, at(vector_done, vector_done.n))
                        for t in range(TILES):
                            eng.bn_stats(stats[:, t, :], src[:, t, :]).then_inc(vector_done.sem, 1)
                            n = vector_done.count()
                        eng.wait_ge(vector_done.sem, at(vector_done, n))
                        eng.sem_inc(passed["dve"], 1)
                        for t in range(TILES):
                            eng.bn_aggr(mean_var[:, t, :], stats[:, t, :]).then_inc(vector_done.sem, 1)
                            n = vector_done.count()
                        eng.wait_ge(vector_done.sem, at(vector_done, n))
                        eng.tensor_scalar(var_eps[:, :], mean_var[:, :, 1], EPS, None, ALU.add).then_inc(vector_done.sem, 1)
                        ps.dve[step] = vector_done.count()
                    elif kind == "norm":
                        what = step[1]
                        src = {"x": x_in, "h": xn, "a": a_sum, "y": acc}[what]
                        dst = hn if what in ("h", "a") else xn
                        if what == "y" and ps.before(("bias", 1), step):
                            eng.wait_ge(gpsimd_done.sem, at(gpsimd_done, ps.pool["bias", 1]))
                        eng.wait_ge(gpsimd_done.sem, at(gpsimd_done, ps.pool[step]))
                        for t in range(TILES):
                            eng.tensor_scalar(dst[:, t, :], src[:, t, :], mean_var[:, t, 0:1], rstd[:, t:t + 1],
                                              ALU.subtract, ALU.mult).then_inc(vector_done.sem, 1)
                            n = vector_done.count()
                        ps.dve[step] = n
                        if what == "a":
                            eng.tensor_tensor(acc[:, :, :], x_bias[:, :, :], a_sum[:, :, :], ALU.add).then_inc(vector_done.sem, 1)
                            ps.dve["residual"] = vector_done.count()
                    elif kind == "turn":
                        src = bank(step)
                        if step[1] in ("x", "y"):
                            eng.tensor_copy(xT[:, :], src).then_inc(vector_done.sem, 1)
                            n = vector_done.count()
                        else:
                            g = COL_G1 if step[1] == "h" else COL_G2
                            eng.tensor_scalar(hT[:, :], src, col[:, g:g + 1], col[:, g + 1:g + 2],
                                              ALU.mult, ALU.add).then_inc(vector_done.sem, 1)
                            n = vector_done.count()
                        ps.work_freed[step] = n
                        ps.dve[step] = n
                    elif kind == "project" and step[2] < 2:
                        _, u, k = step
                        src = bank(step)
                        if u == 1:
                            c = (COL_BQ, COL_BK)[k]
                            eng.tensor_scalar(part[u][:, k, 0, :], src, col[:, c:c + 1], None, ALU.add).then_inc(vector_done.sem, 1)
                            n = vector_done.count()
                        else:
                            eng.tensor_copy(part[u][:, k, 0, :], src).then_inc(vector_done.sem, 1)
                            n = vector_done.count()
                        eng.wait_ge(vector_done.sem, at(vector_done, n))
                        p = ps.projects.index(u)
                        if p:
                            eng.wait_ge(scalar_done.sem, at(scalar_done, ps.act["project", ps.projects[p - 1], k]))
                        if u == 1:
                            eng.scalar_tensor_tensor(out=rest[:, k, :], in0=src, scalar=col[:, c:c + 1],
                                                     in1=part[u][:, k, 0, :], op0=ALU.add,
                                                     op1=ALU.subtract).then_inc(vector_done.sem, 1)
                            n = vector_done.count()
                        else:
                            eng.tensor_tensor(rest[:, k, :], src, part[u][:, k, 0, :], ALU.subtract).then_inc(vector_done.sem, 1)
                            n = vector_done.count()
                        ps.work_freed[step] = n
                        ps.dve[step] = n
                    elif kind == "project":
                        u = step[1]
                        if ps.before(("values", u, QUADS - 1, TILES - 1), step):
                            eng.wait_ge(values_done.sem, at(values_done, ps.done["values", u, QUADS - 1, TILES - 1]))
                        v = bank(step).rearrange("p (t h c) -> p t h c", t=TILES, h=HEADS)
                        if u == 1:
                            bv = rows[:, ROW_BV:ROW_BV + P].rearrange("p (h c) -> p h c", h=HEADS)
                            for t in range(TILES):
                                eng.tensor_tensor(v_ones[u][:, t, :, 0:HD], v[:, t], bv, ALU.add).then_inc(vector_done.sem, 1)
                                n = vector_done.count()
                        else:
                            for t in range(TILES):
                                eng.tensor_copy(v_ones[u][:, t, :, 0:HD], v[:, t]).then_inc(vector_done.sem, 1)
                                n = vector_done.count()
                        ps.work_freed[step] = n
                        ps.dve[step] = n
                    elif kind == "parts":
                        u = step[1]
                        for k in range(2):
                            eng.wait_ge(scalar_done.sem, at(scalar_done, ps.act["project", u, k]))
                            eng.tensor_tensor(part[u][:, k, 2, :], rest[:, k, :], part[u][:, k, 1, :],
                                              ALU.subtract).then_inc(vector_done.sem, 1)
                            ps.dve["part3", u, k] = vector_done.count()
                        eng.wait_ge(vector_done.sem, at(vector_done, vector_done.n))
                    elif kind == "max":
                        _, u, g, i, k = step
                        q = ps.max_quads.index((u, g))
                        hs, keys = max_chunks(u, i)[k]
                        src = bank(step)[:, 0:len(hs) * keys].rearrange("p (h k) -> p h k", h=len(hs))
                        eng.tensor_reduce(neg_max[:, q % 2, hs[0]:hs[0] + len(hs), i], src, AX_X,
                                          ALU.max, negate=True).then_inc(vector_done.sem, 1)
                        n = vector_done.count()
                        ps.work_freed[step] = n
                        if i == TILES - 1 and k == len(max_chunks(u, i)) - 1:
                            m = neg_max[:, q % 2, :, :].rearrange("p h i -> p (h i)")
                            parts, left = max_part[:, q % 2], max_rest[:, q % 2, :]
                            eng.wait_ge(vector_done.sem, at(vector_done, n))
                            if q >= 2:
                                eng.wait_ge(work_full.sem, at(work_full, ps.work["max_turn", *ps.max_quads[q - 2]] + 1))
                            eng.tensor_copy(parts[:, 0, :], m).then_inc(vector_done.sem, 1)
                            eng.wait_ge(vector_done.sem, at(vector_done, vector_done.count()))
                            eng.tensor_tensor(left, m, parts[:, 0, :], ALU.subtract).then_inc(vector_done.sem, 1)
                            eng.wait_ge(vector_done.sem, at(vector_done, vector_done.count()))
                            eng.tensor_copy(parts[:, 1, :], left).then_inc(vector_done.sem, 1)
                            eng.wait_ge(vector_done.sem, at(vector_done, vector_done.count()))
                            eng.tensor_tensor(parts[:, 2, :], left, parts[:, 1, :], ALU.subtract).then_inc(vector_done.sem, 1)
                            ps.dve["max_part", u, g] = vector_done.count()
                    elif kind == "max_turn":
                        q = ps.max_quads.index(step[1:])
                        rows48 = PARTS * QH * TILES
                        src = bank(step)[0:rows48, 0:P // 2].bitcast(BF16)
                        if q >= 2:
                            eng.wait_ge(max_landed[q % 2].sem, at(max_landed[q % 2], 16 * (q // 2)))
                        eng.tensor_copy(maxT[:, q % 2, :], src).then_inc(vector_done.sem, 1)
                        n = vector_done.count()
                        ps.work_freed[step] = n
                        ps.dve[step] = n
                    elif kind == "heads_turn":
                        _, u, g = step
                        src = bank(step).rearrange("p (t h c) -> p t h c", t=TILES, h=QH)
                        eng.wait_ge(vector_done.sem, at(vector_done, vector_done.n))
                        eng.reciprocal(inv_sum[:, :, :], src[:, :, :, SUM_COL]).then_inc(vector_done.sem, 1)
                        eng.wait_ge(vector_done.sem, at(vector_done, vector_done.count()))
                        dst = heads[:, :, g * QH * HD:(g + 1) * QH * HD].rearrange("p t (h c) -> p t h c", h=QH)
                        inv = inv_sum[:, :, :].unsqueeze(3).to_broadcast([P, TILES, QH, HD])
                        eng.tensor_tensor(dst, src[:, :, :, 0:HD], inv, ALU.mult).then_inc(vector_done.sem, 1)
                        n = vector_done.count()
                        ps.work_freed[step] = n
                        ps.dve[step] = n
                    elif kind == "heads_back":
                        eng.tensor_copy(headsT[:, :], bank(step)).then_inc(vector_done.sem, 1)
                        n = vector_done.count()
                        ps.work_freed[step] = n
                        ps.dve[step] = n
                    elif kind == "out_project":
                        u = step[1]
                        dst = (x_bias, a_sum, acc)[u]
                        if ps.before(("bias", u), step):
                            eng.wait_ge(gpsimd_done.sem, at(gpsimd_done, ps.pool["bias", u]))
                        elif u == 2:
                            eng.wait_ge(vector_done.sem, at(vector_done, ps.dve["expert_out", 1, 1, 3]))
                        eng.tensor_tensor(dst[:, :, :].rearrange("p t c -> p (t c)"), bank(step),
                                                     dst[:, :, :].rearrange("p t c -> p (t c)"), ALU.add).then_inc(vector_done.sem, 1)
                        n = vector_done.count()
                        ps.work_freed[step] = n
                        ps.dve[step] = n
                    elif kind == "route":
                        layer = step[1]
                        src = bank(step)[:, 0:TILES * EXPERTS].rearrange("p (t e) -> p t e", t=TILES)

                        def wide(t):
                            return t[:, :].unsqueeze(2).to_broadcast([P, TILES, EXPERTS])

                        if layer == 0:
                            br = rows[:, ROW_BR:ROW_BR + EXPERTS]
                            for t in range(TILES):
                                eng.tensor_tensor(logit[:, t, :], src[:, t, :], br, ALU.add).then_inc(vector_done.sem, 1)
                                n = vector_done.count()
                        else:
                            eng.tensor_copy(logit[:, :, :], src).then_inc(vector_done.sem, 1)
                            n = vector_done.count()
                        ps.work_freed[step] = n
                        eng.wait_ge(vector_done.sem, at(vector_done, n))
                        eng.tensor_reduce(gate_s[:, :], logit[:, :, :], AX_X, ALU.max).then_inc(vector_done.sem, 1)
                        eng.wait_ge(vector_done.sem, at(vector_done, vector_done.count()))
                        eng.tensor_tensor(gate_a[:, :, :], logit[:, :, :], wide(gate_s), ALU.subtract).then_inc(vector_done.sem, 1)
                        n = vector_done.count()
                        ps.dve["logit", layer] = n
                        if layer == 0:
                            for t in range(TILES):
                                eng.max(top8[:, t, :], logit[:, t, :]).then_inc(vector_done.sem, 1)
                                n = vector_done.count()
                            eng.wait_ge(vector_done.sem, at(vector_done, n))
                            eng.tensor_tensor(gate_c[:, :, :], logit[:, :, :],
                                                         top8[:, :, 1:2].to_broadcast([P, TILES, EXPERTS]),
                                                         ALU.is_ge).then_inc(vector_done.sem, 1)
                            eng.wait_ge(vector_done.sem, at(vector_done, vector_done.count()))
                            eng.wait_ge(scalar_done.sem, at(scalar_done, ps.act["route", 0]))
                            eng.tensor_tensor(gate_b[:, :, :], gate_b[:, :, :], gate_c[:, :, :], ALU.mult).then_inc(vector_done.sem, 1)
                            eng.wait_ge(vector_done.sem, at(vector_done, vector_done.count()))
                            eng.tensor_reduce(gate_s[:, :], gate_b[:, :, :], AX_X, ALU.add).then_inc(vector_done.sem, 1)
                            eng.wait_ge(vector_done.sem, at(vector_done, vector_done.count()))
                            eng.reciprocal(gate_t[:, :], gate_s[:, :]).then_inc(vector_done.sem, 1)
                            eng.wait_ge(vector_done.sem, at(vector_done, vector_done.count()))
                            eng.tensor_tensor(gate[:, :, :], gate_b[:, :, :], wide(gate_t), ALU.mult).then_inc(vector_done.sem, 1)
                            n = vector_done.count()
                        else:
                            eng.wait_ge(scalar_done.sem, at(scalar_done, ps.act["route", 1]))
                            eng.tensor_reduce(gate_s[:, :], gate_b[:, :, :], AX_X, ALU.add).then_inc(vector_done.sem, 1)
                            eng.wait_ge(vector_done.sem, at(vector_done, vector_done.count()))
                            eng.reciprocal(gate_t[:, :], gate_s[:, :]).then_inc(vector_done.sem, 1)
                            eng.wait_ge(vector_done.sem, at(vector_done, vector_done.count()))
                            eng.tensor_tensor(logit[:, :, :], gate_b[:, :, :], wide(gate_t), ALU.mult).then_inc(vector_done.sem, 1)
                            n = vector_done.count()
                            eng.wait_ge(vector_done.sem, at(vector_done, n))
                            left = logit
                            for turn, picked in enumerate((gate_a, gate_b)):
                                eng.tensor_reduce(gate_s[:, :], left[:, :, :], AX_X, ALU.max).then_inc(vector_done.sem, 1)
                                eng.wait_ge(vector_done.sem, at(vector_done, vector_done.count()))
                                eng.tensor_tensor(gate_c[:, :, :], left[:, :, :], wide(gate_s), ALU.is_ge).then_inc(vector_done.sem, 1)
                                eng.wait_ge(vector_done.sem, at(vector_done, vector_done.count()))
                                eng.tensor_tensor(gate_c[:, :, :], gate_c[:, :, :], rank[:, :, :], ALU.mult).then_inc(vector_done.sem, 1)
                                eng.wait_ge(vector_done.sem, at(vector_done, vector_done.count()))
                                eng.tensor_reduce(gate_t[:, :], gate_c[:, :, :], AX_X, ALU.max).then_inc(vector_done.sem, 1)
                                eng.wait_ge(vector_done.sem, at(vector_done, vector_done.count()))
                                eng.tensor_tensor(picked[:, :, :], gate_c[:, :, :], wide(gate_t),
                                                             ALU.is_equal).then_inc(vector_done.sem, 1)
                                eng.wait_ge(vector_done.sem, at(vector_done, vector_done.count()))
                                if turn == 0:
                                    eng.scalar_tensor_tensor(out=top8[:, :, :], in0=picked[:, :, :],
                                                                        scalar=-2.0, in1=logit[:, :, :],
                                                                        op0=ALU.mult, op1=ALU.add).then_inc(vector_done.sem, 1)
                                    eng.wait_ge(vector_done.sem, at(vector_done, vector_done.count()))
                                    left = top8
                            eng.tensor_tensor(gate_a[:, :, :], gate_a[:, :, :], gate_b[:, :, :], ALU.add).then_inc(vector_done.sem, 1)
                            eng.wait_ge(vector_done.sem, at(vector_done, vector_done.count()))
                            eng.tensor_tensor(gate[:, :, :], gate_a[:, :, :], logit[:, :, :], ALU.mult).then_inc(vector_done.sem, 1)
                            n = vector_done.count()
                        ps.dve[step] = n
                    elif kind == "route_turn":
                        eng.tensor_copy(gateT[:, :], bank(step)[0:EXPERTS, :]).then_inc(vector_done.sem, 1)
                        n = vector_done.count()
                        ps.work_freed[step] = n
                        ps.dve[step] = n
                    elif kind == "route_bias":
                        eng.wait_ge(vector_done.sem, at(vector_done, ps.dve["residual"] if step[1] == 0 else ps.dve["norm", "y"]))
                        flat = acc[:, :, :].rearrange("p t c -> p (t c)")
                        eng.tensor_tensor(flat, bank(step), flat, ALU.add).then_inc(vector_done.sem, 1)
                        n = vector_done.count()
                        ps.work_freed[step] = n
                        ps.dve[step] = n
                    elif kind == "expert_out":
                        _, layer, e, k = step
                        if layer == 0 and k == 0:
                            continue
                        expert = e if layer == 0 else 4 * e + k
                        eng.wait_ge(values_done.sem, at(values_done, ps.done[step]))
                        src = work_bank[ps.bank[step]]
                        eng.wait_ge(vector_done.sem, at(vector_done, vector_done.n))
                        for t in range(TILES):
                            eng.scalar_tensor_tensor(
                                out=acc[:, t, :], in0=src[:, t * P:(t + 1) * P],
                                scalar=gate[:, t, expert:expert + 1], in1=acc[:, t, :],
                                op0=ALU.mult, op1=ALU.add).then_inc(vector_done.sem, 1)
                            n = vector_done.count()
                        ps.work_freed[step] = n
                        ps.dve[step] = n
                eng.wait_ge(vector_done.sem, at(vector_done, vector_done.n))
                eng.sem_inc(vector_done.sem, PER - vector_done.n)
                eng.sem_inc(arrived["dve"], 1)
                eng.wait_ge(arrived["pe"], counts.number)
                eng.sem_inc(passed["dve"], 1)
                eng.wait_ge(arrived["act"], counts.number)
                eng.sem_inc(passed["dve"], 1)
                eng.wait_ge(arrived["pool"], counts.number)
                eng.sem_inc(passed["dve"], 1)
                eng.wait_ge(arrived["sp"], counts.number)
                eng.sem_inc(passed["dve"], 1)

            counts.begin(0, owned)
            run(first_pass, 0)
            with eng.Fori(0, BATCH - 1) as b:
                counts.begin_looped(b, owned)
                run(middle_pass, b)
            counts.begin(BATCH, owned)
            run(last_pass, BATCH - 1)

        @block.scalar
        def _(eng):
            eng.wait_ge(loaded, 16 * N_LOADS)
            counts = Counts(eng, "act", signals)
            at = counts.at
            owned = (scalar_done, probs_ready)

            def run(ps, b):

                for step in ps.plan:
                    kind = step[0]
                    if kind == "project" and step[2] < 2:
                        _, u, k = step
                        eng.wait_ge(vector_done.sem, at(vector_done, ps.dve[step]))
                        eng.activation(part[u][:, k, 1, :], rest[:, k, :], ACT.Copy).then_inc(scalar_done.sem, 1)
                        assert scalar_done.count() == ps.act[step]
                    elif kind == "scores":
                        _, u, g, j, k = step
                        hs, width, per_bank = score_pairs(u, j)[k]
                        n = ps.pair[step]
                        reader = ps.slot_before[step[:-1]]
                        if k == 0 and reader:
                            eng.wait_ge(values_done.sem, at(values_done, ps.done[reader]))
                        eng.wait_ge(pair_full.sem, at(pair_full, n + 1))
                        dst = probs[:, ps.slot[step[:-1]], hs[0]:hs[0] + len(hs), TILES * P - width:TILES * P]
                        if per_bank == 1:
                            src = pair_bank[n % 2][:, :, 0:width]
                        else:
                            src = pair_bank[n % 2].rearrange("p a q -> p (a q)")[:, 0:len(hs) * width]
                            src = src.rearrange("p (h q) -> p h q", h=len(hs))
                        eng.activation(dst, src, ACT.Exp, scale=SCALE).then_inc(probs_ready.sem, 1)
                        assert probs_ready.count() == n + 1
                    elif kind == "values" and step[3] == TILES - 1:
                        _, u, g, j = step
                        eng.wait_ge(values_done.sem, at(values_done, ps.done[step]))
                        q = ps.head_quads.index((u, g))
                        if q >= 2:
                            eng.wait_ge(work_full.sem, at(work_full, ps.work["heads_turn", *ps.head_quads[q - 2]] + 1))
                        eng.activation(head_sums[:, q % 2, :], sum_bank,
                                       ACT.Copy).then_inc(scalar_done.sem, 1)
                        assert scalar_done.count() == ps.act[step]
                    elif kind == "route":
                        eng.wait_ge(vector_done.sem, at(vector_done, ps.dve["logit", step[1]]))
                        eng.activation(gate_b[:, :, :], gate_a[:, :, :], ACT.Exp).then_inc(scalar_done.sem, 1)
                        assert scalar_done.count() == ps.act[step]
                    elif kind == "expert_in":
                        _, layer, e, k = step
                        n = ps.pair[step]
                        reader = ps.slot_before[step[:-1]]
                        if k == 0 and reader:
                            eng.wait_ge(values_done.sem, at(values_done, ps.done[reader]))
                        eng.wait_ge(pair_full.sem, at(pair_full, n + 1))
                        for f in range(2):
                            c = (COL_BIN if layer else COL_EB1) + 4 * e + 2 * k + f
                            ins = eng.activation(probs[:, ps.slot[step[:-1]], 2 * k + f, :], pair_bank[n % 2][:, f, :],
                                                 ACT.Gelu_apprx_tanh if layer else ACT.Gelu, bias=col[:, c:c + 1])
                        ins.then_inc(probs_ready.sem, 1)
                        assert probs_ready.count() == n + 1
                eng.wait_ge(scalar_done.sem, at(scalar_done, scalar_done.n))
                eng.sem_inc(scalar_done.sem, PER - scalar_done.n)
                eng.wait_ge(probs_ready.sem, at(probs_ready, probs_ready.n))
                eng.sem_inc(probs_ready.sem, PER - probs_ready.n)
                eng.sem_inc(arrived["act"], 1)
                eng.wait_ge(arrived["pe"], counts.number)
                eng.sem_inc(passed["act"], 1)
                eng.wait_ge(arrived["dve"], counts.number)
                eng.sem_inc(passed["act"], 1)
                eng.wait_ge(arrived["pool"], counts.number)
                eng.sem_inc(passed["act"], 1)
                eng.wait_ge(arrived["sp"], counts.number)
                eng.sem_inc(passed["act"], 1)

            counts.begin(0, owned)
            run(first_pass, 0)
            with eng.Fori(0, BATCH - 1) as b:
                counts.begin_looped(b, owned)
                run(middle_pass, b)
            counts.begin(BATCH, owned)
            run(last_pass, BATCH - 1)

        @block.tensor
        def _(eng):
            eng.wait_ge(loaded, 16 * N_LOADS)
            eng.wait_ge(made, N_MADE)
            eng.wait_ge(cleared, N_CLEARED)
            counts = Counts(eng, "pe", signals)
            at = counts.at
            owned = (work_full, pair_full, values_done)

            def run(ps, b):

                def bank(step):
                    if ps.bank_before[step]:
                        eng.wait_ge(vector_done.sem, at(vector_done, ps.work_freed[ps.bank_before[step]]))
                    return work_bank[ps.bank[step]]

                def pair(step):
                    n = ps.pair[step]
                    if n >= 2:
                        eng.wait_ge(probs_ready.sem, at(probs_ready, n - 1))
                    return pair_bank[n % 2]

                for step in ps.plan:
                    kind = step[0]
                    if kind == "turn":
                        src = hn if step[1] in ("h", "a") else xn
                        eng.wait_ge(vector_done.sem, at(vector_done, ps.dve["norm", step[1]]))
                        dst = bank(step)
                        for t in range(TILES):
                            ins = eng.transpose(dst[:, t * P:(t + 1) * P], src[:, t, :], ident[:, :])
                        ins.then_inc(work_full.sem, 1)
                        work_full.count()
                    elif kind == "project":
                        _, u, k = step
                        src = hT if u == 1 else xT
                        eng.wait_ge(vector_done.sem, at(vector_done, ps.dve["turn", ("x", "h", "y")[u]]))
                        dst = bank(step)
                        if k < 2:
                            ins = eng.matmul(dst, projs[:, u, k, :], src[:, :], start=True, stop=True)
                        else:
                            for t in range(TILES):
                                ins = eng.matmul(dst[:, t * P:(t + 1) * P], src[:, t * P:(t + 1) * P],
                                                 projs[:, u, 2, :], start=True, stop=True)
                        ins.then_inc(work_full.sem, 1)
                        work_full.count()
                    elif kind == "max":
                        _, u, g, i, k = step
                        slot = SLOT[u, g // 2]
                        if (g % 2, i, k) == (0, 0, 0) and ps.before(("stack", u, g // 2, PARTS - 1), step):
                            n = 16 * STACK_DMAS * ps.landed["stack", u, g // 2, PARTS - 1]
                            eng.wait_ge(q_landed[slot].sem, at(q_landed[slot], n))
                            eng.wait_ge(k_landed[slot].sem, at(k_landed[slot], n))
                        hs, keys = max_chunks(u, i)[k]
                        dst = bank(step)
                        for c, h in enumerate(hs):
                            head, col0 = 4 * (g % 2) + h, c * keys
                            ins = eng.matmul(dst[:, col0:col0 + keys],
                                             q_stack[slot][0:MAX_ROW, head, i * P:(i + 1) * P],
                                             k_stack[slot][0:MAX_ROW, head, 0:keys], start=True, stop=not CAUSAL[u])
                            if CAUSAL[u]:
                                ins = eng.matmul(dst[:, col0 + keys - P:col0 + keys], ident16[:, :], mask_qk[:, :],
                                                 start=False, stop=True)
                        ins.then_inc(work_full.sem, 1)
                        work_full.count()
                    elif kind == "max_turn":
                        q = ps.max_quads.index(step[1:])
                        dst = bank(step)[0:PARTS * QH * TILES, 0:P // 2].bitcast(BF16)
                        eng.wait_ge(vector_done.sem, at(vector_done, ps.dve["max_part", step[1], step[2]]))
                        eng.sem_inc(passed["pe"], 1)
                        eng.transpose(dst, max_part[:, q % 2].rearrange("p a b -> p (a b)"),
                                      ident16[:, :]).then_inc(work_full.sem, 1)
                        work_full.count()
                    elif kind == "scores":
                        _, u, g, j, k = step
                        slot = SLOT[u, g // 2]
                        if j == 0 and k == 0 and ps.before(("max_turn", u, g), step):
                            q = ps.max_quads.index((u, g))
                            eng.wait_ge(max_landed[q % 2].sem, at(max_landed[q % 2], 16 * (q // 2 + 1)))
                        hs, width, per_bank = score_pairs(u, j)[k]
                        dst = pair(step)
                        for c, h in enumerate(hs):
                            head, col0 = 4 * (g % 2) + h, (c % per_bank) * width
                            o = dst[:, c // per_bank, col0:col0 + width]
                            ins = eng.matmul(o, k_stack[slot][:, head, j * P:(j + 1) * P],
                                             q_stack[slot][:, head, TILES * P - width:TILES * P],
                                             start=True, stop=not CAUSAL[u])
                            if CAUSAL[u]:
                                ins = eng.matmul(o[:, 0:P], ident16[:, :], mask_kq[:, :], start=False, stop=True)
                        ins.then_inc(pair_full.sem, 1)
                        assert pair_full.count() == ps.pair[step] + 1
                    elif kind == "values":
                        _, u, g, j = step
                        if j == 0 and ps.sum_before[step]:
                            eng.wait_ge(scalar_done.sem,
                                        at(scalar_done, ps.act["values", *ps.sum_before[step], TILES - 1]))
                        if j == 0 and ps.before(("project", u, 2), step):
                            eng.wait_ge(vector_done.sem, at(vector_done, ps.dve["project", u, 2]))
                        last_pair = ("scores", u, g, j, len(score_pairs(u, j)) - 1)
                        eng.wait_ge(probs_ready.sem, at(probs_ready, ps.pair[last_pair] + 1))
                        q0 = P * j if CAUSAL[u] else 0
                        for c in range(QH):
                            ins = eng.matmul(sum_bank[32 * c:32 * c + 32, q0:TILES * P],
                                             v_ones[u][:, j, 4 * g + c, :],
                                             probs[:, ps.slot["scores", u, g, j], c, q0:TILES * P],
                                             start=(j == 0), stop=(j == TILES - 1))
                        ins.then_inc(values_done.sem, 1)
                        assert values_done.count() == ps.done[step]
                    elif kind == "heads_turn":
                        _, u, g = step
                        eng.wait_ge(scalar_done.sem, at(scalar_done, ps.act["values", u, g, TILES - 1]))
                        q = ps.head_quads.index((u, g))
                        dst = bank(step)
                        for t in range(TILES):
                            ins = eng.transpose(dst[:, t * P:(t + 1) * P], head_sums[:, q % 2, t * P:(t + 1) * P],
                                                ident[:, :])
                        ins.then_inc(work_full.sem, 1)
                        work_full.count()
                    elif kind == "heads_back":
                        eng.wait_ge(vector_done.sem, at(vector_done, ps.dve["heads_turn", step[1], QUADS - 1]))
                        dst = bank(step)
                        for t in range(TILES):
                            ins = eng.transpose(dst[:, t * P:(t + 1) * P], heads[:, t, :], ident[:, :])
                        ins.then_inc(work_full.sem, 1)
                        work_full.count()
                    elif kind == "out_project":
                        eng.wait_ge(vector_done.sem, at(vector_done, ps.dve["heads_back", step[1]]))
                        dst = bank(step)
                        for t in range(TILES):
                            ins = eng.matmul(dst[:, t * P:(t + 1) * P], headsT[:, t * P:(t + 1) * P],
                                             projs[:, step[1], 3, :], start=True, stop=True)
                        ins.then_inc(work_full.sem, 1)
                        work_full.count()
                    elif kind == "route":
                        src = hT if step[1] == 0 else xT
                        eng.wait_ge(vector_done.sem, at(vector_done, ps.dve["turn", "a" if step[1] == 0 else "y"]))
                        dst = bank(step)
                        for t in range(TILES):
                            ins = eng.matmul(dst[:, t * EXPERTS:(t + 1) * EXPERTS], src[:, t * P:(t + 1) * P],
                                             router[:, step[1], :], start=True, stop=True)
                        ins.then_inc(work_full.sem, 1)
                        work_full.count()
                    elif kind == "route_turn":
                        eng.wait_ge(vector_done.sem, at(vector_done, ps.dve["route", step[1]]))
                        dst = bank(step)
                        for t in range(TILES):
                            ins = eng.transpose(dst[0:EXPERTS, t * P:(t + 1) * P], gate[:, t, :], ident[:, :])
                        ins.then_inc(work_full.sem, 1)
                        work_full.count()
                    elif kind == "route_bias":
                        eng.wait_ge(vector_done.sem, at(vector_done, ps.dve["route_turn", step[1]]))
                        dst = bank(step)
                        for t in range(TILES):
                            ins = eng.matmul(dst[:, t * P:(t + 1) * P], gateT[:, t * P:(t + 1) * P],
                                             ebias[:, step[1], :], start=True, stop=True)
                        ins.then_inc(work_full.sem, 1)
                        work_full.count()
                    elif kind == "expert_in":
                        _, layer, e, k = step
                        if e == 0 and k == 0:
                            eng.wait_ge(experts_loaded, 16 * N_EXPERT_LOADS)
                        dst = pair(step)
                        for f in range(2):
                            w = win[:, 4 * e + 2 * k + f, :] if layer else ew1[:, e, 2 * k + f, :]
                            ins = eng.matmul(dst[:, f, :], w, (xT if layer else hT)[:, :], start=True, stop=True)
                        ins.then_inc(pair_full.sem, 1)
                        assert pair_full.count() == ps.pair[step] + 1
                    elif kind == "expert_out":
                        _, layer, e, k = step
                        if k == 0:
                            eng.wait_ge(probs_ready.sem, at(probs_ready, ps.pair["expert_in", layer, e, 1] + 1))
                        if layer or k == 0:
                            dst = bank(step)
                        middle = probs[:, ps.slot["expert_in", layer, e]]
                        for t in range(TILES) if layer else range(2 * k, 2 * k + 2):
                            chunks = (k,) if layer else range(4)
                            for f in chunks:
                                w = wout[:, 4 * e + k, :] if layer else ew2[:, e, f, :]
                                ins = eng.matmul(dst[:, t * P:(t + 1) * P], middle[:, f, t * P:(t + 1) * P], w,
                                                 start=f == chunks[0], stop=f == chunks[-1])
                        ins.then_inc(values_done.sem, 1)
                        assert values_done.count() == ps.done[step]
                eng.wait_ge(work_full.sem, at(work_full, work_full.n))
                eng.sem_inc(work_full.sem, PER - work_full.n)
                eng.wait_ge(pair_full.sem, at(pair_full, pair_full.n))
                eng.sem_inc(pair_full.sem, PER - pair_full.n)
                eng.wait_ge(values_done.sem, at(values_done, values_done.n))
                eng.sem_inc(values_done.sem, PER - values_done.n)
                eng.sem_inc(arrived["pe"], 1)
                eng.wait_ge(arrived["act"], counts.number)
                eng.sem_inc(passed["pe"], 1)
                eng.wait_ge(arrived["dve"], counts.number)
                eng.sem_inc(passed["pe"], 1)
                eng.wait_ge(arrived["pool"], counts.number)
                eng.sem_inc(passed["pe"], 1)
                eng.wait_ge(arrived["sp"], counts.number)
                eng.sem_inc(passed["pe"], 1)

            counts.begin(0, owned)
            run(first_pass, 0)
            with eng.Fori(0, BATCH - 1) as b:
                counts.begin_looped(b, owned)
                run(middle_pass, b)
            counts.begin(BATCH, owned)
            run(last_pass, BATCH - 1)

        @block.gpsimd
        def _(eng):
            eng.memset(ident[:, :], 0.0).then_inc(made, 1)
            eng.memset(mask_qk[:, :], 0.0).then_inc(made, 1)
            eng.memset(mask_kq[:, :], 0.0).then_inc(made, 1)
            for n, stack in enumerate((q_stack[1], k_stack[1])):
                eng.wait_ge(made, 3 + n)
                eng.memset(stack[64:P, :, :].bitcast(mybir.dt.uint32), 0).then_inc(made, 1)
            eng.wait_ge(made, 5)
            eng.memset(k_stack[1][MAX_ROW:MAX_ROW + PARTS, :, :].bitcast(mybir.dt.uint32), 0x3F803F80)\
               .then_inc(made, 1)
            eng.wait_ge(made, 6)
            eng.affine_select(out=ident[:, :], in_=ident[:, :], compare_op=ALU.not_equal, fill=1.0, base=0,
                              pattern=[[-1, P]], channel_multiplier=1).then_inc(made, 1)
            eng.affine_select(out=mask_qk[:, :], in_=mask_qk[:, :], compare_op=ALU.is_ge, fill=MASKED, base=0,
                              pattern=[[-1, P]], channel_multiplier=1).then_inc(made, 1)
            eng.affine_select(out=mask_kq[:, :], in_=mask_kq[:, :], compare_op=ALU.is_ge, fill=MASKED, base=0,
                              pattern=[[1, P]], channel_multiplier=-1).then_inc(made, 1)
            eng.wait_ge(loaded, 16 * N_LOADS)
            eng.wait_ge(cleared, N_CLEARED)
            counts = Counts(eng, "pool", signals)
            at = counts.at
            owned = (gpsimd_done, *k_landed)

            def run(ps, b):

                for step in ps.plan:
                    kind = step[0]
                    if kind == "norm":
                        eng.wait_ge(vector_done.sem, at(vector_done, ps.dve["stats", step[1]]))
                        eng.tensor_tensor(rstd[:, :], var_eps[:, :], minus_half[:, :], ALU.pow).then_inc(gpsimd_done.sem, 1)
                        assert gpsimd_done.count() == ps.pool[step]
                    elif kind == "bias":
                        dst, src, row0 = ((x_bias, x_in, ROW_BOUT), (a_sum, xn, ROW_BO))[step[1]]
                        if ps.before(("norm", "a"), step):
                            eng.wait_ge(vector_done.sem, at(vector_done, ps.dve["residual"]))
                        else:
                            eng.wait_ge(vector_done.sem, at(vector_done, ps.dve["norm", "x"]))
                        for t in range(TILES):
                            eng.tensor_tensor(dst[:, t, :], src[:, t, :], rows[:, row0:row0 + P],
                                              ALU.add).then_inc(gpsimd_done.sem, 1)
                            n = gpsimd_done.count()
                        assert n == ps.pool[step]
                    elif kind == "stack":
                        _, u, half, j = step
                        slot, reader = SLOT[u, half], ps.stack_before[step]
                        if reader:
                            eng.wait_ge(pair_full.sem, at(pair_full, ps.pair[reader] + 1))
                            eng.sem_inc(passed["pool"], 1)
                        if j == 0:
                            eng.wait_ge(vector_done.sem, at(vector_done, ps.dve["project", u, 1]))
                            eng.sem_inc(passed["pool"], 1)
                        elif j == 1:
                            eng.wait_ge(scalar_done.sem, at(scalar_done, ps.act["project", u, 1]))
                            eng.sem_inc(passed["pool"], 1)
                        else:
                            eng.wait_ge(vector_done.sem, at(vector_done, ps.dve["part3", u, 1]))
                            eng.sem_inc(passed["pool"], 1)
                        for i in range(PARTS):
                            r = 24 * i + 8 * j
                            eng.dma_start(k_stack[slot][r:r + 8, :, :],
                                          part[u][64 * half:64 * half + 64, 1, j, :]).then_inc(k_landed[slot].sem, 16)
                            k_landed[slot].count()
                for slot in range(3):
                    if k_landed[slot].n:
                        eng.wait_ge(k_landed[slot].sem, at(k_landed[slot], k_landed[slot].n))
                        eng.sem_inc(passed["pool"], 1)
                eng.wait_ge(gpsimd_done.sem, at(gpsimd_done, gpsimd_done.n))
                eng.sem_inc(gpsimd_done.sem, PER - gpsimd_done.n)
                eng.sem_inc(arrived["pool"], 1)
                eng.wait_ge(arrived["pe"], counts.number)
                eng.sem_inc(passed["pool"], 1)
                eng.wait_ge(arrived["act"], counts.number)
                eng.sem_inc(passed["pool"], 1)
                eng.wait_ge(arrived["dve"], counts.number)
                eng.sem_inc(passed["pool"], 1)
                eng.wait_ge(arrived["sp"], counts.number)
                eng.sem_inc(passed["pool"], 1)

            counts.begin(0, owned)
            run(first_pass, 0)
            with eng.Fori(0, BATCH - 1) as b:
                counts.begin_looped(b, owned)
                run(middle_pass, b)
            counts.begin(BATCH, owned)
            run(last_pass, BATCH - 1)

        @block.sync
        def _(eng):
            for dst, src in ((projs[:, :, :, :], proj), (col[:, :], cols), (router[:, :, :], routers),
                             (rows[:, :], row.to_broadcast([P, N_ROW])), (ebias[:, :, :], expert_bias)):
                eng.dma_start(dst, src).then_inc(loaded, 16)
            for dst, src in ((ew1[:, :, :, :], w_expert_in), (ew2[:, :, :, :], w_expert_out),
                             (win[:, :, :], w_in), (wout[:, :, :], w_out)):
                eng.dma_start(dst, src).then_inc(experts_loaded, 16)
            eng.wait_ge(cleared, N_CLEARED)
            counts = Counts(eng, "sp", signals)
            at = counts.at
            owned = (x_landed, *q_landed, *max_landed, stored)

            def run(ps, b):

                for step in ps.plan:
                    kind = step[0]
                    if kind == "load":
                        following = bass.ds(b + 1, 1) if ps is middle_pass else slice(0, 1)
                        eng.dma_start(x_in[:, :, :], x[following, :, :].rearrange("b (t p) c -> p (b t) c", p=P))\
                           .then_inc(x_landed.sem, 16)
                        x_landed.count()
                    elif kind == "stack":
                        _, u, half, i = step
                        slot, reader = SLOT[u, half], ps.stack_before[step]
                        if reader:
                            eng.wait_ge(pair_full.sem, at(pair_full, ps.pair[reader] + 1))
                            eng.sem_inc(passed["sp"], 1)
                        if i == 0:
                            eng.wait_ge(vector_done.sem, at(vector_done, ps.dve["project", u, 0]))
                            eng.sem_inc(passed["sp"], 1)
                        elif i == 1:
                            eng.wait_ge(scalar_done.sem, at(scalar_done, ps.act["project", u, 0]))
                            eng.sem_inc(passed["sp"], 1)
                        else:
                            eng.wait_ge(vector_done.sem, at(vector_done, ps.dve["part3", u, 0]))
                            eng.sem_inc(passed["sp"], 1)
                        for j in range(PARTS):
                            r = 24 * i + 8 * j
                            eng.dma_start(q_stack[slot][r:r + 8, :, :],
                                          part[u][64 * half:64 * half + 64, 0, i, :]).then_inc(q_landed[slot].sem, 16)
                            q_landed[slot].count()
                    elif kind == "max_turn":
                        _, u, g = step
                        q = ps.max_quads.index((u, g))
                        slot, head0 = SLOT[u, g // 2], 4 * (g % 2)
                        eng.wait_ge(vector_done.sem, at(vector_done, ps.dve[step]))
                        eng.sem_inc(passed["sp"], 1)
                        eng.dma_start(q_stack[slot][MAX_ROW:MAX_ROW + PARTS, head0:head0 + 4, :],
                                      maxT[:, q % 2, :]).then_inc(max_landed[q % 2].sem, 16)
                        max_landed[q % 2].count()
                    elif kind == "store":
                        eng.wait_ge(vector_done.sem, at(vector_done, ps.dve["out_project", 2]))
                        eng.sem_inc(passed["sp"], 1)
                        this = bass.ds(b, 1) if ps is middle_pass else slice(BATCH - 1, BATCH)
                        eng.dma_start(out[this, :, :].rearrange("b (t p) c -> p (b t) c", p=P),
                                      acc[:, :, :]).then_inc(stored.sem, 16)
                        stored.count()
                for sig in (*q_landed, *max_landed, stored):
                    if sig.n:
                        eng.wait_ge(sig.sem, at(sig, sig.n))
                        eng.sem_inc(passed["sp"], 1)
                eng.sem_inc(arrived["sp"], 1)
                eng.wait_ge(arrived["pe"], counts.number)
                eng.sem_inc(passed["sp"], 1)
                eng.wait_ge(arrived["act"], counts.number)
                eng.sem_inc(passed["sp"], 1)
                eng.wait_ge(arrived["dve"], counts.number)
                eng.sem_inc(passed["sp"], 1)
                eng.wait_ge(arrived["pool"], counts.number)
                eng.sem_inc(passed["sp"], 1)

            counts.begin(0, owned)
            run(first_pass, 0)
            with eng.Fori(0, BATCH - 1) as b:
                counts.begin_looped(b, owned)
                run(middle_pass, b)
            counts.begin(BATCH, owned)
            run(last_pass, BATCH - 1)


def kernel(**inputs):
    import numpy as np
    import concourse.bacc as bacc
    from concourse.bass_utils import run_bass_kernel_spmd

    a = {name: np.asarray(value) for name, value in inputs.items()}
    D = a["L0_attn_x"].shape[2]

    def by_channel(w):
        return w.reshape(*w.shape[:-1], 2, HEADS // 2, HD).swapaxes(-1, -2).reshape(w.shape)

    def of_heads(w):
        return w.transpose(1, 0, 2).reshape(D, D)

    wqkv = a["L0_attn_w_qkv"]
    proj = np.stack([
        np.stack([by_channel(wqkv[:, 0:D]), by_channel(wqkv[:, D:2 * D]), wqkv[:, 2 * D:], a["L0_attn_w_out"]], 1),
        np.stack([by_channel(a["L0_ffn_Wq"]), by_channel(a["L0_ffn_Wk"]), a["L0_ffn_Wv"], a["L0_ffn_Wo"]], 1),
        np.stack([by_channel(of_heads(a["L1_attn_W_query"])), by_channel(of_heads(a["L1_attn_W_key"])),
                  of_heads(a["L1_attn_W_val"]), a["L1_attn_W_out"].reshape(D, D)], 1)], 1)
    cols = np.stack([a["L0_ffn_ln1_g"], a["L0_ffn_ln1_b"], a["L0_ffn_ln2_g"], a["L0_ffn_ln2_b"],
                     by_channel(a["L0_ffn_bq"]), by_channel(a["L0_ffn_bk"]),
                     *a["L0_ffn_e_b1"].reshape(4 * EXPERTS, D), *a["L1_ffn_b_in"]], 1)
    row = np.concatenate([a["L0_attn_b_out"], a["L0_ffn_bo"], a["L0_ffn_bv"], a["L0_ffn_br"]])[None, :]
    arrays = {
        "x": a["L0_attn_x"],
        "proj": proj,
        "w_expert_in": a["L0_ffn_e_w1"].transpose(1, 0, 2).reshape(D, EXPERTS, 4, D),
        "w_expert_out": a["L0_ffn_e_w2"].reshape(EXPERTS, 4, D, D).transpose(2, 0, 1, 3),
        "w_in": a["L1_ffn_w_in"].transpose(1, 0, 2),
        "w_out": a["L1_ffn_w_out"].transpose(1, 0, 2),
        "routers": np.stack([a["L0_ffn_Wr"], a["L1_ffn_router_w"]], 1),
        "cols": cols,
        "row": row,
        "expert_bias": np.stack([a["L0_ffn_e_b2"], a["L1_ffn_b_out"]], 1),
    }
    arrays = {name: np.ascontiguousarray(value) for name, value in arrays.items()}
    nc = bacc.Bacc("TRN2", target_bir_lowering=False, num_devices=1)
    args = [nc.dram_tensor(name, value.shape, F32, kind="ExternalInput").ap() for name, value in arrays.items()]
    out = nc.dram_tensor("out", arrays["x"].shape, F32, kind="ExternalOutput").ap()
    build(nc, *args, out)
    result = run_bass_kernel_spmd(nc, [arrays], core_ids=[0])
    return result.results[0]["out"]
```

```python
from contextlib import ExitStack

import concourse.bass as bass
from concourse import mybir

F32 = mybir.dt.float32
BF16 = mybir.dt.bfloat16
ALU = mybir.AluOpType
ACT = mybir.ActivationFunctionType
AX_X = mybir.AxisListType.X

P = 128
TILES = 4
HEADS, HD = 16, 8
QUADS, QH = 4, 4
EXPERTS = 8
EPS = 1e-5
SCALE = float(HD) ** -0.5
WORK_BANKS = 3
CLEAR_ORDER = (1, 2, 0)
PARTS = 3
MAX_ROW = 96
SUM_COL = 8
MASKED = -1e30
PER = 2048
CAUSAL = (True, True, False)

COL_G1, COL_B1, COL_G2, COL_B2, COL_BQ, COL_BK, COL_EB1 = range(7)
COL_BIN = COL_EB1 + 4 * EXPERTS
N_COLS = COL_BIN + EXPERTS
ROW_BOUT, ROW_BO, ROW_BV, ROW_BR = 0, P, 2 * P, 3 * P
N_ROW = 3 * P + EXPERTS


FIRST_STACKS = {(0, 0): 1, (0, 1): 2, (1, 0): 0, (1, 1): 1}
STACKS = {(1, 0): 0, (1, 1): 1, (0, 0): 2, (0, 1): 0, (2, 0): 1, (2, 1): 2}

COST = {"max": 3, "expert_in": 17, "expert_out": 17, "scores": 5, "values": 9, "project": 9, "turn": 5,
        "heads_turn": 4, "heads_back": 4, "out_project": 9, "route": 2, "route_turn": 4, "route_bias": 9}


def spread(main, extra):
    out, done, total, n = [], 0, sum(COST.get(step[0][0], 0) for step in main), 0
    for step in main:
        while n < len(extra) and done * len(extra) >= total * (n + 0.5):
            out += [extra[n]] if extra[n] else []
            n += 1
        out.append(step)
        done += COST.get(step[0][0], 0)
    return out + [step for step in extra[n:] if step]


def now(*steps):
    return [(step, False) for step in steps]


def ahead(*steps):
    return [(step, True) for step in steps]


def maxima(u, g, of=now):
    return of(*(("max", u, g, i, k) for i in range(TILES) for k in range(len(max_chunks(u, i)))))


def plans():
    def turn(u, g, of=now):
        return of(("max_turn", u, g))

    def heads(u, g, of=now):
        return of(("heads_turn", u, g))

    def projection(u):
        return (("project", u, 0), ("project", u, 1), ("project", u, 2))

    def stack(u, half):
        return tuple(("stack", u, half, n) for n in range(PARTS))

    stream = []
    turns = []

    def take(count):
        out = []
        for _ in range(count):
            out.append(stream.pop(0))
            for entry in turns:
                entry[1] -= 1
            (_, u, g, i, k), is_ahead = out[-1]
            if i == TILES - 1 and k == len(max_chunks(u, i)) - 1:
                turns.append([turn(u, g, ahead if is_ahead else now), 3])
            while turns and turns[0][1] == 0:
                out += turns.pop(0)[0]
        return out

    def due():
        out = [step for entry in turns for step in entry[0]]
        turns.clear()
        return out

    waiting = []

    def window(u, g, of, lag=2, early=(), extra=(), before=(), late=()):
        steps = []
        for j in range(TILES):
            for k in range(len(score_pairs(u, j))):
                steps += of(("scores", u, g, j, k))
                if k == 0:
                    while len(waiting) >= lag:
                        steps += waiting.pop(0)
                    if j == 0:
                        steps += before
                    if j == lag:
                        steps += early
            waiting.append(of(("values", u, g, j)))
        return spread(steps, list(extra)) + list(late)

    def rest():
        out = [step for steps in waiting for step in steps]
        waiting.clear()
        return out

    stream += [step for u, g in [(0, 0), (0, 1), (0, 2), (0, 3), (1, 0), (1, 1)] for step in maxima(u, g, ahead)]
    first = ahead(("load",), ("load_weights",), ("clear_v", 0), ("stats", "x"), ("norm", "x"), ("turn", "x"),
                  ("stats", "h"), ("clear_stack", 1), ("project", 0, 0), ("project", 0, 1), ("second", 0, 0),
                  ("second", 0, 1), ("parts", 0), ("norm", "h"), *stack(0, 0), ("clear_stack", 2), ("project", 0, 2),
                  ("turn", "h"), ("project", 1, 0), ("project", 1, 1), ("second", 1, 0), ("second", 1, 1), ("parts", 1))
    first += take(10) + ahead(*stack(0, 1), ("clear_stack", 0)) + take(4)
    first += ahead(("load_experts",)) + take(6)
    first += window(0, 0, ahead, extra=take(13) + ahead(("clear_v", 1), ("project", 1, 2), ("bias", 0), ("bias", 1)))
    first += window(0, 1, ahead, early=heads(0, 0, ahead),
                    extra=take(4) + ahead(*stack(1, 0), ("clear_v", 2)) + take(8))
    first += ahead(*stack(1, 1))
    first += window(0, 2, ahead, early=heads(0, 1, ahead), extra=take(11))
    first += window(0, 3, ahead, early=heads(0, 2, ahead), extra=take(len(stream)))
    first += rest() + due() + heads(0, 3, ahead) + ahead(("heads_back", 0), ("out_project", 0))
    stream += [step for u, g, of in ([(1, g, now) for g in (2, 3)] + [(0, g, ahead) for g in range(QUADS)]
                                     + [(2, g, now) for g in range(QUADS)] + [(1, g, ahead) for g in range(2)])
              for step in maxima(u, g, of)]
    steps = []
    steps += ahead(("load",))
    steps += window(1, 0, now, extra=take(4) + ahead(("stats", "x")) + take(3) + ahead(("norm", "x")) + take(3)
                    + ahead(("turn", "x")) + take(2), late=ahead(("project", 0, 0)) + ahead(("project", 0, 1)))
    steps += window(1, 1, now, before=take(1), early=heads(1, 0),
                    extra=ahead(("second", 0, 0)) + take(1) + ahead(("second", 0, 1), ("project", 0, 2), ("parts", 0))
                    + take(1) + ahead(*stack(0, 0)) + take(7))
    steps += window(1, 2, now, before=due(), early=heads(1, 1) + ahead(*stack(0, 1)), extra=[None] * 3 + take(6))
    steps += window(1, 3, now, early=heads(1, 2), extra=take(11))
    steps += (rest() + take(2) + heads(1, 3) + take(2) + now(("heads_back", 1)) + take(1)
              + now(("out_project", 1)))
    steps += window(0, 0, ahead, extra=now(("stats", "a")) + take(4) + now(("norm", "a")) + take(4) + now(("turn", "a")))
    steps += window(0, 1, ahead, early=heads(0, 0, ahead),
                    extra=now(("route", 0)) + take(1) + now(("gate_exp", 0)) + take(2))
    steps += rest() + ahead(("bias", 0), ("bias", 1))
    mixture = []
    for e in range(EXPERTS + 1):
        if e < EXPERTS:
            mixture += now(("expert_in", 0, e, 0), ("expert_in", 0, e, 1))
        if e == 1:
            mixture += now(("route_turn", 0))
        if e == EXPERTS - 1:
            mixture += ahead(("turn", "h"))
        if e:
            mixture += now(("expert_out", 0, e - 1, 0), ("expert_out", 0, e - 1, 1))
        if e == 1:
            mixture += now(("route_bias", 0))
        if e == EXPERTS - 1:
            mixture += ahead(*projection(1), ("second", 1, 0), ("second", 1, 1))
    steps += mixture[:1] + now(("gate", 0)) + mixture[1:3] + heads(0, 1, ahead)
    steps += spread(mixture[3:30], ahead(("stats", "h"), ("norm", "h")) + take(11) + due()) + mixture[30:]
    steps += ahead(("parts", 1)) + now(("stats", "y"))
    steps += window(0, 2, ahead, before=now(("norm", "y")), extra=[None] * 6 + now(("turn", "y")) + [None],
                    late=now(*projection(2)))
    steps += window(0, 3, ahead, early=heads(0, 2, ahead),
                    extra=now(("second", 2, 0), ("second", 2, 1), ("route", 1), ("parts", 2), *stack(2, 0),
                              ("gate_exp", 1)))
    steps += rest() + now(("gate", 1))
    steps += now(("expert_in", 1, 0, 0), ("expert_in", 1, 0, 1)) + heads(0, 3, ahead)
    steps += now(*stack(2, 1), ("expert_in", 1, 1, 0))
    steps += take(2) + now(("route_turn", 1)) + ahead(("heads_back", 0)) + take(1) + now(("route_bias", 1))
    steps += take(2) + ahead(("out_project", 0)) + take(1)
    steps += take(4) + now(("expert_in", 1, 1, 1)) + take(2)
    for k in range(4):
        steps += now(("expert_out", 1, 0, k)) + take(2)
    outs = [now(("expert_out", 1, 1, k)) for k in range(4)]
    steps += take(2) + outs[0] + take(1) + outs[1]
    steps += window(2, 0, now, lag=1, extra=take(7) + outs[2] + take(6) + outs[3] + take(6))
    steps += ahead(*stack(1, 0))
    steps += window(2, 1, now, early=heads(2, 0), extra=take(15))
    steps += window(2, 2, now, early=heads(2, 1) + ahead(*stack(1, 1)), extra=take(18))
    steps += window(2, 3, now, early=heads(2, 2), extra=take(len(stream)))
    steps += rest() + due() + heads(2, 3) + now(("heads_back", 2), ("out_project", 2), ("store",))
    return ([step for step, _ in first], [step for step, _ in steps],
            [step for step, is_ahead in steps if not is_ahead])


def score_pairs(u, j):
    width = P * (TILES - j) if CAUSAL[u] else P * TILES
    per_bank = {P: 4, 2 * P: 2}.get(width, 1)
    heads = min(QH, 2 * per_bank)
    return [(list(range(c, c + heads)), width, per_bank) for c in range(0, QH, heads)]


def max_chunks(u, i):
    keys = P * (i + 1) if CAUSAL[u] else P * TILES
    per_bank = {P: 4, 2 * P: 2}.get(keys, 1)
    return [(list(range(c, c + per_bank)), keys) for c in range(0, QH, per_bank)]


class Signal:

    def __init__(self, nc, ctx, name, step=1, first=PER, each=PER):
        self.sem = ctx.enter_context(nc.semaphore(name))
        self.step, self.n, self.first, self.each = step, 0, first, each

    def count(self):
        self.n += self.step
        return self.n


class Counts:

    def __init__(self, eng, name, signals):
        self.eng, self.k = eng, 0
        self.kinds = sorted({(sig.first, sig.each) for sig in signals})
        self.registers = [eng.alloc_register(f"{name}_count{i}") for i in range(6)]

    def begin(self, number, owned):
        self.base = {(first, each): first * min(number, 1) + each * max(number - 1, 0) for first, each in self.kinds}
        self.number, self.looped = number + 1, False
        for sig in owned:
            sig.n = 0

    def begin_looped(self, b, owned):
        self.base = {(first, each): self.eng.snap(b * each + first) for first, each in self.kinds}
        self.number, self.looped = self.eng.snap(b + 2), True
        for sig in owned:
            sig.n = 0

    def at(self, sig, n):
        base = self.base[sig.first, sig.each]
        if not self.looped:
            return base + n
        register = self.registers[self.k % len(self.registers)]
        self.k += 1
        self.eng.reg_add(register, base, n)
        return register


class Pass:

    def __init__(self, plan, stacks):
        self.plan, self.stacks = plan, stacks
        self.place = {step: n for n, step in enumerate(plan)}
        assert len(self.place) == len(plan)
        works = {kind: 1 for kind in ("turn", "project", "max", "max_turn", "heads_turn", "heads_back",
                                      "out_project", "route", "route_turn", "route_bias")}
        self.work, self.pair = {}, {}
        self.bank, self.bank_before = {}, {}
        self.slot, self.slot_before = {}, {}
        self.sum_before = {}
        self.done = {}
        self.act, self.pool = {}, {}
        self.dve = {}
        self.work_freed = {}
        self.stack_before = {}
        self.landed = {}
        n_act = n_pool = 0
        for step in plan:
            if step[0] == "heads_turn":
                assert self.before(("values", *step[1:], TILES - 1), step), step
            if step[0] in ("norm", "turn"):
                needed = ({"norm": "stats", "turn": "norm"}[step[0]], step[1])
                assert self.before(needed, step), step
            if step[0] == "max_turn":
                assert self.before(("max", *step[1:], TILES - 1, len(max_chunks(step[1], TILES - 1)) - 1), step), step
            if step[0] in ("heads_back", "out_project"):
                needed = ("heads_turn", step[1], QUADS - 1) if step[0] == "heads_back" else ("heads_back", step[1])
                assert self.before(needed, step), step
            if step[0] == "scores" and not self.before(("max_turn", *step[1:3]), step):
                assert step[1] == 1 and step[2] < 2, step
        free_slots, free_banks, last = [(n, None) for n in range(3)], [(n, None) for n in range(WORK_BANKS)], {}
        quad_before = None
        fills = {}
        self.max_quads = [step[1:] for step in plan if step[0] == "max_turn"]
        self.head_quads = [step[1:] for step in plan if step[0] == "heads_turn"]
        self.projects = [step[1] for step in plan if step[0] == "parts"]
        for step in plan:
            kind = step[0]
            if kind in works:
                self.work[step] = len(self.work)
            if kind in works or kind == "expert_out" and (step[1] or step[3] == 0):
                self.bank[step], self.bank_before[step] = free_banks.pop(0)
            if kind in works or kind == "expert_out" and step[1]:
                free_banks.append((self.bank[step], step))
            elif kind == "expert_out" and step[3]:
                self.bank[step] = self.bank[*step[:3], 0]
                free_banks.append((self.bank[step], step))
            if kind in ("scores", "expert_in"):
                self.pair[step] = len(self.pair)
                if step[-1] == 0:
                    self.slot[step[:-1]], self.slot_before[step[:-1]] = free_slots.pop(0)
            if kind in ("values", "expert_out"):
                self.done[step] = len(self.done) + 1
                if kind == "values" and step[3] == 0:
                    self.sum_before[step] = quad_before
                    quad_before = step[1:3]
                if kind == "values":
                    free_slots.append((self.slot["scores", *step[1:]], step))
                elif step[3] == (1, TILES - 1)[step[1]]:
                    free_slots.append((self.slot["expert_in", step[1], step[2]], step))
            if kind == "scores":
                last[stacks[step[1], step[2] // 2]] = step
            if kind == "stack":
                slot = stacks[step[1:3]]
                self.stack_before[step] = last.get(slot)
                fills[slot] = fills.get(slot, 0) + (step[3] == PARTS - 1)
                self.landed[step] = fills[slot]
            if kind in ("second", "gate_exp") or kind == "values" and step[3] == TILES - 1:
                n_act += 1
                self.act[step] = n_act
            if kind in ("norm", "bias"):
                n_pool += 1 if kind == "norm" else TILES
                self.pool[step] = n_pool

    def before(self, a, b):
        return a in self.place and self.place[a] < self.place[b]


def build(nc, x, proj, w_expert_in, w_expert_out, w_in, w_out, routers, cols, row, expert_bias, out):
    BATCH = x.shape[0]
    first_pass, middle_pass, last_pass = (
        Pass(plan, stacks) for plan, stacks in zip(plans(), (FIRST_STACKS, STACKS, STACKS)))
    ctx = ExitStack()
    with ctx:
        def sb(name, shape, dt=F32):
            return ctx.enter_context(nc.sbuf_tensor(name, shape, dt))

        signals = []

        def signal(name, counts_in=None, step=1):
            first, each = (counts_in(first_pass), counts_in(middle_pass)) if counts_in else (PER, PER)
            signals.append(Signal(nc, ctx, name, step, first, each))
            return signals[-1]

        projs = sb("projs", [P, 3, 4, P])
        ew1 = sb("ew1", [P, EXPERTS, 4, P])
        ew2 = sb("ew2", [P, EXPERTS, 4, P])
        win = sb("win", [P, EXPERTS, P])
        wout = sb("wout", [P, EXPERTS, P])
        router = sb("router", [P, 2, EXPERTS])
        col = sb("col", [P, N_COLS])
        rows = sb("rows", [P, N_ROW])
        ebias = sb("ebias", [EXPERTS, 2, P])
        ident = sb("ident", [P, P])
        ident16 = sb("ident16", [P, P], BF16)
        mask_qk = sb("mask_qk", [P, P], BF16)
        mask_kq = sb("mask_kq", [P, P], BF16)
        minus_half = sb("minus_half", [P, TILES])
        rank = sb("rank", [P, TILES, EXPERTS])

        x_in = sb("x_in", [P, TILES, P])
        xn = sb("xn", [P, TILES, P])
        hn = sb("hn", [P, TILES, P])
        x_bias = sb("x_bias", [P, TILES, P])
        a_sum = sb("a_sum", [P, TILES, P])
        acc = sb("acc", [P, TILES, P])
        xT = sb("xT", [P, TILES * P])
        hT = sb("hT", [P, TILES * P])
        q_stack = [sb(f"q_stack{s}", [P, HEADS // 2, TILES * P], BF16) for s in range(3)]
        k_stack = [sb(f"k_stack{s}", [P, HEADS // 2, TILES * P], BF16) for s in range(3)]
        v_ones = [sb(f"v_ones{u}", [P, TILES, HEADS, 32]) for u in range(3)]
        part = [sb(f"part{u}", [P, 2, PARTS, TILES * P], BF16) for u in range(3)]
        rest = sb("rest", [P, 2, TILES * P])
        probs = sb("probs", [P, 3, QH, TILES * P])
        head_sums = sb("head_sums", [P, 2, TILES * P])
        heads = sb("heads", [P, TILES, P])
        inv_sum = sb("inv_sum", [P, TILES, QH])
        headsT = sb("headsT", [P, TILES * P])
        neg_max = sb("neg_max", [P, 2, QH, TILES])
        max_part = sb("max_part", [P, 2, PARTS, QH * TILES], BF16)
        max_rest = sb("max_rest", [P, 2, QH * TILES])
        maxT = sb("maxT", [PARTS * QH * TILES, 2, P], BF16)
        stats = sb("stats", [P, TILES, 6])
        mean_var = sb("mean_var", [P, TILES, 2])
        var_eps = sb("var_eps", [P, TILES])
        rstd = sb("rstd", [P, TILES])
        logit = sb("logit", [P, TILES, EXPERTS])
        top8 = sb("top8", [P, TILES, 8])
        gate_a = sb("gate_a", [P, TILES, EXPERTS])
        gate_b = sb("gate_b", [P, TILES, EXPERTS])
        gate_c = sb("gate_c", [P, TILES, EXPERTS])
        gate_s = sb("gate_s", [P, TILES])
        gate_t = sb("gate_t", [P, TILES])
        gate = sb("gate", [P, TILES, EXPERTS])
        gateT = sb("gateT", [EXPERTS, TILES * P])

        psum = ctx.enter_context(nc.psum_tensor("psum", [P, 8, 512], F32))
        pair_bank = [psum[:, 0:2, :], psum[:, 2:4, :]]
        sum_bank = psum[:, 4, :]
        work_bank = [psum[:, 5 + n, :] for n in range(WORK_BANKS)]

        first_loaded = ctx.enter_context(nc.semaphore("first_loaded"))
        loaded = ctx.enter_context(nc.semaphore("loaded"))
        experts_loaded = ctx.enter_context(nc.semaphore("experts_loaded"))
        made = ctx.enter_context(nc.semaphore("made"))
        arrived = {e: ctx.enter_context(nc.semaphore(f"arrived_{e}")) for e in ("pe", "act", "dve", "pool", "sp")}
        passed = {e: ctx.enter_context(nc.semaphore(f"passed_{e}")) for e in arrived}
        work_full = signal("work_full")
        pair_full = signal("pair_full")
        values_done = signal("values_done")
        vector_done = signal("vector_done")
        probs_ready = signal("probs_ready")
        scalar_done = signal("scalar_done")
        gpsimd_done = signal("gpsimd_done")

        def fills(slot, dmas):
            return lambda ps: 16 * dmas * sum(step[3] == 0 and ps.stacks[step[1:3]] == slot for step in ps.landed)

        x_moved = signal("x_moved", lambda ps: 16 * ((("load",) in ps.place) + (("store",) in ps.place)), 16)
        SYNC_DMAS, GPSIMD_DMAS = 12, 6
        sync_landed = [signal(f"sync_landed{slot}", fills(slot, SYNC_DMAS), 16) for slot in range(3)]
        gpsimd_landed = [signal(f"gpsimd_landed{slot}", fills(slot, GPSIMD_DMAS), 16) for slot in range(3)]
        max_landed = [signal("max_landed0", lambda ps: 16 * ((len(ps.max_quads) + 1) // 2), 16),
                      signal("max_landed1", lambda ps: 16 * (len(ps.max_quads) // 2), 16)]

        N_LOADS, N_EXPERT_LOADS = 5, 4
        N_MADE = 8

        block = ctx.enter_context(nc.Block())

        @block.vector
        def _(eng):
            eng.memset(minus_half[:, :], -0.5)
            for e in range(EXPERTS):
                eng.memset(rank[:, :, e:e + 1], float(EXPERTS - e))

            counts = Counts(eng, "dve", signals)
            at = counts.at
            owned = (vector_done,)

            def run(ps, b):
                def bank(step):
                    eng.wait_ge(work_full.sem, at(work_full, ps.work[step] + 1))
                    return work_bank[ps.bank[step]]

                for step in ps.plan:
                    kind = step[0]
                    if kind == "clear_v":
                        _, u = step
                        eng.memset(v_ones[u][:, :, :, :], 0.0).then_inc(vector_done.sem, 1)
                        eng.wait_ge(vector_done.sem, at(vector_done, vector_done.count()))
                        eng.memset(v_ones[u][:, :, :, SUM_COL:SUM_COL + 1], 1.0).then_inc(vector_done.sem, 1)
                        ps.dve[step] = vector_done.count()
                    elif kind == "stats":
                        what = step[1]
                        src = {"x": x_in, "h": xn, "a": a_sum, "y": acc}[what]
                        if what == "x":
                            eng.wait_ge(x_moved.sem, at(x_moved, 16))
                        eng.wait_ge(vector_done.sem, at(vector_done, vector_done.n))
                        for t in range(TILES):
                            eng.bn_stats(stats[:, t, :], src[:, t, :]).then_inc(vector_done.sem, 1)
                            n = vector_done.count()
                        eng.wait_ge(vector_done.sem, at(vector_done, n))
                        eng.sem_inc(passed["dve"], 1)
                        for t in range(TILES):
                            eng.bn_aggr(mean_var[:, t, :], stats[:, t, :]).then_inc(vector_done.sem, 1)
                            n = vector_done.count()
                        eng.wait_ge(vector_done.sem, at(vector_done, n))
                        eng.tensor_scalar(var_eps[:, :], mean_var[:, :, 1], EPS, None, ALU.add)\
                           .then_inc(vector_done.sem, 1)
                        ps.dve[step] = vector_done.count()
                    elif kind == "norm":
                        what = step[1]
                        src = {"x": x_in, "h": xn, "a": a_sum, "y": acc}[what]
                        dst = hn if what in ("h", "a") else xn
                        if what == "y" and ps.before(("bias", 1), step):
                            eng.wait_ge(gpsimd_done.sem, at(gpsimd_done, ps.pool["bias", 1]))
                        eng.wait_ge(gpsimd_done.sem, at(gpsimd_done, ps.pool[step]))
                        for t in range(TILES):
                            eng.tensor_scalar(dst[:, t, :], src[:, t, :], mean_var[:, t, 0:1], rstd[:, t:t + 1],
                                              ALU.subtract, ALU.mult).then_inc(vector_done.sem, 1)
                            n = vector_done.count()
                        ps.dve[step] = n
                        if what == "a":
                            if ps is last_pass:
                                eng.wait_ge(x_moved.sem, at(x_moved, 0))
                            eng.tensor_tensor(acc[:, :, :], x_bias[:, :, :], a_sum[:, :, :], ALU.add)\
                               .then_inc(vector_done.sem, 1)
                            ps.dve["residual"] = vector_done.count()
                    elif kind == "turn":
                        src = bank(step)
                        if step[1] in ("x", "y"):
                            eng.tensor_copy(xT[:, :], src).then_inc(vector_done.sem, 1)
                            n = vector_done.count()
                        else:
                            if ps is first_pass:
                                eng.wait_ge(loaded, 16 * N_LOADS)
                            g = COL_G1 if step[1] == "h" else COL_G2
                            eng.tensor_scalar(hT[:, :], src, col[:, g:g + 1], col[:, g + 1:g + 2],
                                              ALU.mult, ALU.add).then_inc(vector_done.sem, 1)
                            n = vector_done.count()
                        ps.work_freed[step] = n
                        ps.dve[step] = n
                    elif kind == "project" and step[2] < 2:
                        _, u, k = step
                        src = bank(step)
                        if u == 1:
                            c = (COL_BQ, COL_BK)[k]
                            eng.tensor_scalar(part[u][:, k, 0, :], src, col[:, c:c + 1], None, ALU.add)\
                               .then_inc(vector_done.sem, 1)
                            n = vector_done.count()
                        else:
                            eng.tensor_copy(part[u][:, k, 0, :], src).then_inc(vector_done.sem, 1)
                            n = vector_done.count()
                        eng.wait_ge(vector_done.sem, at(vector_done, n))
                        p = ps.projects.index(u)
                        if p:
                            eng.wait_ge(scalar_done.sem, at(scalar_done, ps.act["second", ps.projects[p - 1], k]))
                        if u == 1:
                            eng.scalar_tensor_tensor(out=rest[:, k, :], in0=src, scalar=col[:, c:c + 1],
                                                     in1=part[u][:, k, 0, :], op0=ALU.add,
                                                     op1=ALU.subtract).then_inc(vector_done.sem, 1)
                            n = vector_done.count()
                        else:
                            eng.tensor_tensor(rest[:, k, :], src, part[u][:, k, 0, :], ALU.subtract)\
                               .then_inc(vector_done.sem, 1)
                            n = vector_done.count()
                        ps.work_freed[step] = n
                        ps.dve[step] = n
                    elif kind == "project":
                        u = step[1]
                        if ps.before(("values", u, QUADS - 1, TILES - 1), step):
                            eng.wait_ge(values_done.sem, at(values_done, ps.done["values", u, QUADS - 1, TILES - 1]))
                        if ps.before(("clear_v", u), step):
                            eng.wait_ge(vector_done.sem, at(vector_done, ps.dve["clear_v", u]))
                        v = bank(step).rearrange("p (t h c) -> p t h c", t=TILES, h=HEADS)
                        if u == 1:
                            bv = rows[:, ROW_BV:ROW_BV + P].rearrange("p (h c) -> p h c", h=HEADS)
                            for t in range(TILES):
                                eng.tensor_tensor(v_ones[u][:, t, :, 0:HD], v[:, t], bv, ALU.add)\
                                   .then_inc(vector_done.sem, 1)
                                n = vector_done.count()
                        else:
                            for t in range(TILES):
                                eng.tensor_copy(v_ones[u][:, t, :, 0:HD], v[:, t]).then_inc(vector_done.sem, 1)
                                n = vector_done.count()
                        ps.work_freed[step] = n
                        ps.dve[step] = n
                    elif kind == "parts":
                        u = step[1]
                        for k in range(2):
                            eng.wait_ge(scalar_done.sem, at(scalar_done, ps.act["second", u, k]))
                            eng.tensor_tensor(part[u][:, k, 2, :], rest[:, k, :], part[u][:, k, 1, :],
                                              ALU.subtract).then_inc(vector_done.sem, 1)
                            ps.dve["part3", u, k] = vector_done.count()
                        eng.wait_ge(vector_done.sem, at(vector_done, vector_done.n))
                    elif kind == "max":
                        _, u, g, i, k = step
                        q = ps.max_quads.index((u, g))
                        hs, keys = max_chunks(u, i)[k]
                        src = bank(step)[:, 0:len(hs) * keys].rearrange("p (h k) -> p h k", h=len(hs))
                        eng.tensor_reduce(neg_max[:, q % 2, hs[0]:hs[0] + len(hs), i], src, AX_X,
                                          ALU.max, negate=True).then_inc(vector_done.sem, 1)
                        n = vector_done.count()
                        ps.work_freed[step] = n
                        if i == TILES - 1 and k == len(max_chunks(u, i)) - 1:
                            m = neg_max[:, q % 2, :, :].rearrange("p h i -> p (h i)")
                            parts, left = max_part[:, q % 2], max_rest[:, q % 2, :]
                            eng.wait_ge(vector_done.sem, at(vector_done, n))
                            if q >= 2:
                                eng.wait_ge(work_full.sem, at(work_full, ps.work["max_turn", *ps.max_quads[q - 2]] + 1))
                            eng.tensor_copy(parts[:, 0, :], m).then_inc(vector_done.sem, 1)
                            eng.wait_ge(vector_done.sem, at(vector_done, vector_done.count()))
                            eng.tensor_tensor(left, m, parts[:, 0, :], ALU.subtract).then_inc(vector_done.sem, 1)
                            eng.wait_ge(vector_done.sem, at(vector_done, vector_done.count()))
                            eng.tensor_copy(parts[:, 1, :], left).then_inc(vector_done.sem, 1)
                            eng.wait_ge(vector_done.sem, at(vector_done, vector_done.count()))
                            eng.tensor_tensor(parts[:, 2, :], left, parts[:, 1, :], ALU.subtract)\
                               .then_inc(vector_done.sem, 1)
                            ps.dve["max_part", u, g] = vector_done.count()
                    elif kind == "max_turn":
                        q = ps.max_quads.index(step[1:])
                        rows48 = PARTS * QH * TILES
                        src = bank(step)[0:rows48, 0:P // 2].bitcast(BF16)
                        if q >= 2:
                            eng.wait_ge(max_landed[q % 2].sem, at(max_landed[q % 2], 16 * (q // 2)))
                        eng.tensor_copy(maxT[:, q % 2, :], src).then_inc(vector_done.sem, 1)
                        n = vector_done.count()
                        ps.work_freed[step] = n
                        ps.dve[step] = n
                    elif kind == "heads_turn":
                        _, u, g = step
                        src = bank(step).rearrange("p (t h c) -> p t h c", t=TILES, h=QH)
                        eng.wait_ge(vector_done.sem, at(vector_done, vector_done.n))
                        eng.reciprocal(inv_sum[:, :, :], src[:, :, :, SUM_COL]).then_inc(vector_done.sem, 1)
                        eng.wait_ge(vector_done.sem, at(vector_done, vector_done.count()))
                        dst = heads[:, :, g * QH * HD:(g + 1) * QH * HD].rearrange("p t (h c) -> p t h c", h=QH)
                        inv = inv_sum[:, :, :].unsqueeze(3).to_broadcast([P, TILES, QH, HD])
                        eng.tensor_tensor(dst, src[:, :, :, 0:HD], inv, ALU.mult).then_inc(vector_done.sem, 1)
                        n = vector_done.count()
                        ps.work_freed[step] = n
                        ps.dve[step] = n
                    elif kind == "heads_back":
                        eng.tensor_copy(headsT[:, :], bank(step)).then_inc(vector_done.sem, 1)
                        n = vector_done.count()
                        ps.work_freed[step] = n
                        ps.dve[step] = n
                    elif kind == "out_project":
                        u = step[1]
                        dst = (x_bias, a_sum, acc)[u]
                        if ps.before(("bias", u), step):
                            eng.wait_ge(gpsimd_done.sem, at(gpsimd_done, ps.pool["bias", u]))
                        elif u == 2:
                            eng.wait_ge(vector_done.sem, at(vector_done, ps.dve["expert_out", 1, 1, 3]))
                        eng.tensor_tensor(dst[:, :, :].rearrange("p t c -> p (t c)"), bank(step),
                                          dst[:, :, :].rearrange("p t c -> p (t c)"), ALU.add)\
                                                        .then_inc(vector_done.sem, 1)
                        n = vector_done.count()
                        ps.work_freed[step] = n
                        ps.dve[step] = n
                    elif kind == "route":
                        layer = step[1]
                        src = bank(step)[:, 0:TILES * EXPERTS].rearrange("p (t e) -> p t e", t=TILES)

                        def wide(t):
                            return t[:, :].unsqueeze(2).to_broadcast([P, TILES, EXPERTS])

                        if layer == 0:
                            br = rows[:, ROW_BR:ROW_BR + EXPERTS]
                            for t in range(TILES):
                                eng.tensor_tensor(logit[:, t, :], src[:, t, :], br, ALU.add)\
                                   .then_inc(vector_done.sem, 1)
                                n = vector_done.count()
                        else:
                            eng.tensor_copy(logit[:, :, :], src).then_inc(vector_done.sem, 1)
                            n = vector_done.count()
                        ps.work_freed[step] = n
                        eng.wait_ge(vector_done.sem, at(vector_done, n))
                        eng.tensor_reduce(gate_s[:, :], logit[:, :, :], AX_X, ALU.max).then_inc(vector_done.sem, 1)
                        eng.wait_ge(vector_done.sem, at(vector_done, vector_done.count()))
                        eng.tensor_tensor(gate_a[:, :, :], logit[:, :, :], wide(gate_s), ALU.subtract)\
                           .then_inc(vector_done.sem, 1)
                        ps.dve["logit", layer] = vector_done.count()
                    elif kind == "gate":
                        layer = step[1]

                        def wide(t):
                            return t[:, :].unsqueeze(2).to_broadcast([P, TILES, EXPERTS])

                        eng.wait_ge(vector_done.sem, at(vector_done, vector_done.n))
                        eng.sem_inc(passed["dve"], 1)
                        if layer == 0:
                            for t in range(TILES):
                                eng.max(top8[:, t, :], logit[:, t, :]).then_inc(vector_done.sem, 1)
                                n = vector_done.count()
                            eng.wait_ge(vector_done.sem, at(vector_done, n))
                            eng.tensor_tensor(gate_c[:, :, :], logit[:, :, :],
                                              top8[:, :, 1:2].to_broadcast([P, TILES, EXPERTS]),
                                              ALU.is_ge).then_inc(vector_done.sem, 1)
                            eng.wait_ge(vector_done.sem, at(vector_done, vector_done.count()))
                            eng.wait_ge(scalar_done.sem, at(scalar_done, ps.act["gate_exp", 0]))
                            eng.tensor_tensor(gate_b[:, :, :], gate_b[:, :, :], gate_c[:, :, :], ALU.mult)\
                               .then_inc(vector_done.sem, 1)
                            eng.wait_ge(vector_done.sem, at(vector_done, vector_done.count()))
                            eng.tensor_reduce(gate_s[:, :], gate_b[:, :, :], AX_X, ALU.add).then_inc(vector_done.sem, 1)
                            eng.wait_ge(vector_done.sem, at(vector_done, vector_done.count()))
                            eng.reciprocal(gate_t[:, :], gate_s[:, :]).then_inc(vector_done.sem, 1)
                            eng.wait_ge(vector_done.sem, at(vector_done, vector_done.count()))
                            eng.tensor_tensor(gate[:, :, :], gate_b[:, :, :], wide(gate_t), ALU.mult)\
                               .then_inc(vector_done.sem, 1)
                            n = vector_done.count()
                        else:
                            eng.wait_ge(scalar_done.sem, at(scalar_done, ps.act["gate_exp", 1]))
                            eng.tensor_reduce(gate_s[:, :], gate_b[:, :, :], AX_X, ALU.add).then_inc(vector_done.sem, 1)
                            eng.wait_ge(vector_done.sem, at(vector_done, vector_done.count()))
                            eng.reciprocal(gate_t[:, :], gate_s[:, :]).then_inc(vector_done.sem, 1)
                            eng.wait_ge(vector_done.sem, at(vector_done, vector_done.count()))
                            eng.tensor_tensor(logit[:, :, :], gate_b[:, :, :], wide(gate_t), ALU.mult)\
                               .then_inc(vector_done.sem, 1)
                            n = vector_done.count()
                            eng.wait_ge(vector_done.sem, at(vector_done, n))
                            left = logit
                            for turn, picked in enumerate((gate_a, gate_b)):
                                eng.tensor_reduce(gate_s[:, :], left[:, :, :], AX_X, ALU.max)\
                                   .then_inc(vector_done.sem, 1)
                                eng.wait_ge(vector_done.sem, at(vector_done, vector_done.count()))
                                eng.tensor_tensor(gate_c[:, :, :], left[:, :, :], wide(gate_s), ALU.is_ge)\
                                   .then_inc(vector_done.sem, 1)
                                eng.wait_ge(vector_done.sem, at(vector_done, vector_done.count()))
                                eng.tensor_tensor(gate_c[:, :, :], gate_c[:, :, :], rank[:, :, :], ALU.mult)\
                                   .then_inc(vector_done.sem, 1)
                                eng.wait_ge(vector_done.sem, at(vector_done, vector_done.count()))
                                eng.tensor_reduce(gate_t[:, :], gate_c[:, :, :], AX_X, ALU.max)\
                                   .then_inc(vector_done.sem, 1)
                                eng.wait_ge(vector_done.sem, at(vector_done, vector_done.count()))
                                eng.tensor_tensor(picked[:, :, :], gate_c[:, :, :], wide(gate_t),
                                                  ALU.is_equal).then_inc(vector_done.sem, 1)
                                eng.wait_ge(vector_done.sem, at(vector_done, vector_done.count()))
                                if turn == 0:
                                    eng.scalar_tensor_tensor(out=top8[:, :, :], in0=picked[:, :, :],
                                                             scalar=-2.0, in1=logit[:, :, :],
                                                             op0=ALU.mult, op1=ALU.add)\
                                                                           .then_inc(vector_done.sem, 1)
                                    eng.wait_ge(vector_done.sem, at(vector_done, vector_done.count()))
                                    left = top8
                            eng.tensor_tensor(gate_a[:, :, :], gate_a[:, :, :], gate_b[:, :, :], ALU.add)\
                               .then_inc(vector_done.sem, 1)
                            eng.wait_ge(vector_done.sem, at(vector_done, vector_done.count()))
                            eng.tensor_tensor(gate[:, :, :], gate_a[:, :, :], logit[:, :, :], ALU.mult)\
                               .then_inc(vector_done.sem, 1)
                            n = vector_done.count()
                        ps.dve[step] = n
                    elif kind == "route_turn":
                        eng.tensor_copy(gateT[:, :], bank(step)[0:EXPERTS, :]).then_inc(vector_done.sem, 1)
                        n = vector_done.count()
                        ps.work_freed[step] = n
                        ps.dve[step] = n
                    elif kind == "route_bias":
                        eng.wait_ge(vector_done.sem, at(vector_done, vector_done.n))
                        flat = acc[:, :, :].rearrange("p t c -> p (t c)")
                        eng.tensor_tensor(flat, bank(step), flat, ALU.add).then_inc(vector_done.sem, 1)
                        n = vector_done.count()
                        ps.work_freed[step] = n
                        ps.dve[step] = n
                    elif kind == "expert_out":
                        _, layer, e, k = step
                        if layer == 0 and k == 0:
                            continue
                        expert = e if layer == 0 else 4 * e + k
                        eng.wait_ge(values_done.sem, at(values_done, ps.done[step]))
                        src = work_bank[ps.bank[step]]
                        eng.wait_ge(vector_done.sem, at(vector_done, vector_done.n))
                        for t in range(TILES):
                            eng.scalar_tensor_tensor(
                                out=acc[:, t, :], in0=src[:, t * P:(t + 1) * P],
                                scalar=gate[:, t, expert:expert + 1], in1=acc[:, t, :],
                                op0=ALU.mult, op1=ALU.add).then_inc(vector_done.sem, 1)
                            n = vector_done.count()
                        ps.work_freed[step] = n
                        ps.dve[step] = n
                eng.wait_ge(vector_done.sem, at(vector_done, vector_done.n))
                eng.sem_inc(vector_done.sem, PER - vector_done.n)
                eng.sem_inc(arrived["dve"], 1)
                eng.wait_ge(arrived["pe"], counts.number)
                eng.sem_inc(passed["dve"], 1)
                eng.wait_ge(arrived["act"], counts.number)
                eng.sem_inc(passed["dve"], 1)
                eng.wait_ge(arrived["pool"], counts.number)
                eng.sem_inc(passed["dve"], 1)
                eng.wait_ge(arrived["sp"], counts.number)
                eng.sem_inc(passed["dve"], 1)

            counts.begin(0, owned)
            run(first_pass, 0)
            with eng.Fori(0, BATCH - 1) as b:
                counts.begin_looped(b, owned)
                run(middle_pass, b)
            counts.begin(BATCH, owned)
            run(last_pass, BATCH - 1)

        @block.scalar
        def _(eng):
            counts = Counts(eng, "act", signals)
            at = counts.at
            owned = (scalar_done, probs_ready)

            def run(ps, b):
                for step in ps.plan:
                    kind = step[0]
                    if kind == "second":
                        _, u, k = step
                        eng.wait_ge(vector_done.sem, at(vector_done, ps.dve["project", u, k]))
                        eng.activation(part[u][:, k, 1, :], rest[:, k, :], ACT.Copy).then_inc(scalar_done.sem, 1)
                        assert scalar_done.count() == ps.act[step]
                    elif kind == "scores":
                        _, u, g, j, k = step
                        hs, width, per_bank = score_pairs(u, j)[k]
                        n = ps.pair[step]
                        reader = ps.slot_before[step[:-1]]
                        if k == 0 and reader:
                            eng.wait_ge(values_done.sem, at(values_done, ps.done[reader]))
                        eng.wait_ge(pair_full.sem, at(pair_full, n + 1))
                        dst = probs[:, ps.slot[step[:-1]], hs[0]:hs[0] + len(hs), TILES * P - width:TILES * P]
                        if per_bank == 1:
                            src = pair_bank[n % 2][:, :, 0:width]
                        else:
                            src = pair_bank[n % 2].rearrange("p a q -> p (a q)")[:, 0:len(hs) * width]
                            src = src.rearrange("p (h q) -> p h q", h=len(hs))
                        eng.activation(dst, src, ACT.Exp, scale=SCALE).then_inc(probs_ready.sem, 1)
                        assert probs_ready.count() == n + 1
                    elif kind == "values" and step[3] == TILES - 1:
                        _, u, g, j = step
                        eng.wait_ge(values_done.sem, at(values_done, ps.done[step]))
                        q = ps.head_quads.index((u, g))
                        if q >= 2:
                            eng.wait_ge(work_full.sem, at(work_full, ps.work["heads_turn", *ps.head_quads[q - 2]] + 1))
                        eng.activation(head_sums[:, q % 2, :], sum_bank,
                                       ACT.Copy).then_inc(scalar_done.sem, 1)
                        assert scalar_done.count() == ps.act[step]
                    elif kind == "gate_exp":
                        eng.wait_ge(vector_done.sem, at(vector_done, ps.dve["logit", step[1]]))
                        eng.activation(gate_b[:, :, :], gate_a[:, :, :], ACT.Exp).then_inc(scalar_done.sem, 1)
                        assert scalar_done.count() == ps.act[step]
                    elif kind == "expert_in":
                        _, layer, e, k = step
                        n = ps.pair[step]
                        reader = ps.slot_before[step[:-1]]
                        if k == 0 and reader:
                            eng.wait_ge(values_done.sem, at(values_done, ps.done[reader]))
                        eng.wait_ge(pair_full.sem, at(pair_full, n + 1))
                        for f in range(2):
                            c = (COL_BIN if layer else COL_EB1) + 4 * e + 2 * k + f
                            ins = eng.activation(probs[:, ps.slot[step[:-1]], 2 * k + f, :], pair_bank[n % 2][:, f, :],
                                                 ACT.Gelu_apprx_tanh if layer else ACT.Gelu, bias=col[:, c:c + 1])
                        ins.then_inc(probs_ready.sem, 1)
                        assert probs_ready.count() == n + 1
                eng.wait_ge(scalar_done.sem, at(scalar_done, scalar_done.n))
                eng.sem_inc(scalar_done.sem, PER - scalar_done.n)
                eng.wait_ge(probs_ready.sem, at(probs_ready, probs_ready.n))
                eng.sem_inc(probs_ready.sem, PER - probs_ready.n)
                eng.sem_inc(arrived["act"], 1)
                eng.wait_ge(arrived["pe"], counts.number)
                eng.sem_inc(passed["act"], 1)
                eng.wait_ge(arrived["dve"], counts.number)
                eng.sem_inc(passed["act"], 1)
                eng.wait_ge(arrived["pool"], counts.number)
                eng.sem_inc(passed["act"], 1)
                eng.wait_ge(arrived["sp"], counts.number)
                eng.sem_inc(passed["act"], 1)

            counts.begin(0, owned)
            run(first_pass, 0)
            with eng.Fori(0, BATCH - 1) as b:
                counts.begin_looped(b, owned)
                run(middle_pass, b)
            counts.begin(BATCH, owned)
            run(last_pass, BATCH - 1)

        @block.tensor
        def _(eng):
            counts = Counts(eng, "pe", signals)
            at = counts.at
            owned = (work_full, pair_full, values_done)

            def run(ps, b):
                def bank(step):
                    if ps.bank_before[step]:
                        eng.wait_ge(vector_done.sem, at(vector_done, ps.work_freed[ps.bank_before[step]]))
                    return work_bank[ps.bank[step]]

                def pair(step):
                    n = ps.pair[step]
                    if n >= 2:
                        eng.wait_ge(probs_ready.sem, at(probs_ready, n - 1))
                    return pair_bank[n % 2]

                for step in ps.plan:
                    kind = step[0]
                    if kind == "turn":
                        src = hn if step[1] in ("h", "a") else xn
                        if ps is first_pass and step[1] == "x":
                            eng.wait_ge(made, N_MADE)
                        eng.wait_ge(vector_done.sem, at(vector_done, ps.dve["norm", step[1]]))
                        dst = bank(step)
                        for t in range(TILES):
                            ins = eng.transpose(dst[:, t * P:(t + 1) * P], src[:, t, :], ident[:, :])
                        ins.then_inc(work_full.sem, 1)
                        work_full.count()
                    elif kind == "project":
                        _, u, k = step
                        src = hT if u == 1 else xT
                        if ps is first_pass and (u, k) == (0, 0):
                            eng.wait_ge(first_loaded, 16)
                        eng.wait_ge(vector_done.sem, at(vector_done, ps.dve["turn", ("x", "h", "y")[u]]))
                        dst = bank(step)
                        if k < 2:
                            ins = eng.matmul(dst, projs[:, u, k, :], src[:, :], start=True, stop=True)
                        else:
                            for t in range(TILES):
                                ins = eng.matmul(dst[:, t * P:(t + 1) * P], src[:, t * P:(t + 1) * P],
                                                 projs[:, u, 2, :], start=True, stop=True)
                        ins.then_inc(work_full.sem, 1)
                        work_full.count()
                    elif kind == "max":
                        _, u, g, i, k = step
                        slot = ps.stacks[u, g // 2]
                        if (g % 2, i, k) == (0, 0, 0) and ps.before(("stack", u, g // 2, PARTS - 1), step):
                            n = 16 * ps.landed["stack", u, g // 2, PARTS - 1]
                            eng.wait_ge(sync_landed[slot].sem, at(sync_landed[slot], SYNC_DMAS * n))
                            eng.wait_ge(gpsimd_landed[slot].sem, at(gpsimd_landed[slot], GPSIMD_DMAS * n))
                        hs, keys = max_chunks(u, i)[k]
                        dst = bank(step)
                        for c, h in enumerate(hs):
                            head, col0 = 4 * (g % 2) + h, c * keys
                            ins = eng.matmul(dst[:, col0:col0 + keys],
                                             q_stack[slot][0:MAX_ROW, head, i * P:(i + 1) * P],
                                             k_stack[slot][0:MAX_ROW, head, 0:keys], start=True, stop=not CAUSAL[u])
                            if CAUSAL[u]:
                                ins = eng.matmul(dst[:, col0 + keys - P:col0 + keys], ident16[:, :], mask_qk[:, :],
                                                 start=False, stop=True)
                        ins.then_inc(work_full.sem, 1)
                        work_full.count()
                    elif kind == "max_turn":
                        q = ps.max_quads.index(step[1:])
                        dst = bank(step)[0:PARTS * QH * TILES, 0:P // 2].bitcast(BF16)
                        eng.wait_ge(vector_done.sem, at(vector_done, ps.dve["max_part", step[1], step[2]]))
                        eng.sem_inc(passed["pe"], 1)
                        eng.transpose(dst, max_part[:, q % 2].rearrange("p a b -> p (a b)"),
                                      ident16[:, :]).then_inc(work_full.sem, 1)
                        work_full.count()
                    elif kind == "scores":
                        _, u, g, j, k = step
                        slot = ps.stacks[u, g // 2]
                        if j == 0 and k == 0 and ps.before(("max_turn", u, g), step):
                            q = ps.max_quads.index((u, g))
                            eng.wait_ge(max_landed[q % 2].sem, at(max_landed[q % 2], 16 * (q // 2 + 1)))
                        hs, width, per_bank = score_pairs(u, j)[k]
                        dst = pair(step)
                        for c, h in enumerate(hs):
                            head, col0 = 4 * (g % 2) + h, (c % per_bank) * width
                            o = dst[:, c // per_bank, col0:col0 + width]
                            ins = eng.matmul(o, k_stack[slot][:, head, j * P:(j + 1) * P],
                                             q_stack[slot][:, head, TILES * P - width:TILES * P],
                                             start=True, stop=not CAUSAL[u])
                            if CAUSAL[u]:
                                ins = eng.matmul(o[:, 0:P], ident16[:, :], mask_kq[:, :], start=False, stop=True)
                        ins.then_inc(pair_full.sem, 1)
                        assert pair_full.count() == ps.pair[step] + 1
                    elif kind == "values":
                        _, u, g, j = step
                        if j == 0 and ps.sum_before[step]:
                            eng.wait_ge(scalar_done.sem,
                                        at(scalar_done, ps.act["values", *ps.sum_before[step], TILES - 1]))
                        if j == 0 and ps.before(("project", u, 2), step):
                            eng.wait_ge(vector_done.sem, at(vector_done, ps.dve["project", u, 2]))
                        last_pair = ("scores", u, g, j, len(score_pairs(u, j)) - 1)
                        eng.wait_ge(probs_ready.sem, at(probs_ready, ps.pair[last_pair] + 1))
                        q0 = P * j if CAUSAL[u] else 0
                        for c in range(QH):
                            ins = eng.matmul(sum_bank[32 * c:32 * c + 32, q0:TILES * P],
                                             v_ones[u][:, j, 4 * g + c, :],
                                             probs[:, ps.slot["scores", u, g, j], c, q0:TILES * P],
                                             start=(j == 0), stop=(j == TILES - 1))
                        ins.then_inc(values_done.sem, 1)
                        assert values_done.count() == ps.done[step]
                    elif kind == "heads_turn":
                        _, u, g = step
                        eng.wait_ge(scalar_done.sem, at(scalar_done, ps.act["values", u, g, TILES - 1]))
                        q = ps.head_quads.index((u, g))
                        dst = bank(step)
                        for t in range(TILES):
                            ins = eng.transpose(dst[:, t * P:(t + 1) * P], head_sums[:, q % 2, t * P:(t + 1) * P],
                                                ident[:, :])
                        ins.then_inc(work_full.sem, 1)
                        work_full.count()
                    elif kind == "heads_back":
                        eng.wait_ge(vector_done.sem, at(vector_done, ps.dve["heads_turn", step[1], QUADS - 1]))
                        dst = bank(step)
                        for t in range(TILES):
                            ins = eng.transpose(dst[:, t * P:(t + 1) * P], heads[:, t, :], ident[:, :])
                        ins.then_inc(work_full.sem, 1)
                        work_full.count()
                    elif kind == "out_project":
                        eng.wait_ge(vector_done.sem, at(vector_done, ps.dve["heads_back", step[1]]))
                        dst = bank(step)
                        for t in range(TILES):
                            ins = eng.matmul(dst[:, t * P:(t + 1) * P], headsT[:, t * P:(t + 1) * P],
                                             projs[:, step[1], 3, :], start=True, stop=True)
                        ins.then_inc(work_full.sem, 1)
                        work_full.count()
                    elif kind == "route":
                        src = hT if step[1] == 0 else xT
                        eng.wait_ge(vector_done.sem, at(vector_done, ps.dve["turn", "a" if step[1] == 0 else "y"]))
                        dst = bank(step)
                        for t in range(TILES):
                            ins = eng.matmul(dst[:, t * EXPERTS:(t + 1) * EXPERTS], src[:, t * P:(t + 1) * P],
                                             router[:, step[1], :], start=True, stop=True)
                        ins.then_inc(work_full.sem, 1)
                        work_full.count()
                    elif kind == "route_turn":
                        eng.wait_ge(vector_done.sem, at(vector_done, ps.dve["gate", step[1]]))
                        dst = bank(step)
                        for t in range(TILES):
                            ins = eng.transpose(dst[0:EXPERTS, t * P:(t + 1) * P], gate[:, t, :], ident[:, :])
                        ins.then_inc(work_full.sem, 1)
                        work_full.count()
                    elif kind == "route_bias":
                        eng.wait_ge(vector_done.sem, at(vector_done, ps.dve["route_turn", step[1]]))
                        dst = bank(step)
                        for t in range(TILES):
                            ins = eng.matmul(dst[:, t * P:(t + 1) * P], gateT[:, t * P:(t + 1) * P],
                                             ebias[:, step[1], :], start=True, stop=True)
                        ins.then_inc(work_full.sem, 1)
                        work_full.count()
                    elif kind == "expert_in":
                        _, layer, e, k = step
                        if e == 0 and k == 0:
                            eng.wait_ge(experts_loaded, 16 * N_EXPERT_LOADS)
                        dst = pair(step)
                        for f in range(2):
                            w = win[:, 4 * e + 2 * k + f, :] if layer else ew1[:, e, 2 * k + f, :]
                            ins = eng.matmul(dst[:, f, :], w, (xT if layer else hT)[:, :], start=True, stop=True)
                        ins.then_inc(pair_full.sem, 1)
                        assert pair_full.count() == ps.pair[step] + 1
                    elif kind == "expert_out":
                        _, layer, e, k = step
                        if k == 0:
                            eng.wait_ge(probs_ready.sem, at(probs_ready, ps.pair["expert_in", layer, e, 1] + 1))
                        dst = bank(step) if layer or k == 0 else work_bank[ps.bank[step]]
                        middle = probs[:, ps.slot["expert_in", layer, e]]
                        for t in range(TILES) if layer else range(2 * k, 2 * k + 2):
                            chunks = (k,) if layer else range(4)
                            for f in chunks:
                                w = wout[:, 4 * e + k, :] if layer else ew2[:, e, f, :]
                                ins = eng.matmul(dst[:, t * P:(t + 1) * P], middle[:, f, t * P:(t + 1) * P], w,
                                                 start=f == chunks[0], stop=f == chunks[-1])
                        ins.then_inc(values_done.sem, 1)
                        assert values_done.count() == ps.done[step]
                eng.wait_ge(work_full.sem, at(work_full, work_full.n))
                eng.sem_inc(work_full.sem, PER - work_full.n)
                eng.wait_ge(pair_full.sem, at(pair_full, pair_full.n))
                eng.sem_inc(pair_full.sem, PER - pair_full.n)
                eng.wait_ge(values_done.sem, at(values_done, values_done.n))
                eng.sem_inc(values_done.sem, PER - values_done.n)
                eng.sem_inc(arrived["pe"], 1)
                eng.wait_ge(arrived["act"], counts.number)
                eng.sem_inc(passed["pe"], 1)
                eng.wait_ge(arrived["dve"], counts.number)
                eng.sem_inc(passed["pe"], 1)
                eng.wait_ge(arrived["pool"], counts.number)
                eng.sem_inc(passed["pe"], 1)
                eng.wait_ge(arrived["sp"], counts.number)
                eng.sem_inc(passed["pe"], 1)

            counts.begin(0, owned)
            run(first_pass, 0)
            with eng.Fori(0, BATCH - 1) as b:
                counts.begin_looped(b, owned)
                run(middle_pass, b)
            counts.begin(BATCH, owned)
            run(last_pass, BATCH - 1)

        @block.gpsimd
        def _(eng):
            for tile in (ident, ident16, mask_qk, mask_kq):
                eng.memset(tile[:, :], 0.0).then_inc(made, 1)
            eng.wait_ge(made, 4)
            for tile in (ident, ident16):
                eng.affine_select(out=tile[:, :], in_=tile[:, :], compare_op=ALU.not_equal, fill=1.0, base=0,
                                  pattern=[[-1, P]], channel_multiplier=1).then_inc(made, 1)
            eng.affine_select(out=mask_qk[:, :], in_=mask_qk[:, :], compare_op=ALU.is_ge, fill=MASKED, base=0,
                              pattern=[[-1, P]], channel_multiplier=1).then_inc(made, 1)
            eng.affine_select(out=mask_kq[:, :], in_=mask_kq[:, :], compare_op=ALU.is_ge, fill=MASKED, base=0,
                              pattern=[[1, P]], channel_multiplier=-1).then_inc(made, 1)
            counts = Counts(eng, "pool", signals)
            at = counts.at
            owned = (gpsimd_done, *gpsimd_landed)

            def run(ps, b):
                for step in ps.plan:
                    kind = step[0]
                    if kind == "clear_stack":
                        slot = step[1]
                        n = N_MADE + 3 * CLEAR_ORDER.index(slot)
                        eng.wait_ge(made, n)
                        eng.wait_ge(gpsimd_done.sem, at(gpsimd_done, gpsimd_done.n))
                        eng.memset(q_stack[slot][64:P, :, :].bitcast(mybir.dt.uint32), 0).then_inc(made, 1)
                        eng.wait_ge(made, n + 1)
                        eng.memset(k_stack[slot][64:P, :, :].bitcast(mybir.dt.uint32), 0).then_inc(made, 1)
                        eng.wait_ge(made, n + 2)
                        eng.memset(k_stack[slot][MAX_ROW:MAX_ROW + PARTS, :, :].bitcast(mybir.dt.uint32), 0x3F803F80)\
                           .then_inc(made, 1)
                        eng.wait_ge(made, n + 3)
                    elif kind == "norm":
                        eng.wait_ge(vector_done.sem, at(vector_done, ps.dve["stats", step[1]]))
                        eng.tensor_tensor(rstd[:, :], var_eps[:, :], minus_half[:, :], ALU.pow)\
                           .then_inc(gpsimd_done.sem, 1)
                        assert gpsimd_done.count() == ps.pool[step]
                    elif kind == "bias":
                        dst, src, row0 = ((x_bias, x_in, ROW_BOUT), (a_sum, xn, ROW_BO))[step[1]]
                        if ps.before(("norm", "a"), step):
                            eng.wait_ge(vector_done.sem, at(vector_done, ps.dve["residual"]))
                        else:
                            eng.wait_ge(loaded, 16 * N_LOADS)
                            eng.wait_ge(vector_done.sem, at(vector_done, ps.dve["norm", "x"]))
                        for t in range(TILES):
                            eng.tensor_tensor(dst[:, t, :], src[:, t, :], rows[:, row0:row0 + P],
                                              ALU.add).then_inc(gpsimd_done.sem, 1)
                            n = gpsimd_done.count()
                        assert n == ps.pool[step]
                    elif kind == "stack":
                        _, u, half, j = step
                        if j == PARTS - 1:
                            continue
                        slot, reader = ps.stacks[u, half], ps.stack_before[step]
                        if ps is first_pass:
                            eng.wait_ge(made, N_MADE + 3 * CLEAR_ORDER.index(slot) + 3)
                        if reader:
                            eng.wait_ge(pair_full.sem, at(pair_full, ps.pair[reader] + 1))
                            eng.sem_inc(passed["pool"], 1)
                        if j == 0:
                            eng.wait_ge(vector_done.sem, at(vector_done, ps.dve["project", u, 1]))
                            eng.sem_inc(passed["pool"], 1)
                        else:
                            eng.wait_ge(scalar_done.sem, at(scalar_done, ps.act["second", u, 1]))
                            eng.sem_inc(passed["pool"], 1)
                        for i in range(PARTS):
                            r = 24 * i + 8 * j
                            eng.dma_start(k_stack[slot][r:r + 8, :, :],
                                          part[u][64 * half:64 * half + 64, 1, j, :])\
                               .then_inc(gpsimd_landed[slot].sem, 16)
                            gpsimd_landed[slot].count()
                for slot in range(3):
                    if gpsimd_landed[slot].n:
                        eng.wait_ge(gpsimd_landed[slot].sem, at(gpsimd_landed[slot], gpsimd_landed[slot].n))
                        eng.sem_inc(passed["pool"], 1)
                eng.wait_ge(gpsimd_done.sem, at(gpsimd_done, gpsimd_done.n))
                eng.sem_inc(gpsimd_done.sem, PER - gpsimd_done.n)
                eng.sem_inc(arrived["pool"], 1)
                eng.wait_ge(arrived["pe"], counts.number)
                eng.sem_inc(passed["pool"], 1)
                eng.wait_ge(arrived["act"], counts.number)
                eng.sem_inc(passed["pool"], 1)
                eng.wait_ge(arrived["dve"], counts.number)
                eng.sem_inc(passed["pool"], 1)
                eng.wait_ge(arrived["sp"], counts.number)
                eng.sem_inc(passed["pool"], 1)

            counts.begin(0, owned)
            run(first_pass, 0)
            with eng.Fori(0, BATCH - 1) as b:
                counts.begin_looped(b, owned)
                run(middle_pass, b)
            counts.begin(BATCH, owned)
            run(last_pass, BATCH - 1)

        @block.sync
        def _(eng):
            counts = Counts(eng, "sp", signals)
            at = counts.at
            owned = (x_moved, *sync_landed, *max_landed)

            def run(ps, b):
                for step in ps.plan:
                    kind = step[0]
                    if kind == "load":
                        following = bass.ds(b + 1, 1) if ps is middle_pass else slice(0, 1)
                        eng.dma_start(x_in[:, :, :], x[following, :, :].rearrange("b (t p) c -> p (b t) c", p=P))\
                           .then_inc(x_moved.sem, 16)
                        x_moved.count()
                    elif kind == "load_weights":
                        eng.dma_start(projs[:, 0:1, :, :], proj[:, 0:1, :, :]).then_inc(first_loaded, 16)
                        for dst, src in ((col[:, :], cols), (rows[:, :], row.to_broadcast([P, N_ROW])),
                                         (projs[:, 1:3, :, :], proj[:, 1:3, :, :]), (router[:, :, :], routers),
                                         (ebias[:, :, :], expert_bias)):
                            eng.dma_start(dst, src).then_inc(loaded, 16)
                    elif kind == "load_experts":
                        for dst, src in ((ew1[:, :, :, :], w_expert_in), (ew2[:, :, :, :], w_expert_out),
                                         (win[:, :, :], w_in), (wout[:, :, :], w_out)):
                            eng.dma_start(dst, src).then_inc(experts_loaded, 16)
                    elif kind == "stack":
                        _, u, half, i = step
                        slot, reader = ps.stacks[u, half], ps.stack_before[step]
                        if ps is first_pass:
                            eng.wait_ge(made, N_MADE + 3 * CLEAR_ORDER.index(slot) + 3)
                        if reader:
                            eng.wait_ge(pair_full.sem, at(pair_full, ps.pair[reader] + 1))
                            eng.sem_inc(passed["sp"], 1)
                        if i == 0:
                            eng.wait_ge(vector_done.sem, at(vector_done, ps.dve["project", u, 0]))
                            eng.sem_inc(passed["sp"], 1)
                        elif i == 1:
                            eng.wait_ge(scalar_done.sem, at(scalar_done, ps.act["second", u, 0]))
                            eng.sem_inc(passed["sp"], 1)
                        else:
                            eng.wait_ge(vector_done.sem, at(vector_done, ps.dve["part3", u, 0]))
                            eng.sem_inc(passed["sp"], 1)
                        for j in range(PARTS):
                            r = 24 * i + 8 * j
                            eng.dma_start(q_stack[slot][r:r + 8, :, :],
                                          part[u][64 * half:64 * half + 64, 0, i, :])\
                               .then_inc(sync_landed[slot].sem, 16)
                            sync_landed[slot].count()
                        if i == PARTS - 1:
                            eng.wait_ge(vector_done.sem, at(vector_done, ps.dve["part3", u, 1]))
                            eng.sem_inc(passed["sp"], 1)
                            for n in range(PARTS):
                                r = 24 * n + 8 * i
                                eng.dma_start(k_stack[slot][r:r + 8, :, :],
                                              part[u][64 * half:64 * half + 64, 1, i, :])\
                                   .then_inc(sync_landed[slot].sem, 16)
                                sync_landed[slot].count()
                    elif kind == "max_turn":
                        _, u, g = step
                        q = ps.max_quads.index((u, g))
                        slot, head0 = ps.stacks[u, g // 2], 4 * (g % 2)
                        eng.wait_ge(vector_done.sem, at(vector_done, ps.dve[step]))
                        eng.sem_inc(passed["sp"], 1)
                        eng.dma_start(q_stack[slot][MAX_ROW:MAX_ROW + PARTS, head0:head0 + 4, :],
                                      maxT[:, q % 2, :]).then_inc(max_landed[q % 2].sem, 16)
                        max_landed[q % 2].count()
                    elif kind == "store":
                        eng.wait_ge(vector_done.sem, at(vector_done, ps.dve["out_project", 2]))
                        eng.sem_inc(passed["sp"], 1)
                        this = bass.ds(b, 1) if ps is middle_pass else slice(BATCH - 1, BATCH)
                        eng.dma_start(out[this, :, :].rearrange("b (t p) c -> p (b t) c", p=P),
                                      acc[:, :, :]).then_inc(x_moved.sem, 16)
                        x_moved.count()
                if ps is last_pass:
                    eng.wait_ge(x_moved.sem, at(x_moved, 16))
                for sig in (*sync_landed, *max_landed):
                    if sig.n:
                        eng.wait_ge(sig.sem, at(sig, sig.n))
                        eng.sem_inc(passed["sp"], 1)
                eng.sem_inc(arrived["sp"], 1)
                eng.wait_ge(arrived["pe"], counts.number)
                eng.sem_inc(passed["sp"], 1)
                eng.wait_ge(arrived["act"], counts.number)
                eng.sem_inc(passed["sp"], 1)
                eng.wait_ge(arrived["dve"], counts.number)
                eng.sem_inc(passed["sp"], 1)
                eng.wait_ge(arrived["pool"], counts.number)
                eng.sem_inc(passed["sp"], 1)

            counts.begin(0, owned)
            run(first_pass, 0)
            with eng.Fori(0, BATCH - 1) as b:
                counts.begin_looped(b, owned)
                run(middle_pass, b)
            counts.begin(BATCH, owned)
            run(last_pass, BATCH - 1)


def kernel(**inputs):
    import numpy as np
    import concourse.bacc as bacc
    from concourse.bass_utils import run_bass_kernel_spmd

    a = {name: np.asarray(value) for name, value in inputs.items()}
    D = a["L0_attn_x"].shape[2]

    def by_channel(w):
        return w.reshape(*w.shape[:-1], 2, HEADS // 2, HD).swapaxes(-1, -2).reshape(w.shape)

    def of_heads(w):
        return w.transpose(1, 0, 2).reshape(D, D)

    wqkv = a["L0_attn_w_qkv"]
    proj = np.stack([
        np.stack([by_channel(wqkv[:, 0:D]), by_channel(wqkv[:, D:2 * D]), wqkv[:, 2 * D:], a["L0_attn_w_out"]], 1),
        np.stack([by_channel(a["L0_ffn_Wq"]), by_channel(a["L0_ffn_Wk"]), a["L0_ffn_Wv"], a["L0_ffn_Wo"]], 1),
        np.stack([by_channel(of_heads(a["L1_attn_W_query"])), by_channel(of_heads(a["L1_attn_W_key"])),
                  of_heads(a["L1_attn_W_val"]), a["L1_attn_W_out"].reshape(D, D)], 1)], 1)
    cols = np.stack([a["L0_ffn_ln1_g"], a["L0_ffn_ln1_b"], a["L0_ffn_ln2_g"], a["L0_ffn_ln2_b"],
                     by_channel(a["L0_ffn_bq"]), by_channel(a["L0_ffn_bk"]),
                     *a["L0_ffn_e_b1"].reshape(4 * EXPERTS, D), *a["L1_ffn_b_in"]], 1)
    row = np.concatenate([a["L0_attn_b_out"], a["L0_ffn_bo"], a["L0_ffn_bv"], a["L0_ffn_br"]])[None, :]
    arrays = {
        "x": a["L0_attn_x"],
        "proj": proj,
        "w_expert_in": a["L0_ffn_e_w1"].transpose(1, 0, 2).reshape(D, EXPERTS, 4, D),
        "w_expert_out": a["L0_ffn_e_w2"].reshape(EXPERTS, 4, D, D).transpose(2, 0, 1, 3),
        "w_in": a["L1_ffn_w_in"].transpose(1, 0, 2),
        "w_out": a["L1_ffn_w_out"].transpose(1, 0, 2),
        "routers": np.stack([a["L0_ffn_Wr"], a["L1_ffn_router_w"]], 1),
        "cols": cols,
        "row": row,
        "expert_bias": np.stack([a["L0_ffn_e_b2"], a["L1_ffn_b_out"]], 1),
    }
    arrays = {name: np.ascontiguousarray(value) for name, value in arrays.items()}
    nc = bacc.Bacc("TRN2", target_bir_lowering=False, num_devices=1)
    args = [nc.dram_tensor(name, value.shape, F32, kind="ExternalInput").ap() for name, value in arrays.items()]
    out = nc.dram_tensor("out", arrays["x"].shape, F32, kind="ExternalOutput").ap()
    build(nc, *args, out)
    result = run_bass_kernel_spmd(nc, [arrays], core_ids=[0])
    return result.results[0]["out"]
```
